# Optimizing a Trainium2 kernel written in Bass

```python
import numpy as np
import jax
import jax.numpy as jnp

def _softmax(x, axis=-1):
    return jax.nn.softmax(x, axis=axis)

def _gelu(x):
    return jax.nn.gelu(x, approximate=True)

def _silu(x):
    return jax.nn.silu(x)

def _sigmoid(x):
    return jax.nn.sigmoid(x)

def _layernorm(x, axis=-1, eps=1e-05):
    m = jnp.mean(x, axis=axis, keepdims=True)
    v = jnp.var(x, axis=axis, keepdims=True)
    return (x - m) / jnp.sqrt(v + eps)

def _scatter_add(tgt, idx, src, axis=0):
    return tgt.at[idx].add(src)

def _segment_sum(src, seg, n):
    return jax.ops.segment_sum(src, seg, n)
kernel_name = 'mk_conv_seq_d4_conv_nchw256_r2_bcef01'

def setup_inputs(seed: int=0):
    np.random.seed(seed)
    _w = jnp.asarray

    def _rec_inputs():
        import jax
        import jax.numpy as jnp
        _gk = jax.random.key(seed)
        x = 7.22e-05 + 1 * jax.random.normal(jax.random.fold_in(_gk, 1), (8, 128, 32, 32), jnp.float32)
        return x
    x = _rec_inputs()

    def _L0_conv_setup():
        import jax, jax.numpy as jnp
        import numpy as np
        B, C, CI, H, W = (8, 128, 64, 32, 32)
        BN_EPS = 1e-05

        def _maxpool2(t):
            b, c, h, w = t.shape
            return t.reshape(b, c, h // 2, 2, w // 2, 2).max(axis=(3, 5))
        key = jax.random.key(seed)
        ks = jax.random.split(key, 10)
        s = 1.0 / np.sqrt(C)
        si = 1.0 / np.sqrt(CI)
        return {'x': jax.random.normal(ks[0], (B, C, H, W), dtype=jnp.float32), 'w_theta': jax.random.normal(ks[1], (CI, C), dtype=jnp.float32) * s, 'b_theta': jax.random.normal(ks[2], (CI,), dtype=jnp.float32) * s, 'w_phi': jax.random.normal(ks[3], (CI, C), dtype=jnp.float32) * s, 'b_phi': jax.random.normal(ks[4], (CI,), dtype=jnp.float32) * s, 'w_g': jax.random.normal(ks[5], (CI, C), dtype=jnp.float32) * s, 'b_g': jax.random.normal(ks[6], (CI,), dtype=jnp.float32) * s, 'w_W': jax.random.normal(ks[7], (C, CI), dtype=jnp.float32) * si, 'b_W': jax.random.normal(ks[8], (C,), dtype=jnp.float32) * si, 'bn_gamma': jax.random.uniform(ks[9], (C,), dtype=jnp.float32), 'bn_beta': jax.random.normal(jax.random.fold_in(key, 11), (C,), dtype=jnp.float32) * 0.1, 'bn_mean': jnp.zeros((C,), dtype=jnp.float32), 'bn_var': jnp.ones((C,), dtype=jnp.float32)}
    _L0_conv_all = _L0_conv_setup()
    _L0_conv_in = {k: v for k, v in _L0_conv_all.items() if k in ('w_theta', 'b_theta', 'w_phi', 'b_phi', 'w_g', 'b_g', 'w_W', 'b_W', 'bn_gamma', 'bn_beta', 'bn_mean', 'bn_var')}
    del _L0_conv_all

    def _L1_conv_setup():
        import jax, jax.numpy as jnp
        import numpy as np
        from jax import lax
        EPS = 1e-05

        def haar_dwt(x):
            B, C, H, W = x.shape
            xr = x.reshape(B, C, H // 2, 2, W // 2, 2)
            a = xr[:, :, :, 0, :, 0]
            b = xr[:, :, :, 0, :, 1]
            c = xr[:, :, :, 1, :, 0]
            d = xr[:, :, :, 1, :, 1]
            ll = (a + b + c + d) * 0.5
            lh = (a + b - c - d) * 0.5
            hl = (a - b + c - d) * 0.5
            hh = (a - b - c + d) * 0.5
            return (ll, lh, hl, hh)

        def haar_idwt(ll, lh, hl, hh):
            B, C, h, w = ll.shape
            a = (ll + lh + hl + hh) * 0.5
            b = (ll + lh - hl - hh) * 0.5
            c = (ll - lh + hl - hh) * 0.5
            d = (ll - lh - hl + hh) * 0.5
            out = jnp.stack([jnp.stack([a, b], axis=-1), jnp.stack([c, d], axis=-1)], axis=-2)
            out = out.transpose(0, 1, 2, 4, 3, 5).reshape(B, C, 2 * h, 2 * w)
            return out

        def conv1x1(x, w, b=None):
            y = jnp.einsum('oc,bchw->bohw', w, x)
            if b is not None:
                y = y + b[None, :, None, None]
            return y

        def bn_eval(x, g, b, m, v):
            inv = g * lax.rsqrt(v + EPS)
            return x * inv[None, :, None, None] + (b - m * inv)[None, :, None, None]
        key = jax.random.key(seed)
        ks = jax.random.split(key, 12)
        B, C, H, W = (8, 128, 80, 80)
        hid = C // 16
        f32 = jnp.float32
        x = jax.random.normal(ks[0], (B, C, H, W), f32)
        fusion_w = jax.random.normal(ks[1], (C, 4 * C), f32) * (1.0 / np.sqrt(4 * C))
        fusion_b = jnp.zeros((C,), f32)
        bn1_g = jnp.ones((C,), f32)
        bn1_b = jnp.zeros((C,), f32)
        bn1_m = jax.random.normal(ks[2], (C,), f32) * 0.1
        bn1_v = jax.random.uniform(ks[3], (C,), f32, 0.5, 1.5)
        sa_w = jax.random.normal(ks[4], (1, 2, 7, 7), f32) * (1.0 / np.sqrt(2 * 49))
        ca_w1 = jax.random.normal(ks[5], (hid, C), f32) * (1.0 / np.sqrt(C))
        ca_w2 = jax.random.normal(ks[6], (C, hid), f32) * (1.0 / np.sqrt(hid))
        proj_w = jax.random.normal(ks[7], (4 * C, C), f32) * (1.0 / np.sqrt(C))
        proj_b = jnp.zeros((4 * C,), f32)
        bn2_g = jnp.ones((4 * C,), f32)
        bn2_b = jnp.zeros((4 * C,), f32)
        bn2_m = jax.random.normal(ks[8], (4 * C,), f32) * 0.1
        bn2_v = jax.random.uniform(ks[9], (4 * C,), f32, 0.5, 1.5)
        return dict(x=x, fusion_w=fusion_w, fusion_b=fusion_b, bn1_g=bn1_g, bn1_b=bn1_b, bn1_m=bn1_m, bn1_v=bn1_v, sa_w=sa_w, ca_w1=ca_w1, ca_w2=ca_w2, proj_w=proj_w, proj_b=proj_b, bn2_g=bn2_g, bn2_b=bn2_b, bn2_m=bn2_m, bn2_v=bn2_v)
    _L1_conv_all = _L1_conv_setup()
    _L1_conv_in = {k: v for k, v in _L1_conv_all.items() if k in ('fusion_w', 'fusion_b', 'bn1_g', 'bn1_b', 'bn1_m', 'bn1_v', 'sa_w', 'ca_w1', 'ca_w2', 'proj_w', 'proj_b', 'bn2_g', 'bn2_b', 'bn2_m', 'bn2_v')}
    del _L1_conv_all

    def _L2_conv_setup():
        import jax, jax.numpy as jnp
        import numpy as np
        EPS = 1e-06
        NUM_GROUPS = 16

        def group_norm(x, gamma, beta):
            B, C, H, W = x.shape
            xg = x.reshape(B, NUM_GROUPS, C // NUM_GROUPS, H, W)
            mean = xg.mean(axis=(2, 3, 4), keepdims=True)
            var = xg.var(axis=(2, 3, 4), keepdims=True)
            xg = (xg - mean) * jax.lax.rsqrt(var + EPS)
            x = xg.reshape(B, C, H, W)
            return x * gamma[None, :, None, None] + beta[None, :, None, None]

        def conv1x1(x, w, b):
            return jnp.einsum('bchw,oc->bohw', x, w) + b[None, :, None, None]
        key = jax.random.key(seed)
        ks = jax.random.split(key, 6)
        B, C, H, W = (8, 128, 32, 32)
        s = 1.0 / np.sqrt(C)
        return {'x': jax.random.normal(ks[0], (B, C, H, W), dtype=jnp.float32), 'gamma': jnp.ones((C,), jnp.float32), 'beta': jnp.zeros((C,), jnp.float32), 'wq': jax.random.normal(ks[1], (C, C), dtype=jnp.float32) * s, 'bq': jnp.zeros((C,), jnp.float32), 'wk': jax.random.normal(ks[2], (C, C), dtype=jnp.float32) * s, 'bk': jnp.zeros((C,), jnp.float32), 'wv': jax.random.normal(ks[3], (C, C), dtype=jnp.float32) * s, 'bv': jnp.zeros((C,), jnp.float32), 'wp': jax.random.normal(ks[4], (C, C), dtype=jnp.float32) * s, 'bp': jnp.zeros((C,), jnp.float32)}
    _L2_conv_all = _L2_conv_setup()
    _L2_conv_in = {k: v for k, v in _L2_conv_all.items() if k in ('gamma', 'beta', 'wq', 'bq', 'wk', 'bk', 'wv', 'bv', 'wp', 'bp')}
    del _L2_conv_all

    def _L3_conv_setup():
        import jax, jax.numpy as jnp
        import numpy as np
        NUM_HEADS = 8
        GROUPS = 32
        EPS = 1e-05

        def group_norm(x, gamma, beta):
            B, C, H, W = x.shape
            xg = x.reshape(B, GROUPS, -1)
            mu = xg.mean(axis=-1, keepdims=True)
            var = xg.var(axis=-1, keepdims=True)
            xg = (xg - mu) * jax.lax.rsqrt(var + EPS)
            x = xg.reshape(B, C, H, W)
            return x * gamma[None, :, None, None] + beta[None, :, None, None]
        key = jax.random.key(seed)
        ks = jax.random.split(key, 8)
        C = 128
        B, H, W = (2, 32, 32)
        hid = C // 4
        s_in = 1.0 / np.sqrt(C)
        s_hid = 1.0 / np.sqrt(hid)
        return {'x': jax.random.normal(ks[0], (B, C, H, W), jnp.float32), 'w_qkv': jax.random.normal(ks[1], (3 * C, C), jnp.float32) * s_in, 'w_out': jax.random.normal(ks[2], (C, C), jnp.float32) * s_in, 'b_out': jnp.zeros((C,), jnp.float32), 'temperature': jnp.ones((NUM_HEADS, 1, 1), jnp.float32) * (C // NUM_HEADS) ** (-0.5), 'g1': jnp.ones((C,), jnp.float32), 'beta1': jnp.zeros((C,), jnp.float32), 'g2': jnp.ones((C,), jnp.float32), 'beta2': jnp.zeros((C,), jnp.float32), 'w_mlp1': jax.random.normal(ks[3], (hid, C), jnp.float32) * s_in, 'b_mlp1': jnp.zeros((hid,), jnp.float32), 'w_mlp2': jax.random.normal(ks[4], (C, hid), jnp.float32) * s_hid, 'b_mlp2': jnp.zeros((C,), jnp.float32)}
    _L3_conv_all = _L3_conv_setup()
    _L3_conv_in = {k: v for k, v in _L3_conv_all.items() if k in ('w_qkv', 'w_out', 'b_out', 'temperature', 'g1', 'beta1', 'g2', 'beta2', 'w_mlp1', 'b_mlp1', 'w_mlp2', 'b_mlp2')}
    del _L3_conv_all
    return {'x': x, 'L0_conv_w_theta': _L0_conv_in['w_theta'], 'L0_conv_b_theta': _L0_conv_in['b_theta'], 'L0_conv_w_phi': _L0_conv_in['w_phi'], 'L0_conv_b_phi': _L0_conv_in['b_phi'], 'L0_conv_w_g': _L0_conv_in['w_g'], 'L0_conv_b_g': _L0_conv_in['b_g'], 'L0_conv_w_W': _L0_conv_in['w_W'], 'L0_conv_b_W': _L0_conv_in['b_W'], 'L0_conv_bn_gamma': _L0_conv_in['bn_gamma'], 'L0_conv_bn_beta': _L0_conv_in['bn_beta'], 'L0_conv_bn_mean': _L0_conv_in['bn_mean'], 'L0_conv_bn_var': _L0_conv_in['bn_var'], 'L1_conv_fusion_w': _L1_conv_in['fusion_w'], 'L1_conv_fusion_b': _L1_conv_in['fusion_b'], 'L1_conv_bn1_g': _L1_conv_in['bn1_g'], 'L1_conv_bn1_b': _L1_conv_in['bn1_b'], 'L1_conv_bn1_m': _L1_conv_in['bn1_m'], 'L1_conv_bn1_v': _L1_conv_in['bn1_v'], 'L1_conv_sa_w': _L1_conv_in['sa_w'], 'L1_conv_ca_w1': _L1_conv_in['ca_w1'], 'L1_conv_ca_w2': _L1_conv_in['ca_w2'], 'L1_conv_proj_w': _L1_conv_in['proj_w'], 'L1_conv_proj_b': _L1_conv_in['proj_b'], 'L1_conv_bn2_g': _L1_conv_in['bn2_g'], 'L1_conv_bn2_b': _L1_conv_in['bn2_b'], 'L1_conv_bn2_m': _L1_conv_in['bn2_m'], 'L1_conv_bn2_v': _L1_conv_in['bn2_v'], 'L2_conv_gamma': _L2_conv_in['gamma'], 'L2_conv_beta': _L2_conv_in['beta'], 'L2_conv_wq': _L2_conv_in['wq'], 'L2_conv_bq': _L2_conv_in['bq'], 'L2_conv_wk': _L2_conv_in['wk'], 'L2_conv_bk': _L2_conv_in['bk'], 'L2_conv_wv': _L2_conv_in['wv'], 'L2_conv_bv': _L2_conv_in['bv'], 'L2_conv_wp': _L2_conv_in['wp'], 'L2_conv_bp': _L2_conv_in['bp'], 'L3_conv_w_qkv': _L3_conv_in['w_qkv'], 'L3_conv_w_out': _L3_conv_in['w_out'], 'L3_conv_b_out': _L3_conv_in['b_out'], 'L3_conv_temperature': _L3_conv_in['temperature'], 'L3_conv_g1': _L3_conv_in['g1'], 'L3_conv_beta1': _L3_conv_in['beta1'], 'L3_conv_g2': _L3_conv_in['g2'], 'L3_conv_beta2': _L3_conv_in['beta2'], 'L3_conv_w_mlp1': _L3_conv_in['w_mlp1'], 'L3_conv_b_mlp1': _L3_conv_in['b_mlp1'], 'L3_conv_w_mlp2': _L3_conv_in['w_mlp2'], 'L3_conv_b_mlp2': _L3_conv_in['b_mlp2']}

def reference(x, L0_conv_w_theta, L0_conv_b_theta, L0_conv_w_phi, L0_conv_b_phi, L0_conv_w_g, L0_conv_b_g, L0_conv_w_W, L0_conv_b_W, L0_conv_bn_gamma, L0_conv_bn_beta, L0_conv_bn_mean, L0_conv_bn_var, L1_conv_fusion_w, L1_conv_fusion_b, L1_conv_bn1_g, L1_conv_bn1_b, L1_conv_bn1_m, L1_conv_bn1_v, L1_conv_sa_w, L1_conv_ca_w1, L1_conv_ca_w2, L1_conv_proj_w, L1_conv_proj_b, L1_conv_bn2_g, L1_conv_bn2_b, L1_conv_bn2_m, L1_conv_bn2_v, L2_conv_gamma, L2_conv_beta, L2_conv_wq, L2_conv_bq, L2_conv_wk, L2_conv_bk, L2_conv_wv, L2_conv_bv, L2_conv_wp, L2_conv_bp, L3_conv_w_qkv, L3_conv_w_out, L3_conv_b_out, L3_conv_temperature, L3_conv_g1, L3_conv_beta1, L3_conv_g2, L3_conv_beta2, L3_conv_w_mlp1, L3_conv_b_mlp1, L3_conv_w_mlp2, L3_conv_b_mlp2):
    import jax
    import jax.numpy as jnp

    def _L0_conv_ref(x, w_theta, b_theta, w_phi, b_phi, w_g, b_g, w_W, b_W, bn_gamma, bn_beta, bn_mean, bn_var):
        import jax, jax.numpy as jnp
        import numpy as np
        B, C, CI, H, W = (8, 128, 64, 32, 32)
        BN_EPS = 1e-05

        def _maxpool2(t):
            b, c, h, w = t.shape
            return t.reshape(b, c, h // 2, 2, w // 2, 2).max(axis=(3, 5))
        b, c, h, w = x.shape
        conv1x1 = lambda wgt, bias: jnp.einsum('bchw,oc->bohw', x, wgt) + bias[None, :, None, None]
        theta_x = conv1x1(w_theta, b_theta).reshape(b, CI, h * w)
        phi_x = _maxpool2(conv1x1(w_phi, b_phi)).reshape(b, CI, -1)
        g_x = _maxpool2(conv1x1(w_g, b_g)).reshape(b, CI, -1)
        f = jnp.einsum('bcn,bcm->bnm', theta_x, phi_x)
        f_div_C = jax.nn.softmax(f, axis=-1)
        y = jnp.einsum('bnm,bcm->bcn', f_div_C, g_x).reshape(b, CI, h, w)
        W_y = jnp.einsum('bchw,oc->bohw', y, w_W) + b_W[None, :, None, None]
        inv = bn_gamma / jnp.sqrt(bn_var + BN_EPS)
        W_y = W_y * inv[None, :, None, None] + (bn_beta - bn_mean * inv)[None, :, None, None]
        return W_y + x

    def _L1_conv_ref(x, fusion_w, fusion_b, bn1_g, bn1_b, bn1_m, bn1_v, sa_w, ca_w1, ca_w2, proj_w, proj_b, bn2_g, bn2_b, bn2_m, bn2_v):
        import jax, jax.numpy as jnp
        import numpy as np
        from jax import lax
        EPS = 1e-05

        def haar_dwt(x):
            B, C, H, W = x.shape
            xr = x.reshape(B, C, H // 2, 2, W // 2, 2)
            a = xr[:, :, :, 0, :, 0]
            b = xr[:, :, :, 0, :, 1]
            c = xr[:, :, :, 1, :, 0]
            d = xr[:, :, :, 1, :, 1]
            ll = (a + b + c + d) * 0.5
            lh = (a + b - c - d) * 0.5
            hl = (a - b + c - d) * 0.5
            hh = (a - b - c + d) * 0.5
            return (ll, lh, hl, hh)

        def haar_idwt(ll, lh, hl, hh):
            B, C, h, w = ll.shape
            a = (ll + lh + hl + hh) * 0.5
            b = (ll + lh - hl - hh) * 0.5
            c = (ll - lh + hl - hh) * 0.5
            d = (ll - lh - hl + hh) * 0.5
            out = jnp.stack([jnp.stack([a, b], axis=-1), jnp.stack([c, d], axis=-1)], axis=-2)
            out = out.transpose(0, 1, 2, 4, 3, 5).reshape(B, C, 2 * h, 2 * w)
            return out

        def conv1x1(x, w, b=None):
            y = jnp.einsum('oc,bchw->bohw', w, x)
            if b is not None:
                y = y + b[None, :, None, None]
            return y

        def bn_eval(x, g, b, m, v):
            inv = g * lax.rsqrt(v + EPS)
            return x * inv[None, :, None, None] + (b - m * inv)[None, :, None, None]
        identity = x
        ll, lh, hl, hh = haar_dwt(x)
        wav = jnp.concatenate([ll, lh, hl, hh], axis=1)
        fused = jax.nn.relu(bn_eval(conv1x1(wav, fusion_w, fusion_b), bn1_g, bn1_b, bn1_m, bn1_v))
        avg_sp = jnp.mean(fused, axis=1, keepdims=True)
        max_sp = jnp.max(fused, axis=1, keepdims=True)
        sp_in = jnp.concatenate([avg_sp, max_sp], axis=1)
        sp_map = lax.conv_general_dilated(sp_in, sa_w, (1, 1), ((3, 3), (3, 3)), dimension_numbers=('NCHW', 'OIHW', 'NCHW'))
        spatial_out = jax.nn.sigmoid(sp_map) * fused
        avg_ch = jnp.mean(spatial_out, axis=(2, 3), keepdims=True)
        max_ch = jnp.max(spatial_out, axis=(2, 3), keepdims=True)

        def mlp(p):
            return conv1x1(jax.nn.relu(conv1x1(p, ca_w1)), ca_w2)
        ch_map = jax.nn.sigmoid(mlp(avg_ch) + mlp(max_ch))
        channel_out = ch_map * spatial_out
        projected = jax.nn.relu(bn_eval(conv1x1(channel_out, proj_w, proj_b), bn2_g, bn2_b, bn2_m, bn2_v))
        C = projected.shape[1] // 4
        ll_o = projected[:, :C]
        lh_o = projected[:, C:2 * C]
        hl_o = projected[:, 2 * C:3 * C]
        hh_o = projected[:, 3 * C:]
        reconstructed = haar_idwt(ll_o, lh_o, hl_o, hh_o)
        return reconstructed + identity

    def _L2_conv_ref(x, gamma, beta, wq, bq, wk, bk, wv, bv, wp, bp):
        import jax, jax.numpy as jnp
        import numpy as np
        EPS = 1e-06
        NUM_GROUPS = 16

        def group_norm(x, gamma, beta):
            B, C, H, W = x.shape
            xg = x.reshape(B, NUM_GROUPS, C // NUM_GROUPS, H, W)
            mean = xg.mean(axis=(2, 3, 4), keepdims=True)
            var = xg.var(axis=(2, 3, 4), keepdims=True)
            xg = (xg - mean) * jax.lax.rsqrt(var + EPS)
            x = xg.reshape(B, C, H, W)
            return x * gamma[None, :, None, None] + beta[None, :, None, None]

        def conv1x1(x, w, b):
            return jnp.einsum('bchw,oc->bohw', x, w) + b[None, :, None, None]
        B, C, H, W = x.shape
        identity = x
        h = group_norm(x, gamma, beta)
        q = conv1x1(h, wq, bq).reshape(B, C, H * W)
        k = conv1x1(h, wk, bk).reshape(B, C, H * W)
        v = conv1x1(h, wv, bv).reshape(B, C, H * W)
        alpha = jnp.einsum('bci,bcj->bij', q, k) * C ** (-0.5)
        alpha = jax.nn.softmax(alpha, axis=-1)
        out = jnp.einsum('bcj,bij->bci', v, alpha).reshape(B, C, H, W)
        out = conv1x1(out, wp, bp)
        return identity + out

    def _L3_conv_ref(x, w_qkv, w_out, b_out, temperature, g1, beta1, g2, beta2, w_mlp1, b_mlp1, w_mlp2, b_mlp2):
        import jax, jax.numpy as jnp
        import numpy as np
        NUM_HEADS = 8
        GROUPS = 32
        EPS = 1e-05

        def group_norm(x, gamma, beta):
            B, C, H, W = x.shape
            xg = x.reshape(B, GROUPS, -1)
            mu = xg.mean(axis=-1, keepdims=True)
            var = xg.var(axis=-1, keepdims=True)
            xg = (xg - mu) * jax.lax.rsqrt(var + EPS)
            x = xg.reshape(B, C, H, W)
            return x * gamma[None, :, None, None] + beta[None, :, None, None]
        B, C, H, W = x.shape
        hd = C // NUM_HEADS
        N = H * W
        identity = x
        xn = group_norm(x, g1, beta1)
        qkv = jnp.einsum('oc,bchw->bohw', w_qkv, xn)
        q, k, v = jnp.split(qkv, 3, axis=1)
        q = q.reshape(B, NUM_HEADS, hd, N)
        k = k.reshape(B, NUM_HEADS, hd, N)
        v = v.reshape(B, NUM_HEADS, hd, N)
        temp = jnp.clip(temperature, 0.0001, 10.0)
        attn = jnp.einsum('bhdi,bhdj->bhij', q, k) * temp[None]
        attn = jax.nn.softmax(attn, axis=-1)
        out = jnp.einsum('bhdj,bhij->bhdi', v, attn)
        out = out.reshape(B, C, H, W)
        out = jnp.einsum('oc,bchw->bohw', w_out, out) + b_out[None, :, None, None]
        x = identity + out
        y = group_norm(x, g2, beta2)
        h = jnp.einsum('oc,bchw->bohw', w_mlp1, y) + b_mlp1[None, :, None, None]
        h = jax.nn.gelu(h, approximate=False)
        m = jnp.einsum('oc,bchw->bohw', w_mlp2, h) + b_mlp2[None, :, None, None]
        return x + m

    def _gn(v, G=32, eps=1e-05):
        B_, C_, H_, W_ = v.shape
        g = v.reshape(B_, G, C_ // G, H_, W_)
        m = jnp.mean(g, axis=(2, 3, 4), keepdims=True)
        s = jnp.var(g, axis=(2, 3, 4), keepdims=True)
        return ((g - m) / jnp.sqrt(s + eps)).reshape(v.shape)

    def _ln_c(v, eps=1e-06):
        m = jnp.mean(v, axis=1, keepdims=True)
        s = jnp.var(v, axis=1, keepdims=True)
        return (v - m) / jnp.sqrt(s + eps)

    def _ln_t(v, eps=1e-05):
        m = jnp.mean(v, axis=-1, keepdims=True)
        s = jnp.var(v, axis=-1, keepdims=True)
        return (v - m) / jnp.sqrt(s + eps)

    def _to_tokens(v):
        B_, C_, H_, W_ = v.shape
        return v.reshape(B_, C_, H_ * W_).transpose(0, 2, 1)

    def _from_tokens(t, like):
        B_, C_, H_, W_ = like.shape
        return t.transpose(0, 2, 1).reshape(B_, C_, H_, W_)
    x = _L0_conv_ref(x, L0_conv_w_theta, L0_conv_b_theta, L0_conv_w_phi, L0_conv_b_phi, L0_conv_w_g, L0_conv_b_g, L0_conv_w_W, L0_conv_b_W, L0_conv_bn_gamma, L0_conv_bn_beta, L0_conv_bn_mean, L0_conv_bn_var)
    x = _L1_conv_ref(x, L1_conv_fusion_w, L1_conv_fusion_b, L1_conv_bn1_g, L1_conv_bn1_b, L1_conv_bn1_m, L1_conv_bn1_v, L1_conv_sa_w, L1_conv_ca_w1, L1_conv_ca_w2, L1_conv_proj_w, L1_conv_proj_b, L1_conv_bn2_g, L1_conv_bn2_b, L1_conv_bn2_m, L1_conv_bn2_v)
    x = _L2_conv_ref(x, L2_conv_gamma, L2_conv_beta, L2_conv_wq, L2_conv_bq, L2_conv_wk, L2_conv_bk, L2_conv_wv, L2_conv_bv, L2_conv_wp, L2_conv_bp)
    x = _L3_conv_ref(x, L3_conv_w_qkv, L3_conv_w_out, L3_conv_b_out, L3_conv_temperature, L3_conv_g1, L3_conv_beta1, L3_conv_g2, L3_conv_beta2, L3_conv_w_mlp1, L3_conv_b_mlp1, L3_conv_w_mlp2, L3_conv_b_mlp2)
    return x

_drawn_inputs = setup_inputs


def setup_inputs(seed=0):
    import zlib

    import numpy as np

    out = dict(_drawn_inputs(seed))
    spreads = {'L0_conv_bn_mean': (0.0, 0.1),
     'L0_conv_bn_var': (1.0, 0.2),
     'L1_conv_fusion_b': (0.0, 0.418),
     'L1_conv_bn1_g': (1.0, 0.2),
     'L1_conv_bn1_b': (0.0, 0.439),
     'L1_conv_proj_b': (0.0, 0.1),
     'L1_conv_bn2_g': (1.0, 0.2),
     'L1_conv_bn2_b': (0.0, 0.1),
     'L2_conv_gamma': (1.0, 0.2),
     'L2_conv_beta': (0.0, 0.1),
     'L2_conv_bq': (0.0, 0.8),
     'L2_conv_bk': (0.0, 0.8),
     'L2_conv_bv': (0.0, 0.1),
     'L2_conv_bp': (0.0, 0.1),
     'L3_conv_b_out': (0.0, 0.1),
     'L3_conv_temperature': (0.25, 0.6),
     'L3_conv_g1': (1.0, 0.2),
     'L3_conv_beta1': (0.0, 0.1),
     'L3_conv_g2': (1.0, 0.2),
     'L3_conv_beta2': (0.0, 0.1),
     'L3_conv_b_mlp1': (0.0, 0.1),
     'L3_conv_b_mlp2': (0.0, 0.1)}
    factors = {'L0_conv_b_phi': 8.0, 'L1_conv_bn1_m': 3.067}
    for name, (base, spread) in spreads.items():
        noise = np.random.default_rng([zlib.crc32(name.encode()), seed]).standard_normal(out[name].shape)
        drawn = base * np.exp(spread * noise) if base else spread * noise
        out[name] = jnp.asarray(drawn.astype(out[name].dtype))
    for name, factor in factors.items():
        out[name] = (out[name] * factor).astype(out[name].dtype)
    return out
```

```python
import numpy as np

import concourse.bass as bass
from concourse import mybir
from concourse.alu_op_type import AluOpType as ALU
from contextlib import ExitStack

F32 = mybir.dt.float32
F32R = mybir.dt.float32r
ACT = mybir.ActivationFunctionType
AX = mybir.AxisListType

B, C, H, W = 8, 128, 32, 32
N = H * W
HALF = 512
NH = N // HALF
NC = N // 128
CI = 64
M0 = N // 4
Q = N // 4
QW = W // 2
HID = 8
TAPS, PADW = 7, 2 * QW - 1
HEADS, HD = 8, 16
GH = 4
NG = HEADS // GH
MLP = 32
PACK = 3 * HD

VECS = ["b_W", "bn_gamma", "bn_beta", "bn_mean", "bn_var", "fusion_b", "bn1_g", "bn1_b", "bn1_m", "bn1_v",
        "proj_b0", "proj_b1", "proj_b2", "proj_b3", "bn2_g0", "bn2_g1", "bn2_g2", "bn2_g3",
        "bn2_b0", "bn2_b1", "bn2_b2", "bn2_b3", "bn2_m0", "bn2_m1", "bn2_m2", "bn2_m3",
        "bn2_v0", "bn2_v1", "bn2_v2", "bn2_v3", "gamma", "beta", "bq", "bk", "bv", "bp",
        "temp", "b_out", "g1", "beta1", "g2", "beta2", "b_mlp2", "b_phig"]
V = {name: i for i, name in enumerate(VECS)}


def build(nc, x, vecs, w_theta, b_theta, w_phig, w_W, w_fuse, sa_w, ca_w1, ca_w2, w_proj,
          wq, wk, wv, wp, w_qkv, w_out, w_mlp1, b_mlp1, w_mlp2, out):
    pad_dram = nc.dram_tensor("padded_taps", [2, PADW, PADW], F32, kind="Internal").ap()
    xd = x.rearrange("b c h w -> b c (h w)")
    od = out.rearrange("b c h w -> b c (h w)")

    with ExitStack() as ctx:
        def sb(name, shape, dt=F32):
            return ctx.enter_context(nc.sbuf_tensor(name, shape, dt))

        sems = {}

        def sem(name):
            if name not in sems:
                sems[name] = ctx.enter_context(nc.semaphore(name))
            return sems[name]

        ident = sb("ident", [128, 128])
        ones = sb("ones", [128, 128])
        ones_r = sb("ones_r", [128, 128], F32R)
        grp8 = sb("grp8", [128, 128])
        grp4 = sb("grp4", [128, 128])
        neg_half = sb("neg_half", [128, 16])
        vec = sb("vec", [128, len(VECS)])
        wth = sb("wth", [128, CI])
        bth = sb("bth", [CI, 1])
        wpg = sb("wpg", [128, 128])
        wWT = sb("wWT", [128, 128])
        wfu = sb("wfu", [128, 4, 128])
        wfs = sb("wfs", [128, 4, 128])
        wfc = sb("wfc", [128, 4, 128])
        wca1 = sb("wca1", [128, HID])
        wca2 = sb("wca2", [HID, 128])
        wpr = sb("wpr", [128, 4 * 128])
        wq_s = sb("wq_s", [128, 128])
        wk_s = sb("wk_s", [128, 128])
        wv_s = sb("wv_s", [128, 128])
        wp_s = sb("wp_s", [128, 128])
        wpv = sb("wpv", [128, 128])
        wqkv = sb("wqkv", [128, 3 * 128])
        wo = sb("wo", [128, NG, 128])
        wm1 = sb("wm1", [128, MLP])
        bm1 = sb("bm1", [MLP, 1])
        wm2 = sb("wm2", [MLP, 128])
        pad_sb = sb("pad_sb", [2, PADW * PADW])
        toep = sb("toep", [128, 4, Q])
        idle = sb("idle", [128, 1])
        cst = sb("cst", [128, 32])
        tmpc = sb("tmpc", [128, 64])

        xin = sb("xin", [128, N])
        th = sb("th", [128, N])
        ph = sb("ph", [128, M0])
        pg = sb("pg", [128, M0])
        gt = sb("gt", [128, M0])
        wg = sb("wg", [128, 2, 128])
        nm0 = sb("nm0", [128, NC])
        nm0T = sb("nm0T", [NC, 128])
        rec = sb("rec", [128, N])
        y0 = sb("y0", [128, N])
        x1 = sb("x1", [128, N])
        fused = sb("fused", [128, Q])
        spT = sb("spT", [128, 2, 2])
        sg = sb("sg", [128, Q])
        sg1 = sb("sg1", [128, Q])
        sg2 = sb("sg2", [128, Q])
        spat = sb("spat", [128, Q])
        pool = sb("pool", [128, 2])
        hid = sb("hid", [HID, 2])
        hsum = sb("hsum", [HID, 1])
        chm = sb("chm", [128, 4])
        chout = sb("chout", [128, Q])
        pj = sb("pj", [128, 4, Q])
        sd = sb("sd", [128, 2, 2, Q])
        ux = rec
        x2 = sb("x2", [128, N])
        st = sb("st", [128, 2, 6])
        mv = sb("mv", [128, 16])
        h2 = sb("h2", [128, N])
        qf = sb("qf", [128, N])
        kf = sb("kf", [128, N])
        qh = sb("qh", [128, N], F32R)
        ql = sb("ql", [128, N], F32R)
        kh = sb("kh", [128, N], F32R)
        kl = sb("kl", [128, N], F32R)
        vT = sb("vT", [128, NC, 128])
        mx = sb("mx", [128, NC, NH])
        nm2 = sb("nm2", [128, NC])
        nm2T = sb("nm2T", [NC, 128], F32R)
        nmrow = sb("nmrow", [1, N], F32R)
        pt2 = sb("pt2", [128, 2, N])
        pt0 = pt2
        acc = sb("acc", [128, N])
        x3 = sb("x3", [128, N])
        qp = sb("qp", [128, GH, N], F32R)
        kp = sb("kp", [128, GH, N], F32R)
        vt3 = sb("vt3", [128, NC, HEADS, 32])
        mx3 = sb("mx3", [128, GH, NC, NH])
        nm3 = sb("nm3", [128, GH * NC])
        nm3T = sb("nm3T", [GH * NC, 128], F32R)
        p3 = sb("p3", [128, 2, GH, HALF])
        toep_rev = p3[:, 0, 0:2, :].rearrange("p a (b q) -> p (a b) q", q=Q)
        og = sb("og", [128, N])
        rec3, recs = rec, y0
        yn = sb("yn", [128, NG, N])
        x4 = sb("x4", [128, N])
        gl = sb("gl", [MLP, N])
        xo = sb("xo", [128, N])

        ps = ctx.enter_context(nc.psum_tensor("ps", [128, 8, HALF], F32))

        def two(k):
            return ps[:, k:k + 2, :].rearrange("p a b -> p (a b)")

        def col(name, rows=128):
            return vec[0:rows, V[name]:V[name] + 1]

        def raw(ap):
            return ap.bitcast(F32)

        def half(t, h):
            return t[:, HALF * h:HALF * (h + 1)]

        INV0, C0, INV1, C1, INV2, C2, BQS, B2, BO, TMP = 0, 1, 2, 3, 4, 8, 12, 13, 14, 15
        QS = float(C) ** -0.5
        DVE_STEPS = 32

        loads = [
            (vec[:], vecs), (wth[:], w_theta), (bth[:], b_theta), (wpg[:], w_phig), (wWT[CI:128, :], w_W),
            (wfu[:].rearrange("p k o -> p (k o)"), w_fuse), (wca1[:], ca_w1), (wca2[:], ca_w2), (wpr[:], w_proj),
            (wq_s[:], wq), (wk_s[:], wk), (wv_s[:], wv), (wp_s[:], wp), (wqkv[:], w_qkv),
            (wm1[:], w_mlp1), (bm1[:], b_mlp1), (wm2[:], w_mlp2),
        ]

        block = ctx.enter_context(nc.Block())

        @block.sync
        def _(sp):
            for dst, src in loads:
                sp.dma_start(dst, src).then_inc(sem("weights_in"), 16)
            sp.wait_ge(sem("wo_zeroed"), 1)
            for h in range(HEADS):
                r = 32 * (h % GH)
                sp.dma_start(wo[r:r + HD, h // GH, :], w_out[HD * h:HD * (h + 1), :]).then_inc(sem("wo_in"), 16)
            sp.wait_ge(sem("pad_zeroed"), 1)
            p3d = pad_sb[:].rearrange("c (a b) -> c a b", b=PADW)
            lo = QW - 1 - TAPS // 2
            sp.dma_start(p3d[:, lo:lo + TAPS, lo:lo + TAPS], sa_w).then_inc(sem("taps_in"), 16)
            sp.wait_ge(sem("taps_in"), 16)
            sp.dma_start(pad_dram.rearrange("c a b -> c (a b)"), pad_sb[:]).then_inc(sem("pad_out"), 16)
            sp.wait_ge(sem("pad_out"), 16)
            for c in range(2):
                for yy in range(QW):
                    win = pad_dram[c, yy:yy + QW, 0:QW]
                    src = bass.AP(tensor=win.tensor, offset=win.offset, ap=[[1, QW], [PADW, QW], [1, QW]])
                    r = QW * (yy % 8)
                    sp.dma_start(toep_rev[r:r + QW, 2 * c + yy // 8, :].rearrange("p (a b) -> p a b", b=QW),
                                 src).then_inc(sem("windows_in"), 16)
            sp.wait_ge(sem("ones_ready"), 1)
            for t in range(GH):
                for s in range(2):
                    r = 64 * s + PACK
                    sp.dma_start(raw(kp[r:r + 1, t, :]).rearrange("p (a b) -> p a b", b=128),
                                 raw(ones_r[0:NC, :])).then_inc(sem("k_ones_in"), 16)

            with sp.Fori(0, B) as b:
                sp.wait_ge(sem("x1_ready"), b)
                sp.dma_start(xin[:], xd[b, :, :]).then_inc(sem("x_in"), 16)
                sp.wait_ge(sem("nm0T_ready"), b + 1)
                sp.dma_start(th[CI:CI + 1, :].rearrange("p (a b) -> p a b", b=128), nm0T[:]).then_inc(sem("nm0_row_in"), 16)
                sp.wait_ge(sem("nm2T_ready"), b + 1)
                sp.dma_start(raw(nmrow[0:1, :]).rearrange("p (a b) -> p a b", b=128), raw(nm2T[:])).then_inc(sem("nm2_row_in"), 16)
                sp.wait_ge(sem("k3_split"), b + 1)
                for hd in range(HEADS):
                    t, r, c0 = hd // 2, 64 * (hd % 2), HD * hd
                    for dst, parts in ((qp, (qh, ql, qh)), (kp, (kh, kh, kl))):
                        for i, part in enumerate(parts):
                            sp.dma_start(raw(dst[r + HD * i:r + HD * (i + 1), t, :]),
                                         raw(part[c0:c0 + HD, :])).then_inc(sem("packed"), 16)
                for g in range(NG):
                    sp.wait_ge(sem("nm3T_ready"), b * NG + (g + 1))
                    for i in range(GH):
                        hd = GH * g + i
                        r = 64 * (hd % 2) + PACK
                        sp.dma_start(raw(qp[r:r + 1, hd // 2, :]).rearrange("p (a b) -> p a b", b=128),
                                     raw(nm3T[NC * i:NC * (i + 1), :])).then_inc(sem("nm3_row_in"), 16)
                sp.wait_ge(sem("xo_ready"), b + 1)
                sp.dma_start(od[b, :, :], xo[:]).then_inc(sem("out_done"), 16)
            sp.wait_ge(sem("out_done"), 16 * B)

        @block.gpsimd
        def _(pool_e):
            g = nc.gpsimd
            g.memset(wo[:], 0.0).then_inc(sem("wo_zeroed"), 1)
            g.memset(pad_sb[:], 0.0).then_inc(sem("pad_zeroed"), 1)
            g.memset(neg_half[:], -0.5).then_inc(sem("neg_half_ready"), 1)
            g.memset(ident[:], 0.0).then_inc(sem("ident_zeroed"), 1)
            pool_e.wait_ge(sem("ident_zeroed"), 1)
            g.affine_select(out=ident[:], in_=ident[:], compare_op=ALU.not_equal, fill=1.0, base=0,
                            pattern=[[-1, 128]], channel_multiplier=1).then_inc(sem("ident_ready"), 1)
            for k, (t, width) in enumerate(((grp8, 8), (grp4, 4))):
                g.memset(t[:], 1.0 / width).then_inc(sem("grp_steps"), 1)
                pool_e.wait_ge(sem("grp_steps"), 3 * k + 1)
                v = t[:].rearrange("p (a b) -> p a b", b=width)
                g.affine_select(out=v, in_=v, compare_op=ALU.is_ge, fill=0.0, base=0,
                                pattern=[[-width, 128 // width], [0, width]], channel_multiplier=1).then_inc(sem("grp_steps"), 1)
                pool_e.wait_ge(sem("grp_steps"), 3 * k + 2)
                g.affine_select(out=v, in_=v, compare_op=ALU.is_ge, fill=0.0, base=width - 1,
                                pattern=[[width, 128 // width], [0, width]], channel_multiplier=-1).then_inc(sem("grp_steps"), 1)
            pool_e.wait_ge(sem("vars_ready"), 1)
            pool_e.wait_ge(sem("neg_half_ready"), 1)
            g.tensor_tensor(tmpc[:, 8:14], tmpc[:, 0:6], neg_half[:, 0:6], ALU.pow).then_inc(sem("rsq_ready"), 1)

            with pool_e.Fori(0, B) as b:
                pool_e.wait_ge(sem("var2_ready"), b + 1)
                g.tensor_tensor(mv[:, 5:6], mv[:, 4:5], neg_half[:, 0:1], ALU.pow).then_inc(sem("rstd2_ready"), 1)
                for j in range(1, NC):
                    pool_e.wait_ge(sem("p2_ready"), b * NC * NH + (NH * (j + 1)))
                    if j > 1:
                        pool_e.wait_ge(sem("acc_steps"), b * (NC - 1) + (j - 1))
                    a = pt2[:, 0, :] if j == 1 else acc[:]
                    g.tensor_tensor(acc[:], a, pt2[:, j % 2, :], ALU.add).then_inc(sem("acc_steps"), 1)
                pool_e.wait_ge(sem("var3_ready"), b + 1)
                g.tensor_tensor(mv[:, 5:6], mv[:, 4:5], neg_half[:, 0:1], ALU.pow).then_inc(sem("rstd3_ready"), 1)
                pool_e.wait_ge(sem("var4_ready"), b + 1)
                g.tensor_tensor(mv[:, 5:6], mv[:, 4:5], neg_half[:, 0:1], ALU.pow).then_inc(sem("rstd4_ready"), 1)

        @block.scalar
        def _(act):
            a = nc.scalar
            act.wait_ge(sem("ones_f_ready"), 1)
            a.copy(ones_r[:], ones[:]).then_inc(sem("ones_ready"), 1)
            act.wait_ge(sem("wpv_ps"), 1)
            a.copy(wpv[:], ps[:, 0, 0:128]).then_inc(sem("wpv_ready"), 1)
            act.wait_ge(sem("consts_ready"), 1)

            with act.Fori(0, B) as b:
                act.wait_ge(sem("theta_ps"), b + 1)
                a.activation(th[0:CI, :], ps[0:CI, 0:2, :].rearrange("p a b -> p (a b)"), ACT.Identity,
                             bias=bth[:, 0:1]).then_inc(sem("theta_ready"), 1)
                act.wait_ge(sem("wg_ps"), b + 1)
                a.copy(wg[:].rearrange("p a b -> p (a b)"), ps[:, 2, 0:256]).then_inc(sem("wg_ready"), 1)
                act.wait_ge(sem("nm0T_ps"), b + 1)
                a.copy(nm0T[:], ps[0:NC, 3, 0:128]).then_inc(sem("nm0T_ready"), 1)
                for m in range(2):
                    act.wait_ge(sem("s0_ps"), b * 2 + (m + 1))
                    a.activation(pt0[:, m, :], two(4 + 2 * m), ACT.Exp).then_inc(sem("p0_ready"), 1)
                act.wait_ge(sem("fus_ps"), b + 1)
                a.activation(fused[:], ps[:, 4, 0:Q], ACT.Relu, bias=cst[:, C1:C1 + 1],
                             scale=cst[:, INV1:INV1 + 1]).then_inc(sem("fused_ready"), 1)
                act.wait_ge(sem("conv_ps"), b + 1)
                a.activation(sg[:], ps[:, 6, 0:Q], ACT.Exp, scale=-1.0).then_inc(sem("sg_exp"), 1)
                act.wait_ge(sem("mlp1_ps"), b + 1)
                a.activation(hid[:], ps[0:HID, 7, 0:2], ACT.Relu, accum_out=hsum[:, 0:1]).then_inc(sem("hid_ready"), 1)
                act.wait_ge(sem("mlp2_ps"), b + 1)
                a.activation(chm[:, 0:1], ps[:, 5, 0:1], ACT.Exp, scale=-1.0).then_inc(sem("chm_exp"), 1)
                for k in range(4):
                    act.wait_ge(sem("proj_ps"), b * 4 + (2 * (k // 2) + 2))
                    a.activation(pj[:, k, :], ps[:, k // 2, Q * (k % 2):Q * (k % 2 + 1)], ACT.Relu,
                                 bias=cst[:, C2 + k:C2 + k + 1],
                                 scale=cst[:, INV2 + k:INV2 + k + 1]).then_inc(sem("pj_ready"), 1)
                act.wait_ge(sem("q2_ps"), b + 1)
                a.activation(qf[:], two(0), ACT.Identity, bias=cst[:, BQS:BQS + 1], scale=QS).then_inc(sem("q2_ready"), 1)
                act.wait_ge(sem("k2_ps"), b + 1)
                a.activation(kf[:], two(2), ACT.Identity, bias=col("bk")).then_inc(sem("k2_ready"), 1)
                act.wait_ge(sem("v2_ps"), b + 1)
                a.copy(vT[:].rearrange("p a b -> p (a b)"), two(4)).then_inc(sem("v2_ready"), 1)
                act.wait_ge(sem("nm2T_ps"), b + 1)
                a.copy(nm2T[:], ps[0:NC, 2, 0:128]).then_inc(sem("nm2T_ready"), 1)
                for j in range(NC):
                    if j >= 2:
                        act.wait_ge(sem("pv2_done"), b * NC + (j - 1))
                        act.wait_ge(sem("acc_steps"), b * (NC - 1) + max(j - 2, 1))
                    for h in range(NH):
                        u = NH * j + h
                        act.wait_ge(sem("s2_ps"), b * NC * NH + (u + 1))
                        a.activation(half(pt2[:, j % 2, :], h), ps[:, 4 + u % 4, :], ACT.Exp).then_inc(sem("p2_ready"), 1)
                act.wait_ge(sem("q3_ps"), b + 1)
                a.activation(qf[:], two(4), ACT.Copy, scale=cst[:, TMP:TMP + 1]).then_inc(sem("q3_ready"), 1)
                act.wait_ge(sem("k3_ps"), b + 1)
                a.copy(kf[:], two(6)).then_inc(sem("k3_ready"), 1)
                act.wait_ge(sem("v3_ps"), b + 1)
                a.copy(vt3[:, :, :, 0:HD], two(2).rearrange("p (j h d) -> p j h d", h=HEADS, d=HD)).then_inc(sem("v3_ready"), 1)
                for g in range(NG):
                    act.wait_ge(sem("nm3T_ps"), b * NG + (g + 1))
                    if g:
                        act.wait_ge(sem("nm3_row_in"), 16 * (b * HEADS + GH * g))
                    a.copy(nm3T[:], ps[0:GH * NC, 0, 0:128]).then_inc(sem("nm3T_ready"), 1)
                    for j in range(NC):
                        for h in range(NH):
                            s = (g * NC + j) * NH + h
                            if s >= 2:
                                act.wait_ge(sem("pv3_done"), b * NG * NC * NH + (s - 1))
                            for i in range(GH):
                                u = s * GH + i
                                act.wait_ge(sem("s3_ps"), b * HEADS * NC * NH + (u + 1))
                                a.activation(p3[:, s % 2, i, :], ps[:, 2 + u % 4, :], ACT.Exp).then_inc(sem("p3_ready"), 1)
                    if g:
                        act.wait_ge(sem("yn_ready"), b * NG + g)
                    act.wait_ge(sem("pv3_done"), b * NG * NC * NH + (g + 1) * NC * NH)
                    a.copy(og[:], two(6)).then_inc(sem("og_ready"), 1)
                act.wait_ge(sem("h4_ps"), b + 1)
                a.activation(gl[:], ps[0:MLP, 4:6, :].rearrange("p a b -> p (a b)"), ACT.Gelu,
                             bias=bm1[:, 0:1]).then_inc(sem("gelu_ready"), 1)

        @block.vector
        def _(dve):
            v = nc.vector
            steps = [0]

            def link(ins):
                steps[0] += 1
                ins.then_inc(sem("dve_setup"), 1)
                dve.wait_ge(sem("dve_setup"), steps[0])

            v.memset(ones[:], 1.0).then_inc(sem("ones_f_ready"), 1)
            v.memset(vt3[:], 1.0).then_inc(sem("v_ones"), 1)
            v.memset(ph[CI:CI + 32, :], 1.0).then_inc(sem("ph_ones"), 1)
            dve.wait_ge(sem("weights_in"), 16 * len(loads))
            link(v.tensor_scalar(tmpc[:, 0:1], col("bn_var"), 1e-5, None, ALU.add))
            link(v.tensor_scalar(tmpc[:, 1:2], col("bn1_v"), 1e-5, None, ALU.add))
            v.tensor_scalar(tmpc[:, 2:6], vec[:, V["bn2_v0"]:V["bn2_v0"] + 4], 1e-5, None, ALU.add).then_inc(sem("vars_ready"), 1)
            dve.wait_ge(sem("rsq_ready"), 1)
            link(v.tensor_tensor(cst[:, INV0:INV0 + 1], col("bn_gamma"), tmpc[:, 8:9], ALU.mult))
            link(v.tensor_tensor(tmpc[:, 16:17], col("b_W"), col("bn_mean"), ALU.subtract))
            link(v.scalar_tensor_tensor(cst[:, C0:C0 + 1], tmpc[:, 16:17], cst[:, INV0:INV0 + 1], col("bn_beta"), ALU.mult, ALU.add))
            link(v.tensor_tensor(cst[:, INV1:INV1 + 1], col("bn1_g"), tmpc[:, 9:10], ALU.mult))
            link(v.tensor_tensor(tmpc[:, 17:18], col("fusion_b"), col("bn1_m"), ALU.subtract))
            link(v.scalar_tensor_tensor(cst[:, C1:C1 + 1], tmpc[:, 17:18], cst[:, INV1:INV1 + 1], col("bn1_b"), ALU.mult, ALU.add))
            c4 = lambda n: vec[:, V[n + "0"]:V[n + "0"] + 4]
            link(v.scalar_tensor_tensor(cst[:, INV2:INV2 + 4], c4("bn2_g"), 0.5, tmpc[:, 10:14], ALU.mult, ALU.mult))
            link(v.tensor_tensor(tmpc[:, 20:24], c4("proj_b"), c4("bn2_m"), ALU.subtract))
            link(v.tensor_tensor(tmpc[:, 24:28], tmpc[:, 20:24], cst[:, INV2:INV2 + 4], ALU.mult))
            link(v.scalar_tensor_tensor(cst[:, C2:C2 + 4], c4("bn2_b"), 0.5, tmpc[:, 24:28], ALU.mult, ALU.add))
            link(v.tensor_scalar(cst[:, BQS:BQS + 1], col("bq"), QS, None, ALU.mult))
            dve.wait_ge(sem("wpv_ps"), 1)
            link(v.tensor_tensor(cst[:, B2:B2 + 1], ps[:, 1, 0:1], col("bp"), ALU.add))
            link(v.tensor_scalar(cst[:, TMP:TMP + 1], col("temp"), 1e-4, 10.0, ALU.max, ALU.min))
            link(v.tensor_scalar(wfu[:], wfu[:], 0.5, None, ALU.mult))
            link(v.tensor_tensor(wfs[:, 0, :], wfu[:, 0, :], wfu[:, 1, :], ALU.add))
            link(v.tensor_tensor(wfs[:, 1, :], wfu[:, 2, :], wfu[:, 3, :], ALU.add))
            link(v.tensor_tensor(wfs[:, 2, :], wfu[:, 0, :], wfu[:, 1, :], ALU.subtract))
            link(v.tensor_tensor(wfs[:, 3, :], wfu[:, 2, :], wfu[:, 3, :], ALU.subtract))
            link(v.tensor_tensor(wfc[:, 0, :], wfs[:, 0, :], wfs[:, 1, :], ALU.add))
            link(v.tensor_tensor(wfc[:, 1, :], wfs[:, 0, :], wfs[:, 1, :], ALU.subtract))
            link(v.tensor_tensor(wfc[:, 2, :], wfs[:, 2, :], wfs[:, 3, :], ALU.add))
            link(v.tensor_tensor(wfc[:, 3, :], wfs[:, 2, :], wfs[:, 3, :], ALU.subtract))
            dve.wait_ge(sem("windows_in"), 16 * 2 * QW)
            for t in range(4):
                last = v.tensor_scalar(toep[:, t, :], toep_rev[:, t, ::-1], 1.0 / C if t < 2 else 1.0, None, ALU.mult)
            last.then_inc(sem("consts_ready"), 1)

            with dve.Fori(0, B) as b:
                count = [0]

                def link(ins):
                    count[0] += 1
                    ins.then_inc(sem("dve_step"), 1)
                    dve.wait_ge(sem("dve_step"), b * DVE_STEPS + count[0])

                def carry_wait():
                    v.memset(idle[:], 0.0)

                dve.wait_ge(sem("phig_ps"), b + 1)
                for h in range(NH):
                    src = ps[:, 2 + h, :].rearrange("p (y a x b) -> p y x a b", a=2, b=2, x=QW)
                    dst = pg[:, 128 * h:128 * (h + 1)].rearrange("p (y x) -> p y x", x=QW)
                    last = v.tensor_reduce(dst, src, AX.XY, ALU.max)
                link(last)
                v.tensor_scalar(ph[0:CI, :], pg[0:CI, :], vec[0:CI, V["b_phig"]:V["b_phig"] + 1], None, ALU.add).then_inc(sem("phi_ready"), 1)
                v.tensor_scalar(gt[CI:128, :], pg[CI:128, :], vec[CI:128, V["b_phig"]:V["b_phig"] + 1], None, ALU.add).then_inc(sem("g_ready"), 1)
                for k in range(4):
                    dve.wait_ge(sem("s0max_ps"), b * 4 + (k + 1))
                    v.tensor_reduce(nm0[:, 2 * k:2 * k + 2], ps[:, 4 + k, :].rearrange("p (a b) -> p a b", b=M0), AX.X,
                                    ALU.max, negate=True).then_inc(sem("nm0_ready"), 1)
                dve.wait_ge(sem("den0_ps"), b + 1)
                link(v.reciprocal(rec[:], two(2)))
                link(v.tensor_tensor(y0[:], two(0), rec[:], ALU.mult))
                link(v.tensor_scalar(rec[:], y0[:], cst[:, INV0:INV0 + 1], cst[:, C0:C0 + 1], ALU.mult, ALU.add))
                v.tensor_tensor(x1[:], rec[:], xin[:], ALU.add).then_inc(sem("x1_ready"), 1)

                dve.wait_ge(sem("fT_ps"), b + 1)
                fT = ps[:, 5, 0:2 * 128].rearrange("p (a b) -> p a b", b=128)
                v.tensor_reduce(spT[:, 0, :], fT, AX.X, ALU.add).then_inc(sem("sp_sum"), 1)
                v.tensor_reduce(spT[:, 1, :], fT, AX.X, ALU.max).then_inc(sem("sp_ready"), 1)
                dve.wait_ge(sem("sg_exp"), b + 1)
                link(v.tensor_scalar(sg1[:], sg[:], 1.0, None, ALU.add))
                link(v.reciprocal(sg2[:], sg1[:]))
                dve.wait_ge(sem("fused_ready"), b + 1)
                v.scalar_tensor_tensor(spat[:], sg2[:], 1.0 / Q, fused[:], ALU.mult, ALU.mult,
                                       accum_out=pool[:, 0:1]).then_inc(sem("spat_ready"), 1)
                dve.wait_ge(sem("spat_ready"), b + 1)
                link(v.tensor_reduce(chm[:, 3:4], spat[:], AX.X, ALU.max))
                v.tensor_scalar(pool[:, 1:2], chm[:, 3:4], float(Q), None, ALU.mult).then_inc(sem("pool_ready"), 1)
                dve.wait_ge(sem("chm_exp"), b + 1)
                link(v.tensor_scalar(chm[:, 1:2], chm[:, 0:1], 1.0, None, ALU.add))
                link(v.reciprocal(chm[:, 2:3], chm[:, 1:2]))
                v.tensor_scalar(chout[:], spat[:], chm[:, 2:3], float(Q), ALU.mult, ALU.mult).then_inc(sem("chout_ready"), 1)
                dve.wait_ge(sem("pj_ready"), b * 4 + 4)
                even, odd = pj[:, 0::2, :], pj[:, 1::2, :]
                v.tensor_tensor(sd[:, 0, :, :], even, odd, ALU.add)
                link(v.tensor_tensor(sd[:, 1, :, :], even, odd, ALU.subtract))
                x1v = x1[:].rearrange("p (y r x c) -> p y r x c", r=2, c=2, x=QW)
                uxv = ux[:].rearrange("p (y r x c) -> p y r x c", r=2, c=2, x=QW)
                x2v = x2[:].rearrange("p (y r x c) -> p y r x c", r=2, c=2, x=QW)
                for r in range(2):
                    for c in range(2):
                        s = sd[:, r, 0, :].rearrange("p (y x) -> p y x", x=QW)
                        last = v.tensor_tensor(uxv[:, :, r, :, c], x1v[:, :, r, :, c], s, ALU.add)
                link(last)
                for r in range(2):
                    for c in range(2):
                        s = sd[:, r, 1, :].rearrange("p (y x) -> p y x", x=QW)
                        v.tensor_tensor(x2v[:, :, r, :, c], uxv[:, :, r, :, c], s,
                                        ALU.subtract if c else ALU.add).then_inc(sem("x2_ready"), 1)

                def group_norm(src, ready, n, eps, gam, bet, dst, tag):
                    dve.wait_ge(sem(ready), b * n + n)
                    for h in range(NH):
                        link(v.bn_stats(st[:, h, :], half(src, h)))
                    carry_wait()
                    v.bn_aggr(mv[:, 0:2], st[:]).then_inc(sem("mv" + tag), 1)
                    dve.wait_ge(sem("gm_ps" + tag), b + 1)
                    link(v.tensor_tensor(mv[:, 2:3], mv[:, 0:1], ps[:, 3, 0:1], ALU.subtract))
                    v.scalar_tensor_tensor(mv[:, 3:4], mv[:, 2:3], mv[:, 2:3], mv[:, 1:2], ALU.mult, ALU.add).then_inc(sem("vd" + tag), 1)
                    dve.wait_ge(sem("gv_ps" + tag), b + 1)
                    v.tensor_scalar(mv[:, 4:5], ps[:, 3, 0:1], eps, None, ALU.add).then_inc(sem("var" + tag + "_ready"), 1)
                    dve.wait_ge(sem("rstd" + tag + "_ready"), b + 1)
                    v.tensor_tensor(mv[:, 6:7], mv[:, 5:6], col(gam), ALU.mult)
                    link(v.tensor_tensor(mv[:, 7:8], mv[:, 2:3], mv[:, 0:1], ALU.subtract))
                    link(v.scalar_tensor_tensor(mv[:, 8:9], mv[:, 7:8], mv[:, 6:7], col(bet), ALU.mult, ALU.add))
                    v.tensor_scalar(dst[:], src[:], mv[:, 6:7], mv[:, 8:9], ALU.mult, ALU.add).then_inc(sem("h" + tag + "_ready"), 1)

                def split(f, hi, lo, ready, done):
                    dve.wait_ge(sem(ready), b + 1)
                    v.tensor_copy(hi[:], f[:]).then_inc(sem(done + "_hi"), 1)
                    dve.wait_ge(sem(done + "_hi"), b + 1)
                    v.tensor_tensor(lo[:], f[:], hi[:].bitcast(F32), ALU.subtract).then_inc(sem(done), 1)

                group_norm(x2, "x2_ready", 4, 1e-6, "gamma", "beta", h2, "2")
                split(qf, qh, ql, "q2_ready", "q2_split")
                split(kf, kh, kl, "k2_ready", "k2_split")
                for i in range(NC):
                    for h in range(NH):
                        u = NH * i + h
                        dve.wait_ge(sem("s2max_ps"), b * NC * NH + (u + 1))
                        v.tensor_reduce(mx[:, i, h:h + 1], ps[:, (6, 7, 0, 1)[u % 4], :], AX.X, ALU.max).then_inc(sem("mx2_ready"), 1)
                dve.wait_ge(sem("mx2_ready"), b * NC * NH + NC * NH)
                v.tensor_reduce(nm2[:], mx[:], AX.X, ALU.max, negate=True).then_inc(sem("nm2_ready"), 1)
                dve.wait_ge(sem("den2_ps"), b + 1)
                link(v.reciprocal(rec[:], two(2)))
                link(v.tensor_tensor(y0[:], two(0), rec[:], ALU.mult))
                v.scalar_tensor_tensor(x3[:], y0[:], cst[:, B2:B2 + 1], x2[:], ALU.add, ALU.add).then_inc(sem("x3_ready"), 1)

                group_norm(x3, "x3_ready", 1, 1e-5, "g1", "beta1", h2, "3")
                split(qf, qh, ql, "q3_ready", "q3_split")
                split(kf, kh, kl, "k3_ready", "k3_split")

                def head_maxima(g):
                    for i in range(GH):
                        for c in range(NC):
                            for h in range(NH):
                                u = ((g * GH + i) * NC + c) * NH + h
                                dve.wait_ge(sem("s3max_ps"), b * HEADS * NC * NH + (u + 1))
                                v.tensor_reduce(mx3[:, i, c, h:h + 1], ps[:, u % 2, :], AX.X, ALU.max).then_inc(sem("mx3_ready"), 1)
                    dve.wait_ge(sem("mx3_ready"), b * HEADS * NC * NH + (g + 1) * GH * NC * NH)
                    v.tensor_reduce(nm3[:], mx3[:].rearrange("p i c h -> p (i c) h"), AX.X, ALU.max,
                                    negate=True).then_inc(sem("nm3_ready"), 1)

                def head_norm(g):
                    dve.wait_ge(sem("og_ready"), b * NG + (g + 1))
                    link(v.reciprocal(rec3[:], og[:]))
                    carry_wait()
                    link(v.stream_shuffle(recs[:], rec3[:], mask=[HD + i % HD for i in range(32)]))
                    v.tensor_tensor(yn[:, g, :], og[:], recs[:], ALU.mult).then_inc(sem("yn_ready"), 1)

                head_maxima(0)
                head_maxima(1)
                head_norm(0)
                head_norm(1)
                dve.wait_ge(sem("o3_ps"), b + 1)
                v.scalar_tensor_tensor(x4[:], two(2), col("b_out"), x3[:], ALU.add, ALU.add).then_inc(sem("x4_ready"), 1)
                group_norm(x4, "x4_ready", 1, 1e-5, "g2", "beta2", h2, "4")
                dve.wait_ge(sem("m4_ps"), b + 1)
                dve.wait_ge(sem("out_done"), 16 * b)
                v.scalar_tensor_tensor(xo[:], two(6), col("b_mlp2"), x4[:], ALU.add, ALU.add).then_inc(sem("xo_ready"), 1)
                assert count[0] == DVE_STEPS, count[0]

        @block.tensor
        def _(pe):
            def mm(o, l, r, start=True, stop=True):
                return nc.tensor.matmul(o, l, r, start=start, stop=stop)

            pe.wait_ge(sem("weights_in"), 16 * len(loads))
            mm(ps[:, 0, 0:128], wv_s[:], wp_s[:])
            mm(ps[:, 1, 0:1], wp_s[:], col("bv")).then_inc(sem("wpv_ps"), 1)
            pe.wait_ge(sem("ident_ready"), 1)
            pe.wait_ge(sem("grp_steps"), 6)
            pe.wait_ge(sem("ones_f_ready"), 1)
            pe.wait_ge(sem("ones_ready"), 1)
            pe.wait_ge(sem("wpv_ready"), 1)
            pe.wait_ge(sem("consts_ready"), 1)
            pe.wait_ge(sem("ph_ones"), 1)
            pe.wait_ge(sem("v_ones"), 1)
            pe.wait_ge(sem("wo_in"), 16 * HEADS)
            pe.wait_ge(sem("k_ones_in"), 16 * GH * 2)

            with pe.Fori(0, B) as b:
                pe.wait_ge(sem("x_in"), 16 * b + 16)
                pe.wait_ge(sem("xo_ready"), b)
                for h in range(NH):
                    last = mm(ps[0:CI, h, :], wth[:], half(xin, h))
                last.then_inc(sem("theta_ps"), 1)
                for h in range(NH):
                    last = mm(ps[:, 2 + h, :], wpg[:], half(xin, h))
                last.then_inc(sem("phig_ps"), 1)
                pe.wait_ge(sem("theta_ready"), b + 1)
                pe.wait_ge(sem("phi_ready"), b + 1)
                for c in range(NC):
                    last = mm(ps[:, 4 + c // 2, M0 * (c % 2):M0 * (c % 2 + 1)], th[0:CI, 128 * c:128 * (c + 1)], ph[0:CI, :])
                    if c % 2:
                        last.then_inc(sem("s0max_ps"), 1)
                pe.wait_ge(sem("g_ready"), b + 1)
                for m in range(2):
                    last = mm(ps[:, 2, 128 * m:128 * (m + 1)], gt[CI:128, 128 * m:128 * (m + 1)], wWT[CI:128, :])
                last.then_inc(sem("wg_ps"), 1)
                pe.wait_ge(sem("nm0_ready"), b * 4 + 4)
                nc.tensor.transpose(ps[0:NC, 3, 0:128], nm0[:], ident[:]).then_inc(sem("nm0T_ps"), 1)
                pe.wait_ge(sem("nm0_row_in"), 16 * b + 16)
                for m in range(2):
                    for h in range(NH):
                        last = mm(ps[:, 4 + 2 * m + h, :], ph[0:CI + 1, 128 * m:128 * (m + 1)], th[0:CI + 1, HALF * h:HALF * (h + 1)])
                    last.then_inc(sem("s0_ps"), 1)
                pe.wait_ge(sem("wg_ready"), b + 1)
                for m in range(2):
                    pe.wait_ge(sem("p0_ready"), b * 2 + (m + 1))
                    for h in range(NH):
                        mm(ps[:, h, :], wg[:, m, :], half(pt0[:, m, :], h), start=m == 0, stop=m == 1)
                for m in range(2):
                    for h in range(NH):
                        last = mm(ps[:, 2 + h, :], ones[:], half(pt0[:, m, :], h), start=m == 0, stop=m == 1)
                last.then_inc(sem("den0_ps"), 1)
                pe.wait_ge(sem("x1_ready"), b + 1)
                x1v = x1[:].rearrange("p (y r x c) -> p y r x c", r=2, c=2, x=QW)
                for k in range(4):
                    last = mm(ps[:, 4, 0:Q].rearrange("p (y x) -> p y x", x=QW), wfc[:, k, :], x1v[:, :, k // 2, :, k % 2],
                              start=k == 0, stop=k == 3)
                last.then_inc(sem("fus_ps"), 1)
                pe.wait_ge(sem("fused_ready"), b + 1)
                for k in range(2):
                    last = nc.tensor.transpose(ps[:, 5, 128 * k:128 * (k + 1)], fused[:, 128 * k:128 * (k + 1)], ident[:])
                last.then_inc(sem("fT_ps"), 1)
                pe.wait_ge(sem("sp_sum"), b + 1)
                pe.wait_ge(sem("sp_ready"), b + 1)
                for k in range(4):
                    last = mm(ps[:, 6, 0:Q], spT[:, k // 2, k % 2:k % 2 + 1].to_broadcast([128, 128]), toep[:, k, :],
                              start=k == 0, stop=k == 3)
                last.then_inc(sem("conv_ps"), 1)
                pe.wait_ge(sem("pool_ready"), b + 1)
                mm(ps[0:HID, 7, 0:2], wca1[:], pool[:]).then_inc(sem("mlp1_ps"), 1)
                pe.wait_ge(sem("hid_ready"), b + 1)
                mm(ps[:, 5, 0:1], wca2[:], hsum[:]).then_inc(sem("mlp2_ps"), 1)
                pe.wait_ge(sem("chout_ready"), b + 1)
                for k in range(4):
                    mm(ps[:, k // 2, Q * (k % 2):Q * (k % 2 + 1)], wpr[:, 128 * k:128 * (k + 1)], chout[:]).then_inc(sem("proj_ps"), 1)

                def group_averages(t, tag):
                    pe.wait_ge(sem("mv" + tag), b + 1)
                    mm(ps[:, 3, 0:1], t[:], mv[:, 0:1]).then_inc(sem("gm_ps" + tag), 1)
                    pe.wait_ge(sem("vd" + tag), b + 1)
                    mm(ps[:, 3, 0:1], t[:], mv[:, 3:4]).then_inc(sem("gv_ps" + tag), 1)

                group_averages(grp8, "2")
                pe.wait_ge(sem("h2_ready"), b + 1)
                for name, w, k in (("q2_ps", wq_s, 0), ("k2_ps", wk_s, 2)):
                    for h in range(NH):
                        last = mm(ps[:, k + h, :], w[:], half(h2, h))
                    last.then_inc(sem(name), 1)
                for c in range(NC):
                    last = mm(ps[:, 4 + c // 4, 128 * (c % 4):128 * (c % 4 + 1)], h2[:, 128 * c:128 * (c + 1)], wpv[:])
                last.then_inc(sem("v2_ps"), 1)
                pe.wait_ge(sem("q2_split"), b + 1)
                pe.wait_ge(sem("k2_split_hi"), b + 1)
                for c in range(NC):
                    for h in range(NH):
                        u = NH * c + h
                        if u >= 4:
                            pe.wait_ge(sem("mx2_ready"), b * NC * NH + (u - 3))
                        mm(ps[:, (6, 7, 0, 1)[u % 4], :], qh[:, 128 * c:128 * (c + 1)], half(kh, h)).then_inc(sem("s2max_ps"), 1)
                pe.wait_ge(sem("nm2_ready"), b + 1)
                nc.tensor.transpose(ps[0:NC, 2, 0:128], nm2[:], ident[:]).then_inc(sem("nm2T_ps"), 1)
                pe.wait_ge(sem("k2_split"), b + 1)
                pe.wait_ge(sem("v2_ready"), b + 1)
                pe.wait_ge(sem("nm2_row_in"), 16 * b + 16)

                def scores2(j):
                    k = slice(128 * j, 128 * (j + 1))
                    for h in range(NH):
                        u = NH * j + h
                        if u >= 4:
                            pe.wait_ge(sem("p2_ready"), b * NC * NH + (u - 3))
                        o = ps[:, 4 + u % 4, :]
                        mm(o, kh[:, k], half(qh, h), stop=False)
                        mm(o, kh[:, k], half(ql, h), start=False, stop=False)
                        mm(o, kl[:, k], half(qh, h), start=False, stop=False)
                        mm(o, ones_r[0:1, :], half(nmrow, h), start=False).then_inc(sem("s2_ps"), 1)

                scores2(0)
                for j in range(NC):
                    if j + 1 < NC:
                        scores2(j + 1)
                    pe.wait_ge(sem("p2_ready"), b * NC * NH + NH * (j + 1))
                    for h in range(NH):
                        last = mm(ps[:, h, :], vT[:, j, :], half(pt2[:, j % 2, :], h), start=j == 0, stop=j == NC - 1)
                    last.then_inc(sem("pv2_done"), 1)
                pe.wait_ge(sem("acc_steps"), b * (NC - 1) + (NC - 1))
                for h in range(NH):
                    last = mm(ps[:, 2 + h, :], ones[:], half(acc, h))
                last.then_inc(sem("den2_ps"), 1)

                pe.wait_ge(sem("x3_ready"), b + 1)
                group_averages(grp4, "3")
                pe.wait_ge(sem("h3_ready"), b + 1)
                for name, k, o in (("q3_ps", 4, 0), ("k3_ps", 6, 128)):
                    for h in range(NH):
                        last = mm(ps[:, k + h, :], wqkv[:, o:o + 128], half(h2, h))
                    last.then_inc(sem(name), 1)
                for c in range(NC):
                    last = mm(ps[:, 2 + c // 4, 128 * (c % 4):128 * (c % 4 + 1)], h2[:, 128 * c:128 * (c + 1)], wqkv[:, 256:384])
                last.then_inc(sem("v3_ps"), 1)
                pe.wait_ge(sem("packed"), 16 * HEADS * 6 * b + 16 * HEADS * 6)
                pe.wait_ge(sem("v3_ready"), b + 1)
                pe.wait_ge(sem("q3_ready"), b + 1)
                pe.wait_ge(sem("k3_ready"), b + 1)

                def maxima3(g, n):
                    per = GH * NC * NH // 16
                    for m in range(per):
                        u = g * GH * NC * NH + n * per + m
                        hd, c, h = u // (NC * NH), u // NH % NC, u % NH
                        r, t = 64 * (hd % 2), hd // 2
                        if u >= 2:
                            pe.wait_ge(sem("mx3_ready"), b * HEADS * NC * NH + (u - 1))
                        mm(ps[:, u % 2, :], qp[r:r + PACK, t, 128 * c:128 * (c + 1)],
                           kp[r:r + PACK, t, HALF * h:HALF * (h + 1)]).then_inc(sem("s3max_ps"), 1)

                def max_rows3(g):
                    pe.wait_ge(sem("nm3_ready"), b * NG + (g + 1))
                    nc.tensor.transpose(ps[0:GH * NC, 0, 0:128], nm3[:], ident[:]).then_inc(sem("nm3T_ps"), 1)

                def scores3(s):
                    g, j, h = s // (NC * NH), s // NH % NC, s % NH
                    for i in range(GH):
                        hd, u = GH * g + i, s * GH + i
                        r, t = 64 * (hd % 2), hd // 2
                        if u >= 4:
                            pe.wait_ge(sem("p3_ready"), b * HEADS * NC * NH + (u - 3))
                        mm(ps[:, 2 + u % 4, :], kp[r:r + PACK + 1, t, 128 * j:128 * (j + 1)],
                           qp[r:r + PACK + 1, t, HALF * h:HALF * (h + 1)]).then_inc(sem("s3_ps"), 1)

                def values3(s):
                    g, j, h = s // (NC * NH), s // NH % NC, s % NH
                    pe.wait_ge(sem("p3_ready"), b * HEADS * NC * NH + (s + 1) * GH)
                    for i in range(GH):
                        last = mm(ps[32 * i:32 * (i + 1), 6 + h, :], vt3[:, j, GH * g + i, :], p3[:, s % 2, i, :],
                                  start=j == 0, stop=j == NC - 1)
                    last.then_inc(sem("pv3_done"), 1)

                for n in range(16):
                    maxima3(0, n)
                max_rows3(0)
                for g in range(NG):
                    pe.wait_ge(sem("nm3_row_in"), 16 * (b * HEADS + GH * (g + 1)))
                    if g:
                        pe.wait_ge(sem("og_ready"), b * NG + g)
                    S = NC * NH
                    scores3(g * S)
                    if g + 1 < NG:
                        pe.wait_ge(sem("nm3T_ready"), b * NG + (g + 1))
                    for s in range(S):
                        if s + 1 < S:
                            scores3(g * S + s + 1)
                        if g + 1 < NG:
                            maxima3(g + 1, s)
                        values3(g * S + s)
                    if g + 1 < NG:
                        max_rows3(g + 1)
                pe.wait_ge(sem("yn_ready"), b * NG + NG)
                for g in range(NG):
                    for h in range(NH):
                        last = mm(ps[:, 2 + h, :], wo[:, g, :], half(yn[:, g, :], h), start=g == 0, stop=g == NG - 1)
                last.then_inc(sem("o3_ps"), 1)
                group_averages(grp4, "4")
                pe.wait_ge(sem("h4_ready"), b + 1)
                for h in range(NH):
                    last = mm(ps[0:MLP, 4 + h, :], wm1[:], half(h2, h))
                last.then_inc(sem("h4_ps"), 1)
                pe.wait_ge(sem("gelu_ready"), b + 1)
                for h in range(NH):
                    last = mm(ps[:, 6 + h, :], wm2[:], half(gl, h))
                last.then_inc(sem("m4_ps"), 1)


def kernel(**inputs):
    import concourse.bacc as bacc
    from concourse.bass_utils import run_bass_kernel_spmd

    i = {k.replace("_conv_", "_"): np.asarray(v) for k, v in inputs.items()}

    def t(a):
        return np.ascontiguousarray(a.T)

    cols = {k: i["L0_" + k] for k in ("b_W", "bn_gamma", "bn_beta", "bn_mean", "bn_var")}
    cols |= {k: i["L1_" + k] for k in ("fusion_b", "bn1_g", "bn1_b", "bn1_m", "bn1_v")}
    for k in ("proj_b", "bn2_g", "bn2_b", "bn2_m", "bn2_v"):
        for n in range(4):
            cols[f"{k}{n}"] = i["L1_" + k][C * n:C * (n + 1)]
    cols |= {k: i["L2_" + k] for k in ("gamma", "beta", "bq", "bk", "bv", "bp")}
    cols |= {k: i["L3_" + k] for k in ("b_out", "g1", "beta1", "g2", "beta2", "b_mlp2")}
    cols["temp"] = np.repeat(i["L3_temperature"].reshape(HEADS), HD)
    cols["b_phig"] = np.concatenate([i["L0_b_phi"], i["L0_b_g"]])
    arrays = {
        "x": np.ascontiguousarray(i["x"]),
        "vecs": np.ascontiguousarray(np.stack([cols[k] for k in VECS], axis=1)),
        "w_theta": t(i["L0_w_theta"]),
        "b_theta": np.ascontiguousarray(i["L0_b_theta"].reshape(CI, 1)),
        "w_phig": t(np.concatenate([i["L0_w_phi"], i["L0_w_g"]])),
        "w_W": t(i["L0_w_W"]),
        "w_fuse": np.ascontiguousarray(i["L1_fusion_w"].reshape(C, 4, C).transpose(2, 1, 0).reshape(C, 4 * C)),
        "sa_w": np.ascontiguousarray(i["L1_sa_w"].reshape(2, TAPS, TAPS)),
        "ca_w1": t(i["L1_ca_w1"]),
        "ca_w2": t(i["L1_ca_w2"]),
        "w_proj": t(i["L1_proj_w"]),
        "wq": t(i["L2_wq"]),
        "wk": t(i["L2_wk"]),
        "wv": np.ascontiguousarray(i["L2_wv"]),
        "wp": t(i["L2_wp"]),
        "w_qkv": t(i["L3_w_qkv"]),
        "w_out": t(i["L3_w_out"]),
        "w_mlp1": t(i["L3_w_mlp1"]),
        "b_mlp1": np.ascontiguousarray(i["L3_b_mlp1"].reshape(MLP, 1)),
        "w_mlp2": t(i["L3_w_mlp2"]),
    }
    nc = bacc.Bacc("TRN2", target_bir_lowering=False, num_devices=1)
    aps = [nc.dram_tensor(f"in_{k}", a.shape, mybir.dt.from_np(a.dtype), kind="ExternalInput").ap() for k, a in arrays.items()]
    out = nc.dram_tensor("out", (B, C, H, W), F32, kind="ExternalOutput").ap()
    nc.disable_value_cache = True
    build(nc, *aps, out)
    r = run_bass_kernel_spmd(nc, [{f"in_{k}": a for k, a in arrays.items()}], core_ids=[0])
    return r.results[0]["out"]
```

```python
import numpy as np

import concourse.bass as bass
from concourse import mybir
from concourse.alu_op_type import AluOpType as ALU
from contextlib import ExitStack

F32 = mybir.dt.float32
F32R = mybir.dt.float32r
ACT = mybir.ActivationFunctionType
AX = mybir.AxisListType

B, C, H, W = 8, 128, 32, 32
N = H * W
HALF = 512
NH = N // HALF
NC = N // 128
CI = 64
M0 = N // 4
Q = N // 4
QW = W // 2
HID = 8
TAPS, PADW = 7, 2 * QW - 1
HEADS, HD = 8, 16
GH = 4
NG = HEADS // GH
MLP = 32
PACK = 3 * HD
ROWS = 64 + PACK
TILES = GH * NC * NH
STEPS = NC * NH
LAPS = GH * (STEPS + 1)
M_FIRST, M_LAPS = 6, 52
TL = 2
A2 = (19, 35)
A3 = 53
L0 = 66
HN = 88
L1 = 93
L2 = 109
GN = 6

VECS = ["b_W", "bn_gamma", "bn_beta", "bn_mean", "bn_var", "fusion_b", "bn1_g", "bn1_b", "bn1_m", "bn1_v",
        "proj_b0", "proj_b1", "proj_b2", "proj_b3", "bn2_g0", "bn2_g1", "bn2_g2", "bn2_g3",
        "bn2_b0", "bn2_b1", "bn2_b2", "bn2_b3", "bn2_m0", "bn2_m1", "bn2_m2", "bn2_m3",
        "bn2_v0", "bn2_v1", "bn2_v2", "bn2_v3", "gamma", "beta", "bq", "bk", "bv", "bp",
        "temp", "b_out", "g1", "beta1", "g2", "beta2", "b_mlp2", "b_phig"]
V = {name: i for i, name in enumerate(VECS)}


def key_at(h, j):
    return A2[h] + 3 * j // 2


class Batch:

    def __init__(self, b, off=0):
        self.b, self.off = (b + off, 0) if isinstance(b, int) else (b, off)

    def __add__(self, n):
        return Batch(self.b, self.off + n)

    def is_number(self, n):
        return isinstance(self.b, int) and self.b == n

    def count(self, per, k):
        return self.b * per + (self.off * per + k)


def wait(eng, sem, batch, per=1, k=None):
    k = per if k is None else k
    value = batch.count(per, k)
    if isinstance(value, int):
        value = min(value, B * per)
        if value <= 0:
            return
    eng.wait_ge(sem, value)


class Side:

    def __init__(self, *parts):
        self.parts = (at for part in parts for at in part)
        self.at = next(self.parts, None)

    def upto(self, p):
        while self.at is not None and self.at <= p:
            self.at = next(self.parts, None)

    def finish(self):
        self.upto(4 * LAPS)


def maxima_at(p):
    return [u for u in range(TILES) if M_FIRST + u * M_LAPS // TILES == p]


def walk(eng, start, non_local, wavelet, attention, head_norm, tail, passes):

    def window(bt, tail_before=True, attend_next=True, begin_after=True, heads=True):
        parts = []
        if tail_before:
            parts += [head_norm(bt + -1, 1, TL), tail(bt + -1)]
        if attend_next:
            parts.append(attention(bt + 1))
        if begin_after:
            parts.append(non_local(bt + 2))
        if heads:
            parts.append(head_norm(bt, 0, HN))
        if begin_after:
            parts.append(wavelet(bt + 2))
        passes(bt, Side(*parts), heads, attend_next or not heads)

    start()
    Side(non_local(Batch(0)), wavelet(Batch(0)), attention(Batch(0))).finish()
    window(Batch(-1), tail_before=False, attend_next=False, heads=False)
    window(Batch(0), tail_before=False)
    with eng.Fori(1, B - 2) as b:
        window(Batch(b))
    window(Batch(B - 2), begin_after=False)
    window(Batch(B - 1), attend_next=False, begin_after=False)
    Side(head_norm(Batch(B - 1), 1, TL), tail(Batch(B - 1))).finish()


def build(nc, x, vecs, w_theta, b_theta, w_phig, w_W, w_fuse, sa_w, ca_w1, ca_w2, w_proj,
          wq, wk, wv, wp, w_qkv, w_out, w_mlp1, b_mlp1, w_mlp2, out):
    pad_dram = nc.dram_tensor("padded_taps", [2, PADW, PADW], F32, kind="Internal").ap()
    xd = x.rearrange("b c h w -> b c (h w)")
    od = out.rearrange("b c h w -> b c (h w)")

    with ExitStack() as ctx:
        def sb(name, shape, dt=F32):
            return ctx.enter_context(nc.sbuf_tensor(name, shape, dt))

        sems = {}

        def sem(name):
            if name not in sems:
                sems[name] = ctx.enter_context(nc.semaphore(name))
            return sems[name]

        ident = sb("ident", [128, 128])
        ones = sb("ones", [128, 128])
        ones_r = sb("ones_r", [128, 128], F32R)
        grp8 = sb("grp8", [128, 128])
        grp4 = sb("grp4", [128, 128])
        neg_half = sb("neg_half", [128, 16])
        vec = sb("vec", [128, len(VECS)])
        wth = sb("wth", [128, CI])
        bth = sb("bth", [CI, 1])
        wpg = sb("wpg", [128, 128])
        wWT = sb("wWT", [128, 128])
        wfc = sb("wfc", [128, 4, 128])
        wca1 = sb("wca1", [128, HID])
        wca2 = sb("wca2", [HID, 128])
        wpr = sb("wpr", [128, 4 * 128])
        wq_s = sb("wq_s", [128, 128])
        wk_s = sb("wk_s", [128, 128])
        wpv = sb("wpv", [128, 128])
        wqkv = sb("wqkv", [128, 3 * 128])
        wo = sb("wo", [128, NG, 128])
        wm1 = sb("wm1", [128, MLP])
        bm1 = sb("bm1", [MLP, 1])
        wm2 = sb("wm2", [MLP, 128])
        toep = sb("toep", [128, 4, Q])
        idle = sb("idle", [128, 4])
        cst = sb("cst", [128, 32])
        tmpc = sb("tmpc", [128, 64])

        xin = sb("xin", [128, N])
        th = sb("th", [128, N])
        ph = sb("ph", [128, M0])
        phz = sb("phz", [128, M0])
        pg = sb("pg", [128, M0])
        gt = sb("gt", [128, M0])
        wg = sb("wg", [128, 2, 128])
        nm0 = sb("nm0", [128, NC])
        nm0T = sb("nm0T", [NC, 128])
        inv = sb("inv", [128, NC])
        rec = sb("rec", [128, N])
        ysb = sb("ysb", [128, N])
        x1 = sb("x1", [128, N])
        fused = sb("fused", [128, Q])
        spT = sb("spT", [128, 2, 2])
        sg = sb("sg", [128, 3, Q])
        spat = sb("spat", [128, Q])
        pool = sb("pool", [128, 2])
        hid = sb("hid", [HID, 2])
        hsum = sb("hsum", [HID, 1])
        chm = sb("chm", [128, 4])
        chout = sb("chout", [128, Q])
        pj = sb("pj", [128, 4, Q])
        sd = ysb[:].rearrange("p (a b q) -> p a b q", a=2, b=2)
        ux = rec
        x2 = sb("x2", [128, N])
        st = sb("st", [128, 2, 6])
        mv = sb("mv", [128, 16])
        hn = sb("hn", [128, N])
        qf, kf = ysb, rec
        qh = sb("qh", [128, N], F32R)
        ql = sb("ql", [128, N], F32R)
        kh = sb("kh", [128, N], F32R)
        kl = sb("kl", [128, N], F32R)
        vT = sb("vT", [128, NC, 128])
        mx = sb("mx", [128, NC, NH])
        nm2 = sb("nm2", [128, NC])
        nm2T = sb("nm2T", [NC, 128], F32R)
        nmrow = sb("nmrow", [1, N], F32R)
        p2 = sb("p2", [128, 4, HALF])
        p0 = p2[:].rearrange("p (m h) n -> p m (h n)", m=2)
        acc = sb("acc", [128, NH, HALF])
        x3 = sb("x3", [128, N])
        x3s = sb("x3s", [128, N])
        q3h = sb("q3h", [128, N], F32R)
        q3l = sb("q3l", [128, N], F32R)
        k3h = sb("k3h", [128, N], F32R)
        k3l = sb("k3l", [128, N], F32R)
        qp = sb("qp", [128, HEADS // 2, N], F32R)
        kp = sb("kp", [128, HEADS, N], F32R)
        v3 = sb("v3", [128, NC, HEADS, HD])
        vt3 = [sb(f"vt3_{g}", [128, NC, GH, 32]) for g in range(NG)]
        mx3 = sb("mx3", [128, GH, NC, NH])
        nm3 = sb("nm3", [128, GH * NC])
        nm3T = sb("nm3T", [GH * NC, 128], F32R)
        p3 = sb("p3", [128, 2, GH, HALF])
        og = sb("og", [128, NG, N])
        inv3 = sb("inv3", [128, NC, GH])
        inv3w = ysb[:].rearrange("p (c i r) -> p c i r", i=GH, r=32)
        den_row = sb("den_row", [128, GH])
        x4 = ysb
        gl = x1[0:MLP, :]
        xo = x1
        toep_rev = p3[:, 0, 0:2, :].rearrange("p a (b q) -> p (a b) q", q=Q)
        pad_sb = p3[0:2, 1, 0:2, :].rearrange("p a b -> p (a b)")[:, 0:PADW * PADW]
        wfu = p3[:, 1, 2, :].rearrange("p (k o) -> p k o", k=4)
        wv_s, wp_s = p3[:, 1, 3, 0:128], p3[:, 1, 3, 128:256]
        wfs = pj[:, :, 0:128]

        ps = ctx.enter_context(nc.psum_tensor("ps", [128, 8, HALF], F32))
        MB, SB, FB, VB = 0, 2, 4, 6

        def two(k):
            return ps[:, k:k + 2, :].rearrange("p a b -> p (a b)")

        def col(name, rows=128):
            return vec[0:rows, V[name]:V[name] + 1]

        def raw(ap):
            return ap.bitcast(F32)

        def half(t, h):
            return t[:, HALF * h:HALF * (h + 1)]

        def part(t, c):
            return t[:, 128 * c:128 * (c + 1)]

        def bank_part(k, c):
            return ps[:, k + c // 4, 128 * (c % 4):128 * (c % 4 + 1)]

        INV0, C0, INV1, C1, INV2, C2, BQS, B2, BO, TMP = 0, 1, 2, 3, 4, 8, 12, 13, 14, 15
        QS = float(C) ** -0.5

        loads = [
            (vec[:], vecs), (wth[:], w_theta), (bth[:], b_theta), (wpg[:], w_phig), (wWT[CI:128, :], w_W),
            (wfu.rearrange("p k o -> p (k o)"), w_fuse), (wca1[:], ca_w1), (wca2[:], ca_w2), (wpr[:], w_proj),
            (wq_s[:], wq), (wk_s[:], wk), (wv_s, wv), (wp_s, wp), (wqkv[:], w_qkv),
            (wm1[:], w_mlp1), (bm1[:], b_mlp1), (wm2[:], w_mlp2),
        ]

        block = ctx.enter_context(nc.Block())

        @block.sync
        def _(sp):
            def start():
                for dst, src in loads:
                    sp.dma_start(dst, src).then_inc(sem("weights_in"), 16)
                sp.wait_ge(sem("wo_zeroed"), 1)
                for h in range(HEADS):
                    r = 32 * (h % GH)
                    sp.dma_start(wo[r:r + HD, h // GH, :], w_out[HD * h:HD * (h + 1), :]).then_inc(sem("wo_in"), 16)
                sp.wait_ge(sem("pad_zeroed"), 1)
                p3d = pad_sb.rearrange("c (a b) -> c a b", b=PADW)
                lo = QW - 1 - TAPS // 2
                sp.dma_start(p3d[:, lo:lo + TAPS, lo:lo + TAPS], sa_w).then_inc(sem("taps_in"), 16)
                sp.wait_ge(sem("taps_in"), 16)
                sp.dma_start(pad_dram.rearrange("c a b -> c (a b)"), pad_sb).then_inc(sem("pad_out"), 16)
                sp.wait_ge(sem("pad_out"), 16)
                for c in range(2):
                    for yy in range(QW):
                        win = pad_dram[c, yy:yy + QW, 0:QW]
                        src = bass.AP(tensor=win.tensor, offset=win.offset, ap=[[1, QW], [PADW, QW], [1, QW]])
                        r = QW * (yy % 8)
                        sp.dma_start(toep_rev[r:r + QW, 2 * c + yy // 8, :].rearrange("p (a b) -> p a b", b=QW),
                                     src).then_inc(sem("windows_in"), 16)
                sp.wait_ge(sem("ones_ready"), 1)
                sp.wait_ge(sem("packs_zeroed"), 2)
                for hd in range(HEADS):
                    r = 126 + hd % 2
                    sp.dma_start(raw(kp[r:r + 1, hd, :]).rearrange("p (a b) -> p a b", b=128),
                                 raw(ones_r[0:NC, :])).then_inc(sem("k_ones_in"), 16)

            def non_local(bt):
                yield L0 - 4
                wait(sp, sem("x1_ready"), bt + -1)
                sp.dma_start(xin[:], xd[bt.b + bt.off, :, :]).then_inc(sem("x_in"), 16)
                yield L0 + 9
                wait(sp, sem("nm0T_ready"), bt)
                sp.dma_start(th[CI:CI + 1, :].rearrange("p (a b) -> p a b", b=128), nm0T[:]).then_inc(sem("nm0_row_in"), 16)

            def wavelet(bt):
                yield L2 + GN + 15
                wait(sp, sem("nm2T_ready"), bt)
                sp.dma_start(raw(nmrow[0:1, :]).rearrange("p (a b) -> p a b", b=128), raw(nm2T[:])).then_inc(sem("nm2_row_in"), 16)

            def attention(bt):
                yield A3

            def head_norm(bt, g, at):
                yield at

            def tail(bt):
                yield TL + GN + 11
                wait(sp, sem("xo_ready"), bt)
                sp.dma_start(od[bt.b + bt.off, :, :], xo[:]).then_inc(sem("out_done"), 16)

            def pack(bt, g, i):
                hd = GH * g + i
                r, c = 64 * (hd % 2), HD * hd
                if i == 0:
                    wait(sp, sem("vt3_ready"), bt, NG, g + 1)
                for dst, parts in ((qp[:, hd // 2, :], (q3h, q3l, q3h)), (kp[:, hd, :], (k3h, k3h, k3l))):
                    for n, part3 in enumerate(parts):
                        sp.dma_start(raw(dst[r + HD * n:r + HD * (n + 1), :]), raw(part3[c:c + HD, :])).then_inc(sem(f"packed{i // 2}"), 16)

            def passes(bt, side, heads, more):
                for g, (mb, mg, maxima) in enumerate(((bt, 1, heads), (bt + 1, 0, more))):
                    for p in range(LAPS):
                        if maxima and p % 3 == 0 and p // 3 < GH:
                            pack(mb, mg, p // 3)
                        if maxima and p == M_FIRST + M_LAPS:
                            wait(sp, sem("nm3T_ready"), mb, NG, mg + 1)
                            for i in range(GH):
                                hd = GH * mg + i
                                r = 126 + hd % 2
                                sp.dma_start(raw(qp[r:r + 1, hd // 2, :]).rearrange("p (a b) -> p a b", b=128),
                                             raw(nm3T[NC * i:NC * (i + 1), :])).then_inc(sem("nm3_row_in"), 16)
                        side.upto(LAPS * g + p)
                side.finish()

            walk(sp, start, non_local, wavelet, attention, head_norm, tail, passes)
            sp.wait_ge(sem("out_done"), 16 * B)

        @block.gpsimd
        def _(pool_e):
            g = nc.gpsimd

            def start():
                g.memset(wo[:], 0.0).then_inc(sem("wo_zeroed"), 1)
                g.memset(raw(qp[:]), 0.0).then_inc(sem("packs_zeroed"), 1)
                g.memset(pad_sb, 0.0).then_inc(sem("pad_zeroed"), 1)
                g.memset(neg_half[:], -0.5).then_inc(sem("neg_half_ready"), 1)
                g.memset(ident[:], 0.0).then_inc(sem("ident_zeroed"), 1)
                pool_e.wait_ge(sem("ident_zeroed"), 1)
                g.affine_select(out=ident[:], in_=ident[:], compare_op=ALU.not_equal, fill=1.0, base=0,
                                pattern=[[-1, 128]], channel_multiplier=1).then_inc(sem("ident_ready"), 1)
                for k, (t, width) in enumerate(((grp8, 8), (grp4, 4))):
                    g.memset(t[:], 1.0 / width).then_inc(sem("grp_steps"), 1)
                    pool_e.wait_ge(sem("grp_steps"), 3 * k + 1)
                    v = t[:].rearrange("p (a b) -> p a b", b=width)
                    g.affine_select(out=v, in_=v, compare_op=ALU.is_ge, fill=0.0, base=0,
                                    pattern=[[-width, 128 // width], [0, width]], channel_multiplier=1).then_inc(sem("grp_steps"), 1)
                    pool_e.wait_ge(sem("grp_steps"), 3 * k + 2)
                    g.affine_select(out=v, in_=v, compare_op=ALU.is_ge, fill=0.0, base=width - 1,
                                    pattern=[[width, 128 // width], [0, width]], channel_multiplier=-1).then_inc(sem("grp_steps"), 1)
                g.memset(den_row[:], 0.0).then_inc(sem("den_row_steps"), 1)
                pool_e.wait_ge(sem("den_row_steps"), 1)
                g.affine_select(out=den_row[:], in_=den_row[:], compare_op=ALU.not_equal, fill=1.0, base=-HD,
                                pattern=[[-32, GH]], channel_multiplier=1).then_inc(sem("den_row_steps"), 1)
                pool_e.wait_ge(sem("vars_ready"), 1)
                pool_e.wait_ge(sem("neg_half_ready"), 1)
                g.tensor_tensor(tmpc[:, 8:14], tmpc[:, 0:6], neg_half[:, 0:6], ALU.pow).then_inc(sem("rsq_ready"), 1)

            def rstd(bt, tag):
                wait(pool_e, sem("var" + tag + "_ready"), bt)
                g.tensor_tensor(mv[:, 5:6], mv[:, 4:5], neg_half[:, 0:1], ALU.pow).then_inc(sem("rstd" + tag + "_ready"), 1)

            def non_local(bt):
                yield L0

            def wavelet(bt):
                yield L2 + 4
                rstd(bt, "2")

            def attention(bt):
                for h in range(NH):
                    for j in range(1, NC):
                        yield key_at(h, j) + 1
                        u = NC * h + j
                        wait(pool_e, sem("p2_ready"), bt, NC * NH, u + 1)
                        if j > 1:
                            wait(pool_e, sem("acc_steps"), bt, (NC - 1) * NH, h * (NC - 1) + j - 1)
                        first = p2[:, (u - 1) % 4, :] if j == 1 else acc[:, h, :]
                        g.tensor_tensor(acc[:, h, :], first, p2[:, u % 4, :], ALU.add).then_inc(sem("acc_steps"), 1)
                yield A3 + 4
                rstd(bt, "3")

            def head_norm(bt, grp, at):
                yield at

            def tail(bt):
                yield TL + 9
                rstd(bt, "4")

            def passes(bt, side, heads, more):
                side.finish()

            walk(pool_e, start, non_local, wavelet, attention, head_norm, tail, passes)

        @block.scalar
        def _(act):
            a = nc.scalar

            def start():
                act.wait_ge(sem("ones_f_ready"), 1)
                a.copy(ones_r[:], ones[:]).then_inc(sem("ones_ready"), 1)
                act.wait_ge(sem("wpv_ps"), 1)
                a.copy(wpv[:], ps[:, 0, 0:128]).then_inc(sem("wpv_ready"), 1)
                act.wait_ge(sem("consts_ready"), 1)

            def non_local(bt):
                yield L0 + 1
                wait(act, sem("theta_ps"), bt)
                a.activation(th[0:CI, :], two(FB)[0:CI, :], ACT.Identity, bias=bth[:, 0:1]).then_inc(sem("theta_ready"), 1)
                yield L0 + 8
                wait(act, sem("nm0T_ps"), bt)
                a.copy(nm0T[:], ps[0:NC, FB + 1, 0:128]).then_inc(sem("nm0T_ready"), 1)
                wait(act, sem("wg_ps"), bt)
                a.copy(wg[:].rearrange("p a b -> p (a b)"), ps[:, FB, 0:256]).then_inc(sem("wg_ready"), 1)
                for m in range(2):
                    yield L0 + 12 + 2 * m
                    wait(act, sem("s0_ps"), bt, 2, m + 1)
                    a.activation(p0[:, m, :], two(FB), ACT.Exp).then_inc(sem("p0_ready"), 1)

            def wavelet(bt):
                yield L1 + 1
                wait(act, sem("fus_ps"), bt)
                a.activation(fused[:], ps[:, FB, 0:Q], ACT.Relu, bias=cst[:, C1:C1 + 1],
                             scale=cst[:, INV1:INV1 + 1]).then_inc(sem("fused_ready"), 1)
                yield L1 + 5
                wait(act, sem("conv_ps"), bt)
                a.activation(sg[:, 0, :], ps[:, FB, 0:Q], ACT.Exp, scale=-1.0).then_inc(sem("sg_exp"), 1)
                yield L1 + 8
                wait(act, sem("mlp1_ps"), bt)
                a.activation(hid[:], ps[0:HID, FB + 1, 0:2], ACT.Relu, accum_out=hsum[:, 0:1]).then_inc(sem("hid_ready"), 1)
                yield L1 + 10
                wait(act, sem("mlp2_ps"), bt)
                a.activation(chm[:, 0:1], ps[:, FB, 0:1], ACT.Exp, scale=-1.0).then_inc(sem("chm_exp"), 1)
                yield L1 + 13
                for k in range(4):
                    wait(act, sem("proj_ps"), bt, 2, k // 2 + 1)
                    a.activation(pj[:, k, :], ps[:, FB + k // 2, Q * (k % 2):Q * (k % 2 + 1)], ACT.Relu,
                                 bias=cst[:, C2 + k:C2 + k + 1],
                                 scale=cst[:, INV2 + k:INV2 + k + 1]).then_inc(sem("pj_ready"), 1)
                yield L2 + GN + 1
                wait(act, sem("q2_ps"), bt)
                a.activation(qf[:], two(FB), ACT.Identity, bias=cst[:, BQS:BQS + 1], scale=QS).then_inc(sem("q2_ready"), 1)
                yield L2 + GN + 3
                wait(act, sem("k2_ps"), bt)
                a.activation(kf[:], two(FB), ACT.Identity, bias=col("bk")).then_inc(sem("k2_ready"), 1)
                yield L2 + GN + 5
                wait(act, sem("v2_ps"), bt)
                a.copy(vT[:].rearrange("p a b -> p (a b)"), two(FB)).then_inc(sem("v2_ready"), 1)
                yield L2 + GN + 14
                wait(act, sem("nm2T_ps"), bt)
                a.copy(nm2T[:], ps[0:NC, FB, 0:128]).then_inc(sem("nm2T_ready"), 1)

            def attention(bt):
                for h in range(NH):
                    for j in range(NC):
                        yield key_at(h, j)
                        u = NC * h + j
                        if u >= 4:
                            wait(act, sem("pv2_done"), bt, NC * NH, u - 3)
                            hh, jj = divmod(u - 4, NC)
                            wait(act, sem("acc_steps"), bt, (NC - 1) * NH, hh * (NC - 1) + max(jj, 1))
                        wait(act, sem("s2_ps"), bt, NC * NH, u + 1)
                        a.activation(p2[:, u % 4, :], ps[:, FB, :], ACT.Exp).then_inc(sem("p2_ready"), 1)
                    yield A2[h] + 13
                    wait(act, sem("pv2_done"), bt, NC * NH, NC * (h + 1))
                    a.copy(half(ysb, h), ps[:, FB + 1, :]).then_inc(sem("y2_ready"), 1)
                yield A3 + GN + 1
                wait(act, sem("q3_ps"), bt)
                a.activation(qf[:], two(FB), ACT.Copy, scale=cst[:, TMP:TMP + 1]).then_inc(sem("q3_ready"), 1)
                yield A3 + GN + 3
                wait(act, sem("k3_ps"), bt)
                a.copy(kf[:], two(FB)).then_inc(sem("k3_ready"), 1)
                yield A3 + GN + 5
                wait(act, sem("v3_ps"), bt)
                wait(act, sem("vt3_ready"), bt + -1, NG)
                a.copy(v3[:].rearrange("p j h d -> p (j h d)"), two(FB)).then_inc(sem("v3_ready"), 1)

            def head_norm(bt, g, at):
                yield at

            def tail(bt):
                yield TL + GN + 8
                wait(act, sem("h4_ps"), bt)
                a.activation(gl, two(FB)[0:MLP, :], ACT.Gelu, bias=bm1[:, 0:1]).then_inc(sem("gelu_ready"), 1)

            def passes(bt, side, heads, more):
                for g, (mb, mg, maxima) in enumerate(((bt, 1, heads), (bt + 1, 0, more))):
                    for p in range(LAPS):
                        s, i = divmod(p, GH)
                        if p == 0 and maxima:
                            wait(act, sem("k3_split"), mb)
                            wait(act, sem("v3_ready"), mb)
                            wait(act, sem("pv3_done"), mb + -1, NG * STEPS, (mg + 1) * STEPS)
                            a.copy(vt3[mg][:, :, :, 0:HD], v3[:, :, GH * mg:GH * (mg + 1), :]).then_inc(sem("vt3_ready"), 1)
                        if heads and s < STEPS:
                            step = g * STEPS + s
                            if i == 0 and step >= 2:
                                wait(act, sem("pv3_done"), bt, NG * STEPS, step - 1)
                            elif i == 0:
                                wait(act, sem("pv3_done"), bt + -1, NG * STEPS, NG * STEPS - 1 + step)
                            u = g * TILES + p
                            wait(act, sem("s3_ps"), bt, NG * TILES, u + 1)
                            a.activation(p3[:, s % 2, i, :], ps[:, SB + p % 2, :], ACT.Exp).then_inc(sem("p3_ready"), 1)
                        if maxima and p == M_FIRST + M_LAPS:
                            wait(act, sem("nm3T_ps"), mb, NG, mg + 1)
                            a.copy(nm3T[:], ps[0:GH * NC, MB, 0:128]).then_inc(sem("nm3T_ready"), 1)
                        side.upto(LAPS * g + p)
                    if heads:
                        wait(act, sem("o3_ps"), bt + -1)
                        wait(act, sem("pv3_done"), bt, NG * STEPS, (g + 1) * STEPS)
                        a.copy(og[:, g, :], two(VB)).then_inc(sem("og_ready"), 1)
                side.finish()

            walk(act, start, non_local, wavelet, attention, head_norm, tail, passes)

        @block.vector
        def _(dve):
            v = nc.vector

            def start():
                steps = [0]

                def link(ins):
                    steps[0] += 1
                    ins.then_inc(sem("dve_setup"), 1)
                    dve.wait_ge(sem("dve_setup"), steps[0])

                v.memset(ones[:], 1.0).then_inc(sem("ones_f_ready"), 1)
                v.memset(vt3[0][:], 1.0).then_inc(sem("v_ones"), 1)
                v.memset(vt3[1][:], 1.0).then_inc(sem("v_ones"), 1)
                v.memset(raw(kp[:]), 0.0).then_inc(sem("packs_zeroed"), 1)
                v.memset(th[CI:128, :], 0.0).then_inc(sem("rows_set"), 1)
                v.memset(phz[CI:128, :], 0.0).then_inc(sem("rows_set"), 1)
                link(v.memset(ph[CI:128, :], 0.0))
                v.memset(ph[CI:CI + 1, :], 1.0).then_inc(sem("rows_set"), 1)
                dve.wait_ge(sem("weights_in"), 16 * len(loads))
                link(v.tensor_scalar(tmpc[:, 0:1], col("bn_var"), 1e-5, None, ALU.add))
                link(v.tensor_scalar(tmpc[:, 1:2], col("bn1_v"), 1e-5, None, ALU.add))
                v.tensor_scalar(tmpc[:, 2:6], vec[:, V["bn2_v0"]:V["bn2_v0"] + 4], 1e-5, None, ALU.add).then_inc(sem("vars_ready"), 1)
                dve.wait_ge(sem("rsq_ready"), 1)
                link(v.tensor_tensor(cst[:, INV0:INV0 + 1], col("bn_gamma"), tmpc[:, 8:9], ALU.mult))
                link(v.tensor_tensor(tmpc[:, 16:17], col("b_W"), col("bn_mean"), ALU.subtract))
                link(v.scalar_tensor_tensor(cst[:, C0:C0 + 1], tmpc[:, 16:17], cst[:, INV0:INV0 + 1], col("bn_beta"), ALU.mult, ALU.add))
                link(v.tensor_tensor(cst[:, INV1:INV1 + 1], col("bn1_g"), tmpc[:, 9:10], ALU.mult))
                link(v.tensor_tensor(tmpc[:, 17:18], col("fusion_b"), col("bn1_m"), ALU.subtract))
                link(v.scalar_tensor_tensor(cst[:, C1:C1 + 1], tmpc[:, 17:18], cst[:, INV1:INV1 + 1], col("bn1_b"), ALU.mult, ALU.add))
                c4 = lambda n: vec[:, V[n + "0"]:V[n + "0"] + 4]
                link(v.scalar_tensor_tensor(cst[:, INV2:INV2 + 4], c4("bn2_g"), 0.5, tmpc[:, 10:14], ALU.mult, ALU.mult))
                link(v.tensor_tensor(tmpc[:, 20:24], c4("proj_b"), c4("bn2_m"), ALU.subtract))
                link(v.tensor_tensor(tmpc[:, 24:28], tmpc[:, 20:24], cst[:, INV2:INV2 + 4], ALU.mult))
                link(v.scalar_tensor_tensor(cst[:, C2:C2 + 4], c4("bn2_b"), 0.5, tmpc[:, 24:28], ALU.mult, ALU.add))
                link(v.tensor_scalar(cst[:, BQS:BQS + 1], col("bq"), QS, None, ALU.mult))
                dve.wait_ge(sem("wpv_ps"), 1)
                link(v.tensor_tensor(cst[:, B2:B2 + 1], ps[:, 1, 0:1], col("bp"), ALU.add))
                link(v.tensor_scalar(cst[:, TMP:TMP + 1], col("temp"), 1e-4, 10.0, ALU.max, ALU.min))
                link(v.tensor_scalar(wfu, wfu, 0.5, None, ALU.mult))
                link(v.tensor_tensor(wfs[:, 0, :], wfu[:, 0, :], wfu[:, 1, :], ALU.add))
                link(v.tensor_tensor(wfs[:, 1, :], wfu[:, 2, :], wfu[:, 3, :], ALU.add))
                link(v.tensor_tensor(wfs[:, 2, :], wfu[:, 0, :], wfu[:, 1, :], ALU.subtract))
                link(v.tensor_tensor(wfs[:, 3, :], wfu[:, 2, :], wfu[:, 3, :], ALU.subtract))
                link(v.tensor_tensor(wfc[:, 0, :], wfs[:, 0, :], wfs[:, 1, :], ALU.add))
                link(v.tensor_tensor(wfc[:, 1, :], wfs[:, 0, :], wfs[:, 1, :], ALU.subtract))
                link(v.tensor_tensor(wfc[:, 2, :], wfs[:, 2, :], wfs[:, 3, :], ALU.add))
                link(v.tensor_tensor(wfc[:, 3, :], wfs[:, 2, :], wfs[:, 3, :], ALU.subtract))
                dve.wait_ge(sem("windows_in"), 16 * 2 * QW)
                for t in range(4):
                    last = v.tensor_scalar(toep[:, t, :], toep_rev[:, t, ::-1], 1.0 / C if t < 2 else 1.0, None, ALU.mult)
                last.then_inc(sem("consts_ready"), 1)

            def linker(stage, bt, per):
                count = [0]

                def link(ins):
                    count[0] += 1
                    assert count[0] <= per
                    ins.then_inc(sem(stage + "_steps"), 1)
                    wait(dve, sem(stage + "_steps"), bt, per, count[0])
                return link

            def carry_wait():
                v.memset(idle[:, 0:1], 0.0)

            def group_norm(at, bt, src, ready, n, eps, gam, bet, tag):
                link = linker("norm" + tag, bt, 4)
                yield at
                wait(dve, sem(ready), bt, n)
                for h in range(NH):
                    link(v.bn_stats(st[:, h, :], half(src, h)))
                carry_wait()
                v.bn_aggr(mv[:, 0:2], st[:]).then_inc(sem("mv" + tag), 1)
                yield at + 2
                wait(dve, sem("gm_ps" + tag), bt)
                link(v.tensor_tensor(mv[:, 2:3], mv[:, 0:1], ps[:, FB, 0:1], ALU.subtract))
                v.scalar_tensor_tensor(mv[:, 3:4], mv[:, 2:3], mv[:, 2:3], mv[:, 1:2], ALU.mult, ALU.add).then_inc(sem("vd" + tag), 1)
                yield at + 4
                wait(dve, sem("gv_ps" + tag), bt)
                v.tensor_scalar(mv[:, 4:5], ps[:, FB + 1, 0:1], eps, None, ALU.add).then_inc(sem("var" + tag + "_ready"), 1)
                link(v.tensor_tensor(mv[:, 7:8], mv[:, 2:3], mv[:, 0:1], ALU.subtract))
                wait(dve, sem("rstd" + tag + "_ready"), bt)
                v.tensor_tensor(mv[:, 6:7], mv[:, 5:6], col(gam), ALU.mult).then_inc(sem("norm_scale" + tag), 1)
                wait(dve, sem("norm_scale" + tag), bt)
                v.scalar_tensor_tensor(mv[:, 8:9], mv[:, 7:8], mv[:, 6:7], col(bet), ALU.mult, ALU.add).then_inc(sem("norm_shift" + tag), 1)
                wait(dve, sem("norm_shift" + tag), bt)
                v.tensor_scalar(hn[:], src[:], mv[:, 6:7], mv[:, 8:9], ALU.mult, ALU.add).then_inc(sem("h" + tag + "_ready"), 1)

            def split(bt, f, hi, lo, ready, done):
                wait(dve, sem(ready), bt)
                v.tensor_copy(hi[:], f[:]).then_inc(sem(done + "_hi"), 1)
                wait(dve, sem(done + "_hi"), bt)
                v.tensor_tensor(lo[:], f[:], hi[:].bitcast(F32), ALU.subtract).then_inc(sem(done), 1)

            def non_local(bt):
                link = linker("l0", bt, 2)
                yield L0 + 3
                wait(dve, sem("phig_ps"), bt)
                for h in range(NH):
                    src = ps[:, FB + h, :].rearrange("p (y a x b) -> p y x a b", a=2, b=2, x=QW)
                    dst = pg[:, 128 * h:128 * (h + 1)].rearrange("p (y x) -> p y x", x=QW)
                    last = v.tensor_reduce(dst, src, AX.XY, ALU.max)
                link(last)
                bias = vec[:, V["b_phig"]:V["b_phig"] + 1]
                v.tensor_scalar(phz[0:CI, :], pg[0:CI, :], bias[0:CI, :], None, ALU.add).then_inc(sem("phi_ready"), 1)
                v.tensor_scalar(ph[0:CI, :], pg[0:CI, :], bias[0:CI, :], None, ALU.add).then_inc(sem("phi_ready"), 1)
                v.tensor_scalar(gt[CI:128, :], pg[CI:128, :], bias[CI:128, :], None, ALU.add).then_inc(sem("g_ready"), 1)
                for k in range(4):
                    yield L0 + 5 + k // 2
                    wait(dve, sem("s0max_ps"), bt, 4, k + 1)
                    v.tensor_reduce(nm0[:, 2 * k:2 * k + 2], ps[:, FB + k % 2, :].rearrange("p (a b) -> p a b", b=M0), AX.X,
                                    ALU.max, negate=True).then_inc(sem("nm0_ready"), 1)
                yield L0 + 16
                wait(dve, sem("den0_ps"), bt)
                v.reciprocal(inv[:], ps[:, FB, 0:NC]).then_inc(sem("inv0_ready"), 1)
                yield L0 + 18
                wait(dve, sem("inv0_ps"), bt)
                v.tensor_copy(rec[:], two(FB)).then_inc(sem("rec0_ready"), 1)
                yield L0 + 20
                wait(dve, sem("y0_ps"), bt)
                wait(dve, sem("rec0_ready"), bt)
                link(v.scalar_tensor_tensor(rec[:], two(FB), cst[:, INV0:INV0 + 1], rec[:], ALU.mult, ALU.mult))
                wait(dve, sem("out_done"), bt + -3, 16)
                v.scalar_tensor_tensor(x1[:], rec[:], cst[:, C0:C0 + 1], xin[:], ALU.add, ALU.add).then_inc(sem("x1_ready"), 1)

            def wavelet(bt):
                link = linker("l1", bt, 7)
                yield L1 + 3
                wait(dve, sem("fT_ps"), bt)
                fT = ps[:, FB + 1, 0:2 * 128].rearrange("p (a b) -> p a b", b=128)
                v.tensor_reduce(spT[:, 0, :], fT, AX.X, ALU.add).then_inc(sem("sp_ready"), 1)
                v.tensor_reduce(spT[:, 1, :], fT, AX.X, ALU.max).then_inc(sem("sp_ready"), 1)
                yield L1 + 6
                wait(dve, sem("sg_exp"), bt)
                link(v.tensor_scalar(sg[:, 1, :], sg[:, 0, :], 1.0, None, ALU.add))
                link(v.reciprocal(sg[:, 2, :], sg[:, 1, :]))
                link(v.scalar_tensor_tensor(spat[:], sg[:, 2, :], 1.0 / Q, fused[:], ALU.mult, ALU.mult, accum_out=pool[:, 0:1]))
                link(v.tensor_reduce(chm[:, 3:4], spat[:], AX.X, ALU.max))
                v.tensor_scalar(pool[:, 1:2], chm[:, 3:4], float(Q), None, ALU.mult).then_inc(sem("pool_ready"), 1)
                yield L1 + 11
                wait(dve, sem("chm_exp"), bt)
                link(v.tensor_scalar(chm[:, 1:2], chm[:, 0:1], 1.0, None, ALU.add))
                link(v.reciprocal(chm[:, 2:3], chm[:, 1:2]))
                v.tensor_scalar(chout[:], spat[:], chm[:, 2:3], float(Q), ALU.mult, ALU.mult).then_inc(sem("chout_ready"), 1)
                yield L1 + 14
                wait(dve, sem("pj_ready"), bt, 4)
                even, odd = pj[:, 0::2, :], pj[:, 1::2, :]
                v.tensor_tensor(sd[:, 0, :, :], even, odd, ALU.add)
                link(v.tensor_tensor(sd[:, 1, :, :], even, odd, ALU.subtract))
                x1v = x1[:].rearrange("p (y r x c) -> p y r x c", r=2, c=2, x=QW)
                uxv = ux[:].rearrange("p (y r x c) -> p y r x c", r=2, c=2, x=QW)
                x2v = x2[:].rearrange("p (y r x c) -> p y r x c", r=2, c=2, x=QW)
                for r in range(2):
                    for c in range(2):
                        s = sd[:, r, 0, :].rearrange("p (y x) -> p y x", x=QW)
                        v.tensor_tensor(uxv[:, :, r, :, c], x1v[:, :, r, :, c], s, ALU.add).then_inc(sem("ux_ready"), 1)
                wait(dve, sem("ux_ready"), bt, 4)
                for r in range(2):
                    for c in range(2):
                        s = sd[:, r, 1, :].rearrange("p (y x) -> p y x", x=QW)
                        v.tensor_tensor(x2v[:, :, r, :, c], uxv[:, :, r, :, c], s,
                                        ALU.subtract if c else ALU.add).then_inc(sem("x2_ready"), 1)
                yield from group_norm(L2, bt, x2, "x2_ready", 4, 1e-6, "gamma", "beta", "2")
                yield L2 + GN + 2
                split(bt, qf, qh, ql, "q2_ready", "q2_split")
                yield L2 + GN + 4
                split(bt, kf, kh, kl, "k2_ready", "k2_split")
                for u in range(NC * NH):
                    yield L2 + GN + 5 + u // 2
                    wait(dve, sem("s2max_ps"), bt, NC * NH, u + 1)
                    v.tensor_reduce(mx[:, u // NH, u % NH:u % NH + 1], ps[:, FB + u % 2, :], AX.X, ALU.max).then_inc(sem("mx2_ready"), 1)
                wait(dve, sem("mx2_ready"), bt, NC * NH)
                v.tensor_reduce(nm2[:], mx[:], AX.X, ALU.max, negate=True).then_inc(sem("nm2_ready"), 1)

            def attention(bt):
                link = linker("l2", bt, NH)
                yield A2[0]
                if not bt.is_number(0):
                    wait(dve, sem("x3_ready"), bt + -1, NH)
                    v.tensor_copy(x3s[:], x3[:]).then_inc(sem("x3_kept"), 1)
                for h in range(NH):
                    yield A2[h] + 15
                    wait(dve, sem("den2_ps"), bt, NH, h + 1)
                    v.reciprocal(inv[:, 0:NC // 2], ps[:, FB + 1, 0:NC // 2]).then_inc(sem("inv2_ready"), 1)
                    yield A2[h] + 17
                    wait(dve, sem("inv2_ps"), bt, NH, h + 1)
                    link(v.tensor_tensor(half(rec, h), half(ysb, h), ps[:, FB + 1, :], ALU.mult))
                    v.scalar_tensor_tensor(half(x3, h), half(rec, h), cst[:, B2:B2 + 1], half(x2, h), ALU.add, ALU.add).then_inc(sem("x3_ready"), 1)
                yield from group_norm(A3, bt, x3, "x3_ready", NH, 1e-5, "g1", "beta1", "3")
                yield A3 + GN + 2
                split(bt, qf, q3h, q3l, "q3_ready", "q3_split")
                yield A3 + GN + 4
                split(bt, kf, k3h, k3l, "k3_ready", "k3_split")

            def head_norm(bt, g, at):
                yield at + 1
                wait(dve, sem("den3_ps"), bt, NG, g + 1)
                v.reciprocal(inv3[:].rearrange("p c i -> p (c i)"), ps[:, FB, 0:NC * GH]).then_inc(sem("inv3_ready"), 1)
                wait(dve, sem("inv3_ready"), bt, NG, g + 1)
                v.tensor_copy(inv3w, inv3[:].unsqueeze(3).to_broadcast([128, NC, GH, 32])).then_inc(sem("inv3w_ready"), 1)
                yield at + 3
                wait(dve, sem("inv3_ps"), bt, NG, g + 1)
                v.tensor_tensor(og[:, g, :], og[:, g, :], two(FB), ALU.mult).then_inc(sem("yn_ready"), 1)

            def tail(bt):
                yield TL + 5
                wait(dve, sem("o3_ps"), bt)
                if bt.is_number(B - 1):
                    keep = x3
                    wait(dve, sem("x3_ready"), bt, NH)
                else:
                    keep = x3s
                    wait(dve, sem("x3_kept"), bt)
                v.scalar_tensor_tensor(x4[:], two(FB), col("b_out"), keep[:], ALU.add, ALU.add).then_inc(sem("x4_ready"), 1)
                yield from group_norm(TL + 5, bt, x4, "x4_ready", 1, 1e-5, "g2", "beta2", "4")
                yield TL + GN + 10
                wait(dve, sem("m4_ps"), bt)
                wait(dve, sem("out_done"), bt + -1, 16)
                v.scalar_tensor_tensor(xo[:], two(FB), col("b_mlp2"), x4[:], ALU.add, ALU.add).then_inc(sem("xo_ready"), 1)

            def passes(bt, side, heads, more):
                for g, (mb, mg, maxima) in enumerate(((bt, 1, heads), (bt + 1, 0, more))):
                    for p in range(LAPS):
                        for n in maxima_at(p) if maxima else ():
                            u = mg * TILES + n
                            wait(dve, sem("s3max_ps"), mb, NG * TILES, u + 1)
                            i, c, h = n // (NC * NH), n // NH % NC, n % NH
                            v.tensor_reduce(mx3[:, i, c, h:h + 1], ps[:, MB + n % 2, :], AX.X, ALU.max).then_inc(sem("mx3_ready"), 1)
                        if maxima and p == M_FIRST + M_LAPS:
                            wait(dve, sem("mx3_ready"), mb, NG * TILES, (mg + 1) * TILES)
                            v.tensor_reduce(nm3[:], mx3[:].rearrange("p i c h -> p (i c) h"), AX.X, ALU.max,
                                            negate=True).then_inc(sem("nm3_ready"), 1)
                        side.upto(LAPS * g + p)
                side.finish()

            walk(dve, start, non_local, wavelet, attention, head_norm, tail, passes)

        @block.tensor
        def _(pe):
            def mm(o, l, r, start=True, stop=True):
                return nc.tensor.matmul(o, l, r, start=start, stop=stop)

            def start():
                pe.wait_ge(sem("weights_in"), 16 * len(loads))
                mm(ps[:, 0, 0:128], wv_s, wp_s)
                mm(ps[:, 1, 0:1], wp_s, col("bv")).then_inc(sem("wpv_ps"), 1)
                pe.wait_ge(sem("ident_ready"), 1)
                pe.wait_ge(sem("grp_steps"), 6)
                pe.wait_ge(sem("ones_f_ready"), 1)
                pe.wait_ge(sem("ones_ready"), 1)
                pe.wait_ge(sem("wpv_ready"), 1)
                pe.wait_ge(sem("consts_ready"), 1)
                pe.wait_ge(sem("rows_set"), 3)
                pe.wait_ge(sem("den_row_steps"), 2)
                pe.wait_ge(sem("v_ones"), 2)
                pe.wait_ge(sem("wo_in"), 16 * HEADS)
                pe.wait_ge(sem("k_ones_in"), 16 * HEADS)
                pe.wait_ge(sem("packs_zeroed"), 2)

            def project(w, x, o=FB, rows=slice(0, 128)):
                for h in range(NH):
                    last = mm(ps[rows, o + h, :], w, half(x, h))
                return last

            def project_T(w, x, o=FB):
                for c in range(NC):
                    last = mm(bank_part(o, c), part(x, c), w)
                return last

            def group_averages(at, bt, t, tag):
                yield at + 1
                wait(pe, sem("mv" + tag), bt)
                mm(ps[:, FB, 0:1], t[:], mv[:, 0:1]).then_inc(sem("gm_ps" + tag), 1)
                yield at + 3
                wait(pe, sem("vd" + tag), bt)
                mm(ps[:, FB + 1, 0:1], t[:], mv[:, 3:4]).then_inc(sem("gv_ps" + tag), 1)

            def non_local(bt):
                yield L0
                wait(pe, sem("v3_ready"), bt + -1)
                wait(pe, sem("x_in"), bt, 16)
                project(wth[:], xin, rows=slice(0, CI)).then_inc(sem("theta_ps"), 1)
                yield L0 + 2
                wait(pe, sem("theta_ready"), bt)
                project(wpg[:], xin).then_inc(sem("phig_ps"), 1)
                for k in range(4):
                    yield L0 + 4 + k // 2
                    wait(pe, sem("phi_ready"), bt, 2)
                    if k >= 2:
                        wait(pe, sem("nm0_ready"), bt, 4, k - 1)
                    for c in (2 * k, 2 * k + 1):
                        last = mm(ps[:, FB + k % 2, M0 * (c % 2):M0 * (c % 2 + 1)], part(th, c), phz[:])
                    last.then_inc(sem("s0max_ps"), 1)
                yield L0 + 7
                wait(pe, sem("g_ready"), bt)
                wait(pe, sem("nm0_ready"), bt, 4)
                nc.tensor.transpose(ps[0:NC, FB + 1, 0:128], nm0[:], ident[:]).then_inc(sem("nm0T_ps"), 1)
                for m in range(2):
                    last = mm(ps[:, FB, 128 * m:128 * (m + 1)], part(gt[CI:128, :], m), wWT[CI:128, :])
                last.then_inc(sem("wg_ps"), 1)
                for m in range(2):
                    yield L0 + 11 + 2 * m
                    if m == 0:
                        wait(pe, sem("nm0_row_in"), bt, 16)
                        wait(pe, sem("wg_ready"), bt)
                    else:
                        wait(pe, sem("p0_ready"), bt, 2, m)
                    project(part(ph, m), th).then_inc(sem("s0_ps"), 1)
                yield L0 + 15
                wait(pe, sem("p0_ready"), bt, 2)
                for c in range(NC):
                    for m in range(2):
                        last = mm(ps[:, FB, c:c + 1], part(p0[:, m, :], c), ones[:, 0:1], start=m == 0, stop=m == 1)
                last.then_inc(sem("den0_ps"), 1)
                yield L0 + 17
                wait(pe, sem("inv0_ready"), bt)
                for c in range(NC):
                    last = mm(bank_part(FB, c), inv[:, c:c + 1].to_broadcast([128, 128]), ident[:])
                last.then_inc(sem("inv0_ps"), 1)
                yield L0 + 19
                wait(pe, sem("rec0_ready"), bt)
                for m in range(2):
                    for h in range(NH):
                        last = mm(ps[:, FB + h, :], wg[:, m, :], half(p0[:, m, :], h), start=m == 0, stop=m == 1)
                last.then_inc(sem("y0_ps"), 1)

            def wavelet(bt):
                yield L1
                wait(pe, sem("x1_ready"), bt)
                wait(pe, sem("yn_ready"), bt + -2, NG, 1)
                x1v = x1[:].rearrange("p (y r x c) -> p y r x c", r=2, c=2, x=QW)
                for k in range(4):
                    last = mm(ps[:, FB, 0:Q].rearrange("p (y x) -> p y x", x=QW), wfc[:, k, :], x1v[:, :, k // 2, :, k % 2],
                              start=k == 0, stop=k == 3)
                last.then_inc(sem("fus_ps"), 1)
                yield L1 + 2
                wait(pe, sem("fused_ready"), bt)
                for k in range(2):
                    last = nc.tensor.transpose(ps[:, FB + 1, 128 * k:128 * (k + 1)], part(fused, k), ident[:])
                last.then_inc(sem("fT_ps"), 1)
                yield L1 + 4
                wait(pe, sem("sp_ready"), bt, 2)
                for k in range(4):
                    last = mm(ps[:, FB, 0:Q], spT[:, k // 2, k % 2:k % 2 + 1].to_broadcast([128, 128]), toep[:, k, :],
                              start=k == 0, stop=k == 3)
                last.then_inc(sem("conv_ps"), 1)
                yield L1 + 7
                wait(pe, sem("pool_ready"), bt)
                mm(ps[0:HID, FB + 1, 0:2], wca1[:], pool[:]).then_inc(sem("mlp1_ps"), 1)
                yield L1 + 9
                wait(pe, sem("hid_ready"), bt)
                mm(ps[:, FB, 0:1], wca2[:], hsum[:]).then_inc(sem("mlp2_ps"), 1)
                yield L1 + 12
                wait(pe, sem("chout_ready"), bt)
                for k in range(4):
                    last = mm(ps[:, FB + k // 2, Q * (k % 2):Q * (k % 2 + 1)], part(wpr, k), chout[:])
                    if k % 2:
                        last.then_inc(sem("proj_ps"), 1)
                yield from group_averages(L2, bt, grp8, "2")
                yield L2 + GN
                wait(pe, sem("h2_ready"), bt)
                project(wq_s[:], hn).then_inc(sem("q2_ps"), 1)
                yield L2 + GN + 2
                wait(pe, sem("q2_ready"), bt)
                project(wk_s[:], hn).then_inc(sem("k2_ps"), 1)
                yield L2 + GN + 4
                wait(pe, sem("k2_ready"), bt)
                project_T(wpv[:], hn).then_inc(sem("v2_ps"), 1)
                for u in range(NC * NH):
                    yield L2 + GN + 5 + u // 2
                    if u == 0:
                        wait(pe, sem("v2_ready"), bt)
                        wait(pe, sem("k2_split_hi"), bt)
                    if u >= 2:
                        wait(pe, sem("mx2_ready"), bt, NC * NH, u - 1)
                    mm(ps[:, FB + u % 2, :], part(qh, u // NH), half(kh, u % NH)).then_inc(sem("s2max_ps"), 1)
                yield L2 + GN + 13
                wait(pe, sem("nm2_ready"), bt)
                nc.tensor.transpose(ps[0:NC, FB, 0:128], nm2[:], ident[:]).then_inc(sem("nm2T_ps"), 1)

            def attention(bt):
                def scores(h, j):
                    u = NC * h + j
                    if u:
                        wait(pe, sem("p2_ready"), bt, NC * NH, u)
                    o = ps[:, FB, :]
                    mm(o, part(kh, j), half(qh, h), stop=False)
                    mm(o, part(kh, j), half(ql, h), start=False, stop=False)
                    mm(o, part(kl, j), half(qh, h), start=False, stop=False)
                    mm(o, ones_r[0:1, :], half(nmrow, h), start=False).then_inc(sem("s2_ps"), 1)

                def values(h, j):
                    u = NC * h + j
                    wait(pe, sem("p2_ready"), bt, NC * NH, u + 1)
                    mm(ps[:, FB + 1, :], vT[:, j, :], p2[:, u % 4, :], start=j == 0, stop=j == NC - 1).then_inc(sem("pv2_done"), 1)

                yield A2[0]
                wait(pe, sem("xo_ready"), bt + -2)
                wait(pe, sem("k2_split"), bt)
                wait(pe, sem("nm2_row_in"), bt, 16)
                for h in range(NH):
                    for j in range(NC):
                        yield key_at(h, j)
                        scores(h, j)
                        if j == 1 and h:
                            wait(pe, sem("x3_ready"), bt, NH, h)
                        if j:
                            values(h, j - 1)
                    yield A2[h] + 12
                    values(h, NC - 1)
                    yield A2[h] + 14
                    wait(pe, sem("y2_ready"), bt, NH, h + 1)
                    wait(pe, sem("acc_steps"), bt, (NC - 1) * NH, (NC - 1) * (h + 1))
                    for c in range(NC // 2):
                        last = mm(ps[:, FB + 1, c:c + 1], part(acc[:, h, :], c), ones[:, 0:1])
                    last.then_inc(sem("den2_ps"), 1)
                    yield A2[h] + 16
                    wait(pe, sem("inv2_ready"), bt, NH, h + 1)
                    for c in range(NC // 2):
                        last = mm(ps[:, FB + 1, 128 * c:128 * (c + 1)], inv[:, c:c + 1].to_broadcast([128, 128]), ident[:])
                    last.then_inc(sem("inv2_ps"), 1)
                yield from group_averages(A3, bt, grp4, "3")
                yield A3 + GN
                wait(pe, sem("h3_ready"), bt)
                project(wqkv[:, 0:128], hn).then_inc(sem("q3_ps"), 1)
                yield A3 + GN + 2
                wait(pe, sem("q3_ready"), bt)
                project(wqkv[:, 128:256], hn).then_inc(sem("k3_ps"), 1)
                yield A3 + GN + 4
                wait(pe, sem("k3_ready"), bt)
                project_T(wqkv[:, 256:384], hn).then_inc(sem("v3_ps"), 1)

            def head_norm(bt, g, at):
                yield at
                wait(pe, sem("og_ready"), bt, NG, g + 1)
                if g == 0:
                    wait(pe, sem("xo_ready"), bt + -1)
                    wait(pe, sem("v3_ready"), bt + 1)
                    wait(pe, sem("x1_ready"), bt + 2)
                else:
                    wait(pe, sem("yn_ready"), bt, NG, 1)
                    wait(pe, sem("nm2T_ready"), bt + 2)
                    wait(pe, sem("xo_ready"), bt + -1)
                for c in range(NC):
                    last = mm(ps[:, FB, GH * c:GH * (c + 1)], part(og[:, g, :], c), den_row[:])
                last.then_inc(sem("den3_ps"), 1)
                yield at + 2
                wait(pe, sem("inv3w_ready"), bt, NG, g + 1)
                for c in range(NC):
                    last = mm(bank_part(FB, c), inv3w[:, c, :, :].rearrange("p i r -> p (i r)"), ident[:])
                last.then_inc(sem("inv3_ps"), 1)

            def tail(bt):
                yield TL + 4
                wait(pe, sem("yn_ready"), bt, NG)
                for g in range(NG):
                    for h in range(NH):
                        last = mm(ps[:, FB + h, :], wo[:, g, :], half(og[:, g, :], h), start=g == 0, stop=g == NG - 1)
                last.then_inc(sem("o3_ps"), 1)
                yield from group_averages(TL + 5, bt, grp4, "4")
                yield TL + GN + 7
                wait(pe, sem("h4_ready"), bt)
                project(wm1[:], hn, rows=slice(0, MLP)).then_inc(sem("h4_ps"), 1)
                yield TL + GN + 9
                wait(pe, sem("gelu_ready"), bt)
                project(wm2[:], gl).then_inc(sem("m4_ps"), 1)

            def passes(bt, side, heads, more):
                for g, (mb, mg, maxima) in enumerate(((bt, 1, heads), (bt + 1, 0, more))):
                    if heads:
                        wait(pe, sem("nm3_row_in"), bt, 16 * HEADS, 16 * GH * (g + 1))
                    for p in range(LAPS):
                        s, i = divmod(p, GH)
                        j, h = divmod(s, NH)
                        if heads and s < STEPS:
                            hd, u = GH * g + i, g * TILES + p
                            wait(pe, sem("p3_ready"), bt, NG * TILES, u - 1)
                            mm(ps[:, SB + p % 2, :], part(kp[:, hd, :], j), half(qp[:, hd // 2, :], h)).then_inc(sem("s3_ps"), 1)
                        for n in maxima_at(p) if maxima else ():
                            hd, c, hh = GH * mg + n // (NC * NH), n // NH % NC, n % NH
                            u = mg * TILES + n
                            if n % (2 * NC * NH) == 0:
                                wait(pe, sem(f"packed{hd % GH // 2}"), mb, 16 * 12 * NG, 16 * 12 * (mg + 1))
                            if n == 0:
                                wait(pe, sem("nm3T_ready"), mb, NG, mg)
                            wait(pe, sem("mx3_ready"), mb, NG * TILES, u - 1)
                            mm(ps[:, MB + n % 2, :], part(qp[0:ROWS, hd // 2, :], c), half(kp[0:ROWS, hd, :], hh)).then_inc(sem("s3max_ps"), 1)
                        if heads and i == GH - 1 and s:
                            j, h = divmod(s - 1, NH)
                            if j == 0 and h == 0:
                                wait(pe, sem("og_ready"), bt, NG, g)
                                wait(pe, sem("vt3_ready"), bt, NG, g + 1)
                            wait(pe, sem("p3_ready"), bt, NG * TILES, g * TILES + GH * s)
                            for q in range(GH):
                                last = mm(ps[32 * q:32 * (q + 1), VB + h, :], vt3[g][:, j, q, :], p3[:, (s - 1) % 2, q, :],
                                          start=j == 0, stop=j == NC - 1)
                            last.then_inc(sem("pv3_done"), 1)
                        if maxima and p == M_FIRST + M_LAPS:
                            wait(pe, sem("nm3_ready"), mb, NG, mg + 1)
                            nc.tensor.transpose(ps[0:GH * NC, MB, 0:128], nm3[:], ident[:]).then_inc(sem("nm3T_ps"), 1)
                        side.upto(LAPS * g + p)
                side.finish()

            walk(pe, start, non_local, wavelet, attention, head_norm, tail, passes)


def kernel(**inputs):
    import concourse.bacc as bacc
    from concourse.bass_utils import run_bass_kernel_spmd

    i = {k.replace("_conv_", "_"): np.asarray(v) for k, v in inputs.items()}

    def t(a):
        return np.ascontiguousarray(a.T)

    cols = {k: i["L0_" + k] for k in ("b_W", "bn_gamma", "bn_beta", "bn_mean", "bn_var")}
    cols |= {k: i["L1_" + k] for k in ("fusion_b", "bn1_g", "bn1_b", "bn1_m", "bn1_v")}
    for k in ("proj_b", "bn2_g", "bn2_b", "bn2_m", "bn2_v"):
        for n in range(4):
            cols[f"{k}{n}"] = i["L1_" + k][C * n:C * (n + 1)]
    cols |= {k: i["L2_" + k] for k in ("gamma", "beta", "bq", "bk", "bv", "bp")}
    cols |= {k: i["L3_" + k] for k in ("b_out", "g1", "beta1", "g2", "beta2", "b_mlp2")}
    cols["temp"] = np.repeat(i["L3_temperature"].reshape(HEADS), HD)
    cols["b_phig"] = np.concatenate([i["L0_b_phi"], i["L0_b_g"]])
    arrays = {
        "x": np.ascontiguousarray(i["x"]),
        "vecs": np.ascontiguousarray(np.stack([cols[k] for k in VECS], axis=1)),
        "w_theta": t(i["L0_w_theta"]),
        "b_theta": np.ascontiguousarray(i["L0_b_theta"].reshape(CI, 1)),
        "w_phig": t(np.concatenate([i["L0_w_phi"], i["L0_w_g"]])),
        "w_W": t(i["L0_w_W"]),
        "w_fuse": np.ascontiguousarray(i["L1_fusion_w"].reshape(C, 4, C).transpose(2, 1, 0).reshape(C, 4 * C)),
        "sa_w": np.ascontiguousarray(i["L1_sa_w"].reshape(2, TAPS, TAPS)),
        "ca_w1": t(i["L1_ca_w1"]),
        "ca_w2": t(i["L1_ca_w2"]),
        "w_proj": t(i["L1_proj_w"]),
        "wq": t(i["L2_wq"]),
        "wk": t(i["L2_wk"]),
        "wv": np.ascontiguousarray(i["L2_wv"]),
        "wp": t(i["L2_wp"]),
        "w_qkv": t(i["L3_w_qkv"]),
        "w_out": t(i["L3_w_out"]),
        "w_mlp1": t(i["L3_w_mlp1"]),
        "b_mlp1": np.ascontiguousarray(i["L3_b_mlp1"].reshape(MLP, 1)),
        "w_mlp2": t(i["L3_w_mlp2"]),
    }
    nc = bacc.Bacc("TRN2", target_bir_lowering=False, num_devices=1)
    aps = [nc.dram_tensor(f"in_{k}", a.shape, mybir.dt.from_np(a.dtype), kind="ExternalInput").ap() for k, a in arrays.items()]
    out = nc.dram_tensor("out", (B, C, H, W), F32, kind="ExternalOutput").ap()
    nc.disable_value_cache = True
    build(nc, *aps, out)
    r = run_bass_kernel_spmd(nc, [{f"in_{k}": a for k, a in arrays.items()}], core_ids=[0])
    return r.results[0]["out"]
```

```python
import numpy as np

import concourse.bass as bass
from concourse import mybir
from concourse.alu_op_type import AluOpType as ALU
from contextlib import ExitStack

F32 = mybir.dt.float32
F32R = mybir.dt.float32r
ACT = mybir.ActivationFunctionType
AX = mybir.AxisListType

B, C, H, W = 8, 128, 32, 32
N = H * W
HALF = 512
NH = N // HALF
NC = N // 128
CI = 64
M0 = N // 4
Q = N // 4
QW = W // 2
HID = 8
TAPS, PADW = 7, 2 * QW - 1
HEADS, HD = 8, 16
GH = 4
NG = HEADS // GH
MLP = 32
PACK = 3 * HD
ROWS = 64 + PACK
TILES = GH * NC * NH
STEPS = NC * NH
LAPS = GH * (STEPS + 1)
M_END = 61
A2 = (1, 25)
A2_QUARTERS = 9
A2_END = (-2, 0, 1, 2)
A3 = 51
HN = 69
L1, L1_SIXTHS = 76, 9
L2 = 102
TL, TL_SIXTHS = 4, 7
L0, L0_SIXTHS = 36, 16
X3_KEPT = 16
GN_AT, GN = (3, 3, 4, 5), 8
PR_AT = (0, 1, 2, 3, 4, 5)
MAXIMA_TILES = ("00000020220320222011110001212211121100011212222220231001011110000000",
                "00000002200222202200110212131120220112022031020220311200002020000000")

VECS = ["b_W", "bn_gamma", "bn_beta", "bn_mean", "bn_var", "fusion_b", "bn1_g", "bn1_b", "bn1_m", "bn1_v",
        "proj_b0", "proj_b1", "proj_b2", "proj_b3", "bn2_g0", "bn2_g1", "bn2_g2", "bn2_g3",
        "bn2_b0", "bn2_b1", "bn2_b2", "bn2_b3", "bn2_m0", "bn2_m1", "bn2_m2", "bn2_m3",
        "bn2_v0", "bn2_v1", "bn2_v2", "bn2_v3", "gamma", "beta", "bq", "bk", "bv", "bp",
        "temp", "b_out", "g1", "beta1", "g2", "beta2", "b_mlp2", "b_phig"]
V = {name: i for i, name in enumerate(VECS)}


def key_at(h, j):
    return A2[h] + A2_QUARTERS * j // 4


def maxima2_at(u):
    return L2 + GN + PR_AT[5] + u


def non_local_at(k):
    return L0 + L0_SIXTHS * k // 6


def tail_at(k):
    return TL + TL_SIXTHS * k // 6


def late_at(k):
    return non_local_at((20, 40)[k])


def wavelet_at(k):
    return L1 + L1_SIXTHS * k // 6


class Batch:

    def __init__(self, b, off=0):
        self.b, self.off = (b + off, 0) if isinstance(b, int) else (b, off)

    def __add__(self, n):
        return Batch(self.b, self.off + n)

    def is_first(self):
        return isinstance(self.b, int) and self.b == -3

    def exists(self):
        return not isinstance(self.b, int) or 0 <= self.b < B

    def count(self, per, k, b=None):
        return (self.b if b is None else b) * per + (self.off * per + k)


def wait(eng, sem, batch, per=1, k=None):
    k = per if k is None else k
    value = batch.count(per, k)
    if isinstance(value, int):
        value = min(value, B * per)
        if value <= 0:
            return
    else:
        assert batch.count(per, k, 1) > 0
    eng.wait_ge(sem, value)


class Side:

    def __init__(self, *parts):
        self.parts = (at for part in parts for at in part)
        self.at = next(self.parts, None)

    def upto(self, p):
        while self.at is not None and self.at <= p:
            self.at = next(self.parts, None)

    def finish(self):
        self.upto(4 * LAPS)


def maxima_at(g, p):
    tiles = [int(n) for n in MAXIMA_TILES[g]]
    first = sum(tiles[:p])
    tiles = range(first, first + tiles[p])
    return tiles[:1], tiles[1:]


def walk(eng, start, late_start, non_local, wavelet, queries, attention, head_norm, tail, passes):

    def window(bt):
        x, y = [late_start()] if bt.is_first() else [], []
        if (bt + 1).exists():
            x.append(attention(bt + 1))
        if bt.exists():
            x.append(head_norm(bt, 0, HN))
        if (bt + 2).exists():
            x += [wavelet(bt + 2), queries(bt + 2)]
        if (bt + -1).exists():
            y += [head_norm(bt + -1, 1, TL), tail(bt + -1)]
        if (bt + 3).exists():
            y.append(non_local(bt + 3))
        passes(bt, (Side(*x), Side(*y)))

    start()
    for b in range(-3, 1):
        window(Batch(b))
    with eng.Fori(1, B - 3) as b:
        window(Batch(b))
    for b in range(B - 3, B + 1):
        window(Batch(b))


def build(nc, x, vecs, w_theta, b_theta, w_phig, w_W, w_fuse, sa_w, ca_w1, ca_w2, w_proj,
          wq, wk, wv, wp, w_qkv, w_out, w_mlp1, b_mlp1, w_mlp2, out):
    pad_dram = nc.dram_tensor("padded_taps", [2, PADW, PADW], F32, kind="Internal").ap()
    xd = x.rearrange("b c h w -> b c (h w)")
    od = out.rearrange("b c h w -> b c (h w)")

    with ExitStack() as ctx:
        def sb(name, shape, dt=F32):
            return ctx.enter_context(nc.sbuf_tensor(name, shape, dt))

        def raw(ap):
            return ap.bitcast(F32)

        sems = {}

        def sem(name):
            if name not in sems:
                sems[name] = ctx.enter_context(nc.semaphore(name))
            return sems[name]

        ident = sb("ident", [128, 128])
        ones = sb("ones", [128, 128])
        ones_r = sb("ones_r", [128, 128], F32R)
        grp8 = sb("grp8", [128, 128])
        grp4 = sb("grp4", [128, 128])
        neg_half = sb("neg_half", [128, 16])
        vec = sb("vec", [128, len(VECS)])
        wth = sb("wth", [128, CI])
        bth = sb("bth", [CI, 1])
        wpg = sb("wpg", [128, 128])
        wWT = sb("wWT", [128, 128])
        wfc = sb("wfc", [128, 4, 128])
        wca1 = sb("wca1", [128, HID])
        wca2 = sb("wca2", [HID, 128])
        wpr = sb("wpr", [128, 4 * 128])
        wq_s = sb("wq_s", [128, 128])
        wk_s = sb("wk_s", [128, 128])
        wpv = sb("wpv", [128, 128])
        wqkv = sb("wqkv", [128, 3 * 128])
        wo = sb("wo", [128, NG, 128])
        wm1 = sb("wm1", [128, MLP])
        bm1 = sb("bm1", [NH * MLP, 1])
        wm2 = sb("wm2", [NH * MLP, 128])
        toep = sb("toep", [128, 4, Q])
        idle = sb("idle", [128, 4])
        cst = sb("cst", [128, 32])
        tmpc = sb("tmpc", [128, 64])

        xin = sb("xin", [128, N])
        th = sb("th", [128, N])
        ph = sb("ph", [128, M0])
        phz = sb("phz", [128, M0])
        pg = sb("pg", [128, M0])
        gt = sb("gt", [128, M0])
        wg = sb("wg", [128, 2, 128])
        nm0 = sb("nm0", [128, NC])
        nm0T = sb("nm0T", [NC, 128])
        inv0 = sb("inv0", [128, NC])
        p0 = sb("p0", [128, 2, N])
        x1 = sb("x1", [128, N])
        fused = sb("fused", [128, Q])
        spT = sb("spT", [128, 2, 2])
        sg = sb("sg", [128, Q])
        spat = sb("spat", [128, Q])
        pool = sb("pool", [128, 2])
        hid = sb("hid", [HID, 2])
        hsum = sb("hsum", [HID, 1])
        chm = sb("chm", [128, 4])
        chout = sb("chout", [128, Q])
        pj = sb("pj", [128, 4, Q])
        x2 = sb("x2", [128, N])
        mv = sb("mv", [128, 32])
        mv4 = sb("mv4", [128, 32])
        hn = sb("hn", [128, N])
        sd = hn[:].rearrange("p (a b q) -> p a b q", a=2, b=2)
        qh = sb("qh", [128, N], F32R)
        ql = sb("ql", [128, N], F32R)
        kh = sb("kh", [128, N], F32R)
        kl = sb("kl", [128, N], F32R)
        vT = sb("vT", [128, NC, 128])
        mx = sb("mx", [128, NC, NH])
        nm2 = sb("nm2", [128, NC])
        nm2T = sb("nm2T", [NC, 128], F32R)
        nmrow = sb("nmrow", [1, N], F32R)
        p2 = sb("p2", [128, 4, HALF])
        acc = sb("acc", [128, NH, HALF])
        ysb = sb("ysb", [128, HALF])
        inv2 = sb("inv2", [128, NC // 2])
        x3 = sb("x3", [128, N])
        x3s = sb("x3s", [128, N])
        q3h = sb("q3h", [128, N], F32R)
        q3l = sb("q3l", [128, N], F32R)
        k3h = sb("k3h", [128, N], F32R)
        k3l = sb("k3l", [128, N], F32R)
        qp = sb("qp", [128, HEADS // 2, N], F32R)
        kp = sb("kp", [128, HEADS, N], F32R)
        v3 = sb("v3", [128, NC, HEADS, HD])
        vt3 = [sb(f"vt3_{g}", [128, NC, GH, 32]) for g in range(NG)]
        mx3 = sb("mx3", [128, GH, NC, NH])
        nm3 = sb("nm3", [128, GH * NC])
        nm3T = sb("nm3T", [GH * NC, 128], F32R)
        p3 = sb("p3", [128, 2, GH, HALF])
        og = sb("og", [128, NG, N])
        inv3 = sb("inv3", [128, NC, GH])
        heads_inverse = [t.rearrange("p (c i r) -> p c i r", i=GH, r=32) for t in (acc[:].rearrange("p a b -> p (a b)"), p0[:, 0, :])]
        den_row = sb("den_row", [128, GH])
        x4, hn4 = p0[:, 0, :], p0[:, 1, :]
        gl = pj[0:NH * MLP, 0:2, :].rearrange("p a b -> p (a b)")
        xo = hn4
        toep_rev = p3[:, 0, 0:2, :].rearrange("p a (b q) -> p (a b) q", q=Q)
        pad_sb = p3[0:2, 1, 0:2, :].rearrange("p a b -> p (a b)")[:, 0:PADW * PADW]
        wfu = p3[:, 1, 2, :].rearrange("p (k o) -> p k o", k=4)
        wv_s, wp_s = p3[:, 1, 3, 0:128], p3[:, 1, 3, 128:256]
        wfs = pj[:, :, 0:128]

        ps = ctx.enter_context(nc.psum_tensor("ps", [128, 8, HALF], F32))
        MB, SB, VB, XB, YB = 0, 2, 4, 5, 7
        HEAD_BANKS = [(XB, XB + 1), (YB, YB)]

        def two(k):
            return ps[:, k:k + 2, :].rearrange("p a b -> p (a b)")

        def col(name, rows=128):
            return vec[0:rows, V[name]:V[name] + 1]

        def half(t, h):
            return t[:, HALF * h:HALF * (h + 1)]

        def part(t, c):
            return t[:, 128 * c:128 * (c + 1)]

        def bank_part(k, c):
            return ps[:, k + c // 4, 128 * (c % 4):128 * (c % 4 + 1)]

        INV0, C0, INV1, C1, INV2, C2, BQS, B2, BO, TMP = 0, 1, 2, 3, 4, 8, 12, 13, 14, 15
        QS = float(C) ** -0.5

        first_loads = [(vec[:], vecs), (wth[:], w_theta), (bth[:], b_theta), (wpg[:], w_phig), (wWT[CI:128, :], w_W)]
        loads = [
            (wfu.rearrange("p k o -> p (k o)"), w_fuse), (wca1[:], ca_w1), (wca2[:], ca_w2), (wpr[:], w_proj),
            (wq_s[:], wq), (wk_s[:], wk), (wv_s, wv), (wp_s, wp), (wqkv[:], w_qkv),
            (wm1[:], w_mlp1), *((bm1[MLP * h:MLP * (h + 1), :], b_mlp1) for h in range(NH)),
            *((wm2[MLP * h:MLP * (h + 1), :], w_mlp2) for h in range(NH)),
        ]

        block = ctx.enter_context(nc.Block())

        @block.sync
        def _(sp):
            def start():
                for dst, src in first_loads:
                    sp.dma_start(dst, src).then_inc(sem("first_in"), 16)
                sp.dma_start(xin[:], xd[0, :, :]).then_inc(sem("x_in"), 16)
                for dst, src in loads:
                    sp.dma_start(dst, src).then_inc(sem("weights_in"), 16)

            def late_start():
                yield late_at(0)
                sp.wait_ge(sem("wo_zeroed"), 1)
                for h in range(HEADS):
                    r = 32 * (h % GH)
                    sp.dma_start(wo[r:r + HD, h // GH, :], w_out[HD * h:HD * (h + 1), :]).then_inc(sem("wo_in"), 16)
                sp.wait_ge(sem("ones_ready"), 1)
                sp.wait_ge(sem("packs_zeroed"), 2)
                for hd in range(HEADS):
                    r = 126 + hd % 2
                    sp.dma_start(raw(kp[r:r + 1, hd, :]).rearrange("p (a b) -> p a b", b=128),
                                 raw(ones_r[0:NC, :])).then_inc(sem("k_ones_in"), 16)

            def non_local(bt):
                yield L0 - 4
                if (bt + -1).exists():
                    wait(sp, sem("x1_ready"), bt + -1, NH)
                    sp.dma_start(xin[:], xd[bt.b + bt.off, :, :]).then_inc(sem("x_in"), 16)
                yield non_local_at(18)
                wait(sp, sem("nm0T_ready"), bt)
                sp.dma_start(th[CI:CI + 1, :].rearrange("p (a b) -> p a b", b=128), nm0T[:]).then_inc(sem("nm0_row_in"), 16)

            def wavelet(bt):
                yield L1

            def queries(bt):
                yield maxima2_at(NC * NH) + 2
                wait(sp, sem("nm2T_ready"), bt)
                sp.dma_start(raw(nmrow[0:1, :]).rearrange("p (a b) -> p a b", b=128), raw(nm2T[:])).then_inc(sem("nm2_row_in"), 16)

            def attention(bt):
                yield A3

            def head_norm(bt, g, at):
                yield at

            def tail(bt):
                yield tail_at(24)
                wait(sp, sem("xo_ready"), bt, NH)
                sp.dma_start(od[bt.b + bt.off, :, :], xo[:]).then_inc(sem("out_done"), 16)

            def pack(bt, g, i):
                hd = GH * g + i
                r, c = 64 * (hd % 2), HD * hd
                if i == 0:
                    wait(sp, sem("vt3_ready"), bt, NG, g + 1)
                for dst, parts in ((qp[:, hd // 2, :], (q3h, q3l, q3h)), (kp[:, hd, :], (k3h, k3h, k3l))):
                    for n, part3 in enumerate(parts):
                        sp.dma_start(raw(dst[r + HD * n:r + HD * (n + 1), :]), raw(part3[c:c + HD, :])).then_inc(sem(f"packed{i // 2}"), 16)

            def passes(bt, sides):
                heads = bt.exists()
                for g, (mb, mg) in enumerate(((bt, 1), (bt + 1, 0))):
                    maxima = mb.exists()
                    for p in range(LAPS):
                        if maxima and p % 3 == 0 and p // 3 < GH:
                            pack(mb, mg, p // 3)
                        if maxima and p == M_END + 3:
                            wait(sp, sem("nm3T_ready"), mb, NG, mg + 1)
                            for i in range(GH):
                                hd = GH * mg + i
                                r = 126 + hd % 2
                                sp.dma_start(raw(qp[r:r + 1, hd // 2, :]).rearrange("p (a b) -> p a b", b=128),
                                             raw(nm3T[NC * i:NC * (i + 1), :])).then_inc(sem("nm3_row_in"), 16)
                        for side in sides:
                            side.upto(LAPS * g + p)
                for side in sides:
                    side.finish()

            walk(sp, start, late_start, non_local, wavelet, queries, attention, head_norm, tail, passes)
            sp.wait_ge(sem("out_done"), 16 * B)

        @block.gpsimd
        def _(pool_e):
            g = nc.gpsimd

            def start():
                g.memset(ident[:], 0.0).then_inc(sem("ident_zeroed"), 1)
                pool_e.wait_ge(sem("ident_zeroed"), 1)
                g.affine_select(out=ident[:], in_=ident[:], compare_op=ALU.not_equal, fill=1.0, base=0,
                                pattern=[[-1, 128]], channel_multiplier=1).then_inc(sem("ident_ready"), 1)
                g.memset(neg_half[:], -0.5).then_inc(sem("neg_half_ready"), 1)
                pool_e.wait_ge(sem("vars_ready"), 1)
                pool_e.wait_ge(sem("neg_half_ready"), 1)
                g.tensor_tensor(tmpc[:, 8:14], tmpc[:, 0:6], neg_half[:, 0:6], ALU.pow).then_inc(sem("rsq_ready"), 1)
                g.memset(pad_sb, 0.0).then_inc(sem("pad_zeroed"), 1)
                pool_e.wait_ge(sem("pad_zeroed"), 1)
                p3d = pad_sb.rearrange("c (a b) -> c a b", b=PADW)
                lo = QW - 1 - TAPS // 2
                g.dma_start(p3d[:, lo:lo + TAPS, lo:lo + TAPS], sa_w).then_inc(sem("taps_in"), 16)
                pool_e.wait_ge(sem("taps_in"), 16)
                g.dma_start(pad_dram.rearrange("c a b -> c (a b)"), pad_sb).then_inc(sem("pad_out"), 16)
                pool_e.wait_ge(sem("pad_out"), 16)
                for c in range(2):
                    for yy in range(QW):
                        win = pad_dram[c, yy:yy + QW, 0:QW]
                        src = bass.AP(tensor=win.tensor, offset=win.offset, ap=[[1, QW], [PADW, QW], [1, QW]])
                        r = QW * (yy % 8)
                        g.dma_start(toep_rev[r:r + QW, 2 * c + yy // 8, :].rearrange("p (a b) -> p a b", b=QW),
                                    src).then_inc(sem("windows_in"), 16)
                g.memset(wo[:], 0.0).then_inc(sem("wo_zeroed"), 1)
                for k, (t, width) in enumerate(((grp8, 8), (grp4, 4))):
                    g.memset(t[:], 1.0 / width).then_inc(sem("grp_steps"), 1)
                    pool_e.wait_ge(sem("grp_steps"), 3 * k + 1)
                    v = t[:].rearrange("p (a b) -> p a b", b=width)
                    g.affine_select(out=v, in_=v, compare_op=ALU.is_ge, fill=0.0, base=0,
                                    pattern=[[-width, 128 // width], [0, width]], channel_multiplier=1).then_inc(sem("grp_steps"), 1)
                    pool_e.wait_ge(sem("grp_steps"), 3 * k + 2)
                    g.affine_select(out=v, in_=v, compare_op=ALU.is_ge, fill=0.0, base=width - 1,
                                    pattern=[[width, 128 // width], [0, width]], channel_multiplier=-1).then_inc(sem("grp_steps"), 1)
                g.memset(den_row[:], 0.0).then_inc(sem("den_row_steps"), 1)
                pool_e.wait_ge(sem("den_row_steps"), 1)
                g.affine_select(out=den_row[:], in_=den_row[:], compare_op=ALU.not_equal, fill=1.0, base=-HD,
                                pattern=[[-32, GH]], channel_multiplier=1).then_inc(sem("den_row_steps"), 1)

            def late_start():
                yield late_at(0)
                g.memset(raw(qp[:]), 0.0).then_inc(sem("packs_zeroed"), 1)

            def rstd(bt, tag, mv):
                wait(pool_e, sem("var" + tag + "_ready"), bt)
                g.tensor_tensor(mv[:, 5:6], mv[:, 4:5], neg_half[:, 0:1], ALU.pow).then_inc(sem("rstd" + tag + "_ready"), 1)

            def non_local(bt):
                yield L0

            def wavelet(bt):
                yield L1

            def queries(bt):
                yield L2 + GN_AT[3]
                rstd(bt, "2", mv)

            def attention(bt):
                for h in range(NH):
                    for j in range(1, NC):
                        yield key_at(h, j) + 1
                        u = NC * h + j
                        wait(pool_e, sem("p2_ready"), bt, NC * NH, u + 1)
                        if j > 1:
                            wait(pool_e, sem("acc_steps"), bt, (NC - 1) * NH, h * (NC - 1) + j - 1)
                        first = p2[:, (u - 1) % 4, :] if j == 1 else acc[:, h, :]
                        g.tensor_tensor(acc[:, h, :], first, p2[:, u % 4, :], ALU.add).then_inc(sem("acc_steps"), 1)
                yield A3 + GN_AT[3]
                rstd(bt, "3", mv)

            def head_norm(bt, grp, at):
                yield at

            def tail(bt):
                yield tail_at(10) + GN_AT[3]
                rstd(bt, "4", mv4)

            def passes(bt, sides):
                for p in range(2 * LAPS):
                    for side in sides:
                        side.upto(p)

            walk(pool_e, start, late_start, non_local, wavelet, queries, attention, head_norm, tail, passes)

        @block.scalar
        def _(act):
            a = nc.scalar

            def start():
                act.wait_ge(sem("ones_f_ready"), 1)
                a.copy(ones_r[:], ones[:]).then_inc(sem("ones_ready"), 1)
                act.wait_ge(sem("first_in"), 16 * len(first_loads))
                act.wait_ge(sem("norms_ready"), 1)

            def late_start():
                yield late_at(0)
                act.wait_ge(sem("wpv_ps"), 1)
                a.copy(wpv[:], ps[:, XB, 0:128]).then_inc(sem("wpv_ready"), 1)
                act.wait_ge(sem("weights_in"), 16 * len(loads))

            def non_local(bt):
                for h in range(NH):
                    yield non_local_at(1 + 2 * h)
                    wait(act, sem("theta_ps"), bt, NH, h + 1)
                    a.activation(half(th[0:CI, :], h), ps[0:CI, YB, :], ACT.Identity, bias=bth[:, 0:1]).then_inc(sem("theta_ready"), 1)
                yield non_local_at(17)
                wait(act, sem("nm0T_ps"), bt)
                a.copy(nm0T[:], ps[0:NC, YB, 256:384]).then_inc(sem("nm0T_ready"), 1)
                a.copy(wg[:].rearrange("p a b -> p (a b)"), ps[:, YB, 0:256]).then_inc(sem("wg_ready"), 1)
                for k in range(2 * NH):
                    yield non_local_at(22 + 2 * k)
                    wait(act, sem("s0_ps"), bt, 2 * NH, k + 1)
                    if k == NH:
                        wait(act, sem("out_done"), bt + -4, 16)
                    a.activation(half(p0[:, k // NH, :], k % NH), ps[:, YB, :], ACT.Exp).then_inc(sem("p0_ready"), 1)

                for h in range(NH):
                    yield non_local_at(32 + 2 * h)
                    wait(act, sem("inv0_ps"), bt, NH, h + 1)
                    a.copy(half(x1, h), ps[:, YB, :]).then_inc(sem("rec0_ready"), 1)

            def wavelet(bt):
                yield wavelet_at(1)
                wait(act, sem("fus_ps"), bt)
                a.activation(fused[:], ps[:, XB, 0:Q], ACT.Relu, bias=cst[:, C1:C1 + 1],
                             scale=cst[:, INV1:INV1 + 1]).then_inc(sem("fused_ready"), 1)
                yield wavelet_at(5)
                wait(act, sem("conv_ps"), bt)
                a.activation(sg[:], ps[:, XB, 0:Q], ACT.Exp, scale=-1.0).then_inc(sem("sg_exp"), 1)
                yield wavelet_at(9)
                wait(act, sem("mlp1_ps"), bt)
                a.activation(hid[:], ps[0:HID, XB, 0:2], ACT.Relu, accum_out=hsum[:, 0:1]).then_inc(sem("hid_ready"), 1)
                yield wavelet_at(11)
                wait(act, sem("mlp2_ps"), bt)
                a.activation(chm[:, 0:1], ps[:, XB, 0:1], ACT.Exp, scale=-1.0).then_inc(sem("chm_exp"), 1)
                yield wavelet_at(14)
                for k in range(4):
                    wait(act, sem("proj_ps"), bt, 2, k // 2 + 1)
                    a.activation(pj[:, k, :], ps[:, XB + k // 2, Q * (k % 2):Q * (k % 2 + 1)], ACT.Relu,
                                 bias=cst[:, C2 + k:C2 + k + 1],
                                 scale=cst[:, INV2 + k:INV2 + k + 1]).then_inc(sem("pj_ready"), 1)

            def normalise(bt, src, tag):
                wait(act, sem("norm_shift" + tag), bt)
                a.activation(hn[:], src[:], ACT.Identity, bias=mv[:, 8:9], scale=mv[:, 6:7]).then_inc(sem("h" + tag + "_ready"), 1)

            def queries(bt):
                yield L2 + GN_AT[3]
                normalise(bt, x2, "2")
                for name, hi, at, bias in (("q2", qh, 1, cst[:, BQS:BQS + 1]), ("k2", kh, 3, col("bk"))):
                    yield L2 + GN + PR_AT[at]
                    for h in range(NH):
                        wait(act, sem(name + "_ps"), bt, NH, h + 1)
                        a.activation(half(hi, h), ps[:, XB + h, :], ACT.Identity, bias=bias).then_inc(sem(name + "_hi"), 1)
                yield L2 + GN + PR_AT[5]
                wait(act, sem("v2_ps"), bt)
                a.copy(vT[:].rearrange("p a b -> p (a b)"), two(XB)).then_inc(sem("v2_ready"), 1)
                yield maxima2_at(NC * NH) + 1
                wait(act, sem("nm2T_ps"), bt)
                a.copy(nm2T[:], ps[0:NC, XB, 0:128]).then_inc(sem("nm2T_ready"), 1)

            def attention(bt):
                for h in range(NH):
                    for j in range(NC):
                        yield key_at(h, j)
                        u = NC * h + j
                        if u >= 4:
                            wait(act, sem("pv2_done"), bt, NC * NH, u - 3)
                            hh, jj = divmod(u - 4, NC)
                            wait(act, sem("acc_steps"), bt, (NC - 1) * NH, hh * (NC - 1) + max(jj, 1))
                        wait(act, sem("s2_ps"), bt, NC * NH, u + 1)
                        a.activation(p2[:, u % 4, :], ps[:, XB, :], ACT.Exp).then_inc(sem("p2_ready"), 1)
                    yield A2[h] + A2_QUARTERS * NC // 4 + A2_END[0] + 1
                    wait(act, sem("pv2_done"), bt, NC * NH, NC * (h + 1))
                    a.copy(ysb[:], ps[:, XB + 1, :]).then_inc(sem("y2_ready"), 1)
                yield A3 + GN_AT[3]
                normalise(bt, x3, "3")
                for name, hi, at, scale in (("q3", q3h, 1, cst[:, TMP:TMP + 1]), ("k3", k3h, 3, 1.0)):
                    yield A3 + GN + PR_AT[at]
                    for h in range(NH):
                        wait(act, sem(name + "_ps"), bt, NH, h + 1)
                        a.activation(half(hi, h), ps[:, XB + h, :], ACT.Copy, scale=scale).then_inc(sem(name + "_hi"), 1)
                yield A3 + GN + PR_AT[5]
                wait(act, sem("v3_ps"), bt)
                wait(act, sem("vt3_ready"), bt + -1, NG)
                a.copy(v3[:].rearrange("p j h d -> p (j h d)"), two(XB)).then_inc(sem("v3_ready"), 1)

            def head_norm(bt, g, at):
                yield at + 1
                wait(act, sem("inv3_ready"), bt, NG, g + 1)
                a.copy(heads_inverse[g], inv3[:].unsqueeze(3).to_broadcast([128, NC, GH, 32])).then_inc(sem("inv3w_ready"), 1)

            def tail(bt):
                yield tail_at(18)
                wait(act, sem("h4_ps"), bt)
                a.activation(gl, ps[0:NH * MLP, YB, :], ACT.Gelu, bias=bm1[:, 0:1]).then_inc(sem("gelu_ready"), 1)

            def passes(bt, sides):
                heads = bt.exists()
                for g, (mb, mg) in enumerate(((bt, 1), (bt + 1, 0))):
                    maxima = mb.exists()
                    for p in range(LAPS):
                        s, i = divmod(p, GH)
                        if p == 0 and maxima:
                            wait(act, sem("k3_split"), mb, NH)
                            wait(act, sem("v3_ready"), mb)
                            wait(act, sem("pv3_done"), mb + -1, NG * STEPS, (mg + 1) * STEPS)
                            a.copy(vt3[mg][:, :, :, 0:HD], v3[:, :, GH * mg:GH * (mg + 1), :]).then_inc(sem("vt3_ready"), 1)
                        if heads and s < STEPS:
                            step = g * STEPS + s
                            if i == 0 and step >= 2:
                                wait(act, sem("pv3_done"), bt, NG * STEPS, step - 1)
                            elif i == 0:
                                wait(act, sem("pv3_done"), bt + -1, NG * STEPS, NG * STEPS - 1 + step)
                            u = g * TILES + p
                            wait(act, sem("s3_ps"), bt, NG * TILES, u + 1)
                            a.activation(p3[:, s % 2, i, :], ps[:, SB + p % 2, :], ACT.Exp).then_inc(sem("p3_ready"), 1)
                        if heads and i == GH - 1 and s and s % NC == 0:
                            wait(act, sem("o3_ps"), bt + -1, NH)
                            wait(act, sem("pv3_done"), bt, NG * STEPS, g * STEPS + s)
                            a.copy(half(og[:, g, :], s // NC - 1), ps[:, VB, :]).then_inc(sem("og_ready"), 1)
                        if maxima and p == M_END + 2:
                            wait(act, sem("nm3T_ps"), mb, NG, mg + 1)
                            a.copy(nm3T[:], ps[0:GH * NC, MB, 0:128]).then_inc(sem("nm3T_ready"), 1)
                        for side in sides:
                            side.upto(LAPS * g + p)
                for side in sides:
                    side.finish()

            walk(act, start, late_start, non_local, wavelet, queries, attention, head_norm, tail, passes)

        @block.vector
        def _(dve):
            v = nc.vector

            steps = [0]

            def link0(ins):
                steps[0] += 1
                ins.then_inc(sem("dve_setup"), 1)
                dve.wait_ge(sem("dve_setup"), steps[0])

            def start():
                v.memset(ones[:], 1.0).then_inc(sem("ones_f_ready"), 1)
                v.memset(th[CI:128, :], 0.0).then_inc(sem("rows_set"), 1)
                v.memset(phz[CI:128, :], 0.0).then_inc(sem("rows_set"), 1)
                link0(v.memset(ph[CI:128, :], 0.0))
                v.memset(ph[CI:CI + 1, :], 1.0).then_inc(sem("rows_set"), 1)
                dve.wait_ge(sem("first_in"), 16 * len(first_loads))
                link0(v.tensor_scalar(tmpc[:, 0:1], col("bn_var"), 1e-5, None, ALU.add))
                link0(v.tensor_scalar(tmpc[:, 1:2], col("bn1_v"), 1e-5, None, ALU.add))
                v.tensor_scalar(tmpc[:, 2:6], vec[:, V["bn2_v0"]:V["bn2_v0"] + 4], 1e-5, None, ALU.add).then_inc(sem("vars_ready"), 1)
                dve.wait_ge(sem("rsq_ready"), 1)
                link0(v.tensor_tensor(cst[:, INV0:INV0 + 1], col("bn_gamma"), tmpc[:, 8:9], ALU.mult))
                link0(v.tensor_tensor(tmpc[:, 16:17], col("b_W"), col("bn_mean"), ALU.subtract))
                link0(v.scalar_tensor_tensor(cst[:, C0:C0 + 1], tmpc[:, 16:17], cst[:, INV0:INV0 + 1], col("bn_beta"), ALU.mult, ALU.add))
                link0(v.tensor_tensor(cst[:, INV1:INV1 + 1], col("bn1_g"), tmpc[:, 9:10], ALU.mult))
                link0(v.tensor_tensor(tmpc[:, 17:18], col("fusion_b"), col("bn1_m"), ALU.subtract))
                link0(v.scalar_tensor_tensor(cst[:, C1:C1 + 1], tmpc[:, 17:18], cst[:, INV1:INV1 + 1], col("bn1_b"), ALU.mult, ALU.add))
                c4 = lambda n: vec[:, V[n + "0"]:V[n + "0"] + 4]
                link0(v.scalar_tensor_tensor(cst[:, INV2:INV2 + 4], c4("bn2_g"), 0.5, tmpc[:, 10:14], ALU.mult, ALU.mult))
                link0(v.tensor_tensor(tmpc[:, 20:24], c4("proj_b"), c4("bn2_m"), ALU.subtract))
                link0(v.tensor_tensor(tmpc[:, 24:28], tmpc[:, 20:24], cst[:, INV2:INV2 + 4], ALU.mult))
                link0(v.scalar_tensor_tensor(cst[:, C2:C2 + 4], c4("bn2_b"), 0.5, tmpc[:, 24:28], ALU.mult, ALU.add))
                link0(v.tensor_scalar(cst[:, BQS:BQS + 1], col("bq"), QS, None, ALU.mult))
                v.tensor_scalar(cst[:, TMP:TMP + 1], col("temp"), 1e-4, 10.0, ALU.max, ALU.min).then_inc(sem("norms_ready"), 1)

            def late_start():
                yield late_at(0)
                for t in vt3:
                    v.memset(t[:], 1.0).then_inc(sem("v_ones"), 1)
                v.memset(raw(kp[:]), 0.0).then_inc(sem("packs_zeroed"), 1)
                dve.wait_ge(sem("weights_in"), 16 * len(loads))
                v.tensor_scalar(wq_s[:], wq_s[:], QS, None, ALU.mult)
                dve.wait_ge(sem("wpv_ps"), 1)
                link0(v.tensor_tensor(cst[:, B2:B2 + 1], ps[:, XB + 1, 0:1], col("bp"), ALU.add))
                link0(v.tensor_scalar(wfu, wfu, 0.5, None, ALU.mult))
                link0(v.tensor_tensor(wfs[:, 0, :], wfu[:, 0, :], wfu[:, 1, :], ALU.add))
                link0(v.tensor_tensor(wfs[:, 1, :], wfu[:, 2, :], wfu[:, 3, :], ALU.add))
                link0(v.tensor_tensor(wfs[:, 2, :], wfu[:, 0, :], wfu[:, 1, :], ALU.subtract))
                link0(v.tensor_tensor(wfs[:, 3, :], wfu[:, 2, :], wfu[:, 3, :], ALU.subtract))
                link0(v.tensor_tensor(wfc[:, 0, :], wfs[:, 0, :], wfs[:, 1, :], ALU.add))
                link0(v.tensor_tensor(wfc[:, 1, :], wfs[:, 0, :], wfs[:, 1, :], ALU.subtract))
                link0(v.tensor_tensor(wfc[:, 2, :], wfs[:, 2, :], wfs[:, 3, :], ALU.add))
                link0(v.tensor_tensor(wfc[:, 3, :], wfs[:, 2, :], wfs[:, 3, :], ALU.subtract))
                yield late_at(1)
                dve.wait_ge(sem("windows_in"), 16 * 2 * QW)
                for t in range(4):
                    last = v.tensor_scalar(toep[:, t, :], toep_rev[:, t, ::-1], 1.0 / C if t < 2 else 1.0, None, ALU.mult)
                last.then_inc(sem("consts_ready"), 1)


            def linker(stage, bt, per):
                count = [0]

                def link(ins):
                    count[0] += 1
                    assert count[0] <= per
                    ins.then_inc(sem(stage + "_steps"), 1)
                    wait(dve, sem(stage + "_steps"), bt, per, count[0])
                return link

            def carry_wait():
                v.memset(idle[:, 0:1], 0.0)

            def group_norm(at, bt, src, ready, n, eps, gam, bet, tag, hn, mv, gm, gv):
                link = linker("norm" + tag, bt, 4)
                yield at
                wait(dve, sem(ready), bt, n)
                for h in range(NH):
                    link(v.bn_stats(mv[:, 16 + 6 * h:22 + 6 * h], half(src, h)))
                carry_wait()
                v.bn_aggr(mv[:, 0:2], mv[:, 16:28].rearrange("p (a b) -> p a b", b=6)).then_inc(sem("mv" + tag), 1)
                yield at + GN_AT[1]
                wait(dve, sem("gm_ps" + tag), bt)
                link(v.tensor_tensor(mv[:, 2:3], mv[:, 0:1], gm, ALU.subtract))
                v.scalar_tensor_tensor(mv[:, 3:4], mv[:, 2:3], mv[:, 2:3], mv[:, 1:2], ALU.mult, ALU.add).then_inc(sem("vd" + tag), 1)
                yield at + GN_AT[3]
                wait(dve, sem("gv_ps" + tag), bt)
                v.tensor_scalar(mv[:, 4:5], gv, eps, None, ALU.add).then_inc(sem("var" + tag + "_ready"), 1)
                link(v.tensor_tensor(mv[:, 7:8], mv[:, 2:3], mv[:, 0:1], ALU.subtract))
                wait(dve, sem("rstd" + tag + "_ready"), bt)
                v.tensor_tensor(mv[:, 6:7], mv[:, 5:6], col(gam), ALU.mult).then_inc(sem("norm_scale" + tag), 1)
                wait(dve, sem("norm_scale" + tag), bt)
                v.scalar_tensor_tensor(mv[:, 8:9], mv[:, 7:8], mv[:, 6:7], col(bet), ALU.mult, ALU.add).then_inc(sem("norm_shift" + tag), 1)
                if tag == "4":
                    wait(dve, sem("norm_shift" + tag), bt)
                    v.tensor_scalar(hn[:], src[:], mv[:, 6:7], mv[:, 8:9], ALU.mult, ALU.add).then_inc(sem("h" + tag + "_ready"), 1)

            def low_parts(bt, name, hi, lo, scalar, op):
                for h in range(NH):
                    wait(dve, sem(name + "_hi"), bt, NH, h + 1)
                    if scalar is None:
                        ins = v.tensor_tensor(half(lo, h), ps[:, XB + h, :], raw(half(hi, h)), ALU.subtract)
                    else:
                        ins = v.scalar_tensor_tensor(half(lo, h), ps[:, XB + h, :], scalar, raw(half(hi, h)), op, ALU.subtract)
                    ins.then_inc(sem(name + "_split"), 1)

            def non_local(bt):
                link = linker("l0", bt, 2)
                for h in range(NH):
                    yield non_local_at(5 + 2 * h)
                    wait(dve, sem("phig_ps"), bt, NH, h + 1)
                    src = ps[:, YB, :].rearrange("p (y a x b) -> p y x a b", a=2, b=2, x=QW)
                    v.tensor_reduce(part(pg, h).rearrange("p (y x) -> p y x", x=QW), src, AX.XY, ALU.max).then_inc(sem("pooled"), 1)
                wait(dve, sem("pooled"), bt, NH)
                bias = vec[:, V["b_phig"]:V["b_phig"] + 1]
                v.tensor_scalar(phz[0:CI, :], pg[0:CI, :], bias[0:CI, :], None, ALU.add).then_inc(sem("phi_ready"), 1)
                v.tensor_scalar(ph[0:CI, :], pg[0:CI, :], bias[0:CI, :], None, ALU.add).then_inc(sem("phi_ready"), 1)
                v.tensor_scalar(gt[CI:128, :], pg[CI:128, :], bias[CI:128, :], None, ALU.add).then_inc(sem("g_ready"), 1)
                for k in range(4):
                    yield non_local_at(9 + 2 * k)
                    wait(dve, sem("s0max_ps"), bt, 4, k + 1)
                    v.tensor_reduce(nm0[:, 2 * k:2 * k + 2], ps[:, YB, :].rearrange("p (a b) -> p a b", b=M0), AX.X,
                                    ALU.max, negate=True).then_inc(sem("nm0_ready"), 1)
                yield non_local_at(30)
                wait(dve, sem("den0_ps"), bt)
                v.reciprocal(inv0[:], ps[:, YB, 0:NC]).then_inc(sem("inv0_ready"), 1)
                for h in range(NH):
                    yield non_local_at(36 + 2 * h)
                    wait(dve, sem("y0_ps"), bt, NH, h + 1)
                    link(v.scalar_tensor_tensor(half(x1, h), ps[:, YB, :], cst[:, INV0:INV0 + 1], half(x1, h), ALU.mult, ALU.mult))
                    v.scalar_tensor_tensor(half(x1, h), half(x1, h), cst[:, C0:C0 + 1], half(xin, h), ALU.add, ALU.add).then_inc(sem("x1_ready"), 1)

            def wavelet(bt):
                link = linker("l1", bt, 7)
                yield wavelet_at(3)
                wait(dve, sem("fT_ps"), bt)
                fT = ps[:, XB, 256:512].rearrange("p (a b) -> p a b", b=128)
                v.tensor_reduce(spT[:, 0, :], fT, AX.X, ALU.add).then_inc(sem("sp_ready"), 1)
                v.tensor_reduce(spT[:, 1, :], fT, AX.X, ALU.max).then_inc(sem("sp_ready"), 1)
                yield wavelet_at(6)
                wait(dve, sem("sg_exp"), bt)
                link(v.tensor_scalar(sg[:], sg[:], 1.0, None, ALU.add))
                link(v.reciprocal(sg[:], sg[:]))
                link(v.scalar_tensor_tensor(spat[:], sg[:], 1.0 / Q, fused[:], ALU.mult, ALU.mult, accum_out=pool[:, 0:1]))
                link(v.tensor_reduce(chm[:, 3:4], spat[:], AX.X, ALU.max))
                v.tensor_scalar(pool[:, 1:2], chm[:, 3:4], float(Q), None, ALU.mult).then_inc(sem("pool_ready"), 1)
                yield wavelet_at(12)
                wait(dve, sem("chm_exp"), bt)
                link(v.tensor_scalar(chm[:, 1:2], chm[:, 0:1], 1.0, None, ALU.add))
                link(v.reciprocal(chm[:, 2:3], chm[:, 1:2]))
                v.tensor_scalar(chout[:], spat[:], chm[:, 2:3], float(Q), ALU.mult, ALU.mult).then_inc(sem("chout_ready"), 1)
                yield wavelet_at(15)
                wait(dve, sem("pj_ready"), bt, 4)
                even, odd = pj[:, 0::2, :], pj[:, 1::2, :]
                v.tensor_tensor(sd[:, 0, :, :], even, odd, ALU.add)
                link(v.tensor_tensor(sd[:, 1, :, :], even, odd, ALU.subtract))
                x1v = x1[:].rearrange("p (y r x c) -> p y r x c", r=2, c=2, x=QW)
                x2v = x2[:].rearrange("p (y r x c) -> p y r x c", r=2, c=2, x=QW)
                for r in range(2):
                    for c in range(2):
                        s = sd[:, r, 0, :].rearrange("p (y x) -> p y x", x=QW)
                        v.tensor_tensor(x2v[:, :, r, :, c], x1v[:, :, r, :, c], s, ALU.add).then_inc(sem("ux_ready"), 1)
                wait(dve, sem("ux_ready"), bt, 4)
                for r in range(2):
                    for c in range(2):
                        s = sd[:, r, 1, :].rearrange("p (y x) -> p y x", x=QW)
                        v.tensor_tensor(x2v[:, :, r, :, c], x2v[:, :, r, :, c], s,
                                        ALU.subtract if c else ALU.add).then_inc(sem("x2_ready"), 1)

            def queries(bt):
                yield from group_norm(L2, bt, x2, "x2_ready", 4, 1e-6, "gamma", "beta", "2", hn, mv, ps[:, XB, 0:1], ps[:, XB + 1, 0:1])
                yield L2 + GN + PR_AT[1]
                low_parts(bt, "q2", qh, ql, cst[:, BQS:BQS + 1], ALU.add)
                yield L2 + GN + PR_AT[3]
                low_parts(bt, "k2", kh, kl, col("bk"), ALU.add)
                for u in range(NC * NH):
                    yield maxima2_at(u)
                    wait(dve, sem("s2max_ps"), bt, NC * NH, u + 1)
                    v.tensor_reduce(mx[:, u // NH, u % NH:u % NH + 1], ps[:, XB + u % 2, :], AX.X, ALU.max).then_inc(sem("mx2_ready"), 1)
                wait(dve, sem("mx2_ready"), bt, NC * NH)
                v.tensor_reduce(nm2[:], mx[:], AX.X, ALU.max, negate=True).then_inc(sem("nm2_ready"), 1)

            def attention(bt):
                link = linker("l2", bt, NH)
                yield X3_KEPT
                if (bt + -1).exists():
                    wait(dve, sem("x4_ready"), bt + -2, NH)
                    wait(dve, sem("x3_ready"), bt + -1, NH)
                    v.tensor_copy(x3s[:], x3[:]).then_inc(sem("x3_kept"), 1)
                for h in range(NH):
                    yield A2[h] + A2_QUARTERS * NC // 4 + A2_END[2]
                    wait(dve, sem("den2_ps"), bt, NH, h + 1)
                    v.reciprocal(inv2[:], ps[:, XB + 1, 0:NC // 2]).then_inc(sem("inv2_ready"), 1)
                    yield A2[h] + A2_QUARTERS * NC // 4 + A2_END[3]
                    wait(dve, sem("inv2_ps"), bt, NH, h + 1)
                    link(v.tensor_tensor(half(x3, h), ysb[:], ps[:, XB + 1, :], ALU.mult))
                    v.scalar_tensor_tensor(half(x3, h), half(x3, h), cst[:, B2:B2 + 1], half(x2, h), ALU.add, ALU.add).then_inc(sem("x3_ready"), 1)
                yield from group_norm(A3, bt, x3, "x3_ready", NH, 1e-5, "g1", "beta1", "3", hn, mv, ps[:, XB, 0:1], ps[:, XB + 1, 0:1])
                yield A3 + GN + PR_AT[1]
                low_parts(bt, "q3", q3h, q3l, cst[:, TMP:TMP + 1], ALU.mult)
                yield A3 + GN + PR_AT[3]
                low_parts(bt, "k3", k3h, k3l, None, None)

            def head_norm(bt, g, at):
                inv3w, banks = heads_inverse[g], HEAD_BANKS[g]
                yield at + 1
                wait(dve, sem("den3_ps"), bt, NG, g + 1)
                v.reciprocal(inv3[:].rearrange("p c i -> p (c i)"), ps[:, banks[0], 0:NC * GH]).then_inc(sem("inv3_ready"), 1)
                for h in range(NH):
                    yield at + 3 + 2 * h
                    n = NH * g + h
                    wait(dve, sem("inv3_ps"), bt, NG * NH, n + 1)
                    v.tensor_tensor(half(og[:, g, :], h), half(og[:, g, :], h), ps[:, banks[h], :], ALU.mult).then_inc(sem("yn_ready"), 1)

            def tail(bt):
                if not (bt + 1).exists():
                    x3_kept = x3
                    wait(dve, sem("x3_ready"), bt, NH)
                else:
                    x3_kept = x3s
                    wait(dve, sem("x3_kept"), bt)
                for h in range(NH):
                    yield tail_at(7 + 2 * h)
                    wait(dve, sem("o3_ps"), bt, NH, h + 1)
                    v.scalar_tensor_tensor(half(x4, h), ps[:, YB, :], col("b_out"), half(x3_kept, h), ALU.add, ALU.add).then_inc(sem("x4_ready"), 1)
                if not (bt + 3).exists():
                    wait(dve, sem("out_done"), bt + -1, 16)
                yield from group_norm(tail_at(10), bt, x4, "x4_ready", NH, 1e-5, "g2", "beta2", "4", hn4, mv4, ps[:, YB, 0:1], ps[:, YB, 1:2])
                for h in range(NH):
                    yield tail_at(21 + 2 * h)
                    wait(dve, sem("m4_ps"), bt, NH, h + 1)
                    v.scalar_tensor_tensor(half(xo, h), ps[:, YB, :], col("b_mlp2"), half(x4, h), ALU.add, ALU.add).then_inc(sem("xo_ready"), 1)

            def largest(n, mb, mg):
                u = mg * TILES + n
                wait(dve, sem("s3max_ps"), mb, NG * TILES, u + 1)
                i, c, h = n // (NC * NH), n // NH % NC, n % NH
                v.tensor_reduce(mx3[:, i, c, h:h + 1], ps[:, MB + n % 2, :], AX.X, ALU.max).then_inc(sem("mx3_ready"), 1)

            def passes(bt, sides):
                heads = bt.exists()
                for g, (mb, mg) in enumerate(((bt, 1), (bt + 1, 0))):
                    maxima = mb.exists()
                    for p in range(LAPS):
                        early, late = maxima_at(mg, p) if maxima else ((), ())
                        for n in early:
                            largest(n, mb, mg)
                        if maxima and p == M_END:
                            wait(dve, sem("mx3_ready"), mb, NG * TILES, (mg + 1) * TILES)
                            v.tensor_reduce(nm3[:], mx3[:].rearrange("p i c h -> p (i c) h"), AX.X, ALU.max,
                                            negate=True).then_inc(sem("nm3_ready"), 1)
                        for side in sides:
                            side.upto(LAPS * g + p)
                        for n in late:
                            largest(n, mb, mg)
                for side in sides:
                    side.finish()

            walk(dve, start, late_start, non_local, wavelet, queries, attention, head_norm, tail, passes)

        @block.tensor
        def _(pe):
            def mm(o, l, r, start=True, stop=True):
                return nc.tensor.matmul(o, l, r, start=start, stop=stop)

            def start():
                pe.wait_ge(sem("first_in"), 16 * len(first_loads))
                pe.wait_ge(sem("ident_ready"), 1)
                pe.wait_ge(sem("ones_f_ready"), 1)
                pe.wait_ge(sem("rows_set"), 3)

            def late_start():
                yield late_at(0)
                pe.wait_ge(sem("weights_in"), 16 * len(loads))
                mm(ps[:, XB, 0:128], wv_s, wp_s)
                mm(ps[:, XB + 1, 0:1], wp_s, col("bv")).then_inc(sem("wpv_ps"), 1)
                yield late_at(1)
                pe.wait_ge(sem("wpv_ready"), 1)
                pe.wait_ge(sem("consts_ready"), 1)
                pe.wait_ge(sem("ones_ready"), 1)
                pe.wait_ge(sem("grp_steps"), 6)
                pe.wait_ge(sem("den_row_steps"), 2)

            def project_T(w, x, o):
                for c in range(NC):
                    last = mm(bank_part(o, c), part(x, c), w)
                return last

            def split_products(at, bt, q, k, wq, wk, wv, tag):
                yield at
                wait(pe, sem("h" + tag + "_ready"), bt)
                for h in range(NH):
                    mm(ps[:, XB + h, :], wq, half(hn, h)).then_inc(sem(q + "_ps"), 1)
                yield at + PR_AT[2]
                for h in range(NH):
                    wait(pe, sem(q + "_split"), bt, NH, h + 1)
                    mm(ps[:, XB + h, :], wk, half(hn, h)).then_inc(sem(k + "_ps"), 1)
                yield at + PR_AT[4]
                wait(pe, sem(k + "_split"), bt, NH)
                project_T(wv, hn, XB).then_inc(sem("v" + tag + "_ps"), 1)

            def group_averages(at, bt, t, tag, mv, gm, gv):
                yield at + GN_AT[0]
                wait(pe, sem("mv" + tag), bt)
                mm(gm, t[:], mv[:, 0:1]).then_inc(sem("gm_ps" + tag), 1)
                yield at + GN_AT[2]
                wait(pe, sem("vd" + tag), bt)
                mm(gv, t[:], mv[:, 3:4]).then_inc(sem("gv_ps" + tag), 1)

            def non_local(bt):
                yield L0
                wait(pe, sem("x1_ready"), bt + -1, NH)
                wait(pe, sem("xo_ready"), bt + -4, NH)
                wait(pe, sem("x_in"), bt, 16)
                for h in range(NH):
                    yield non_local_at(2 * h)
                    if h:
                        wait(pe, sem("theta_ready"), bt, NH, h)
                    mm(ps[0:CI, YB, :], wth[:], half(xin, h)).then_inc(sem("theta_ps"), 1)
                for h in range(NH):
                    yield non_local_at(4 + 2 * h)
                    if h:
                        wait(pe, sem("pooled"), bt, NH, h)
                    else:
                        wait(pe, sem("theta_ready"), bt, NH)
                    mm(ps[:, YB, :], wpg[:], half(xin, h)).then_inc(sem("phig_ps"), 1)
                for k in range(4):
                    yield non_local_at(8 + 2 * k)
                    if k:
                        wait(pe, sem("nm0_ready"), bt, 4, k)
                    else:
                        wait(pe, sem("phi_ready"), bt, 2)
                    for c in (2 * k, 2 * k + 1):
                        last = mm(ps[:, YB, M0 * (c % 2):M0 * (c % 2 + 1)], part(th, c), phz[:])
                    last.then_inc(sem("s0max_ps"), 1)
                yield non_local_at(16)
                wait(pe, sem("g_ready"), bt)
                wait(pe, sem("nm0_ready"), bt, 4)
                for m in range(2):
                    mm(ps[:, YB, 128 * m:128 * (m + 1)], part(gt[CI:128, :], m), wWT[CI:128, :])
                nc.tensor.transpose(ps[0:NC, YB, 256:384], nm0[:], ident[:]).then_inc(sem("nm0T_ps"), 1)
                for k in range(2 * NH):
                    yield non_local_at(21 + 2 * k)
                    if k:
                        wait(pe, sem("p0_ready"), bt, 2 * NH, k)
                    else:
                        wait(pe, sem("nm0_row_in"), bt, 16)
                        wait(pe, sem("wg_ready"), bt)
                    mm(ps[:, YB, :], part(ph, k // NH), half(th, k % NH)).then_inc(sem("s0_ps"), 1)
                yield non_local_at(29)
                wait(pe, sem("p0_ready"), bt, 2 * NH)
                for c in range(NC):
                    for m in range(2):
                        last = mm(ps[:, YB, c:c + 1], part(p0[:, m, :], c), ones[:, 0:1], start=m == 0, stop=m == 1)
                last.then_inc(sem("den0_ps"), 1)
                for h in range(NH):
                    yield non_local_at(31 + 2 * h)
                    if h:
                        wait(pe, sem("rec0_ready"), bt, NH, h)
                    else:
                        wait(pe, sem("inv0_ready"), bt)
                    for c in range(NC // 2):
                        k = NC // 2 * h + c
                        last = mm(part(ps[:, YB, :], c), inv0[:, k:k + 1].to_broadcast([128, 128]), ident[:])
                    last.then_inc(sem("inv0_ps"), 1)
                for h in range(NH):
                    yield non_local_at(35 + 2 * h)
                    if h:
                        wait(pe, sem("x1_ready"), bt, NH, h)
                    else:
                        wait(pe, sem("rec0_ready"), bt, NH)
                    for m in range(2):
                        last = mm(ps[:, YB, :], wg[:, m, :], half(p0[:, m, :], h), start=m == 0, stop=m == 1)
                    last.then_inc(sem("y0_ps"), 1)

            def wavelet(bt):
                yield L1
                wait(pe, sem("x1_ready"), bt, NH)
                wait(pe, sem("yn_ready"), bt + -2, NG * NH, NH)
                wait(pe, sem("v3_ready"), bt + -1)
                x1v = x1[:].rearrange("p (y r x c) -> p y r x c", r=2, c=2, x=QW)
                for k in range(4):
                    last = mm(ps[:, XB, 0:Q].rearrange("p (y x) -> p y x", x=QW), wfc[:, k, :], x1v[:, :, k // 2, :, k % 2],
                              start=k == 0, stop=k == 3)
                last.then_inc(sem("fus_ps"), 1)
                yield wavelet_at(2)
                wait(pe, sem("fused_ready"), bt)
                for k in range(2):
                    last = nc.tensor.transpose(ps[:, XB, 256 + 128 * k:384 + 128 * k], part(fused, k), ident[:])
                last.then_inc(sem("fT_ps"), 1)
                yield wavelet_at(4)
                wait(pe, sem("sp_ready"), bt, 2)
                for k in range(4):
                    last = mm(ps[:, XB, 0:Q], spT[:, k // 2, k % 2:k % 2 + 1].to_broadcast([128, 128]), toep[:, k, :],
                              start=k == 0, stop=k == 3)
                last.then_inc(sem("conv_ps"), 1)
                yield wavelet_at(8)
                wait(pe, sem("pool_ready"), bt)
                mm(ps[0:HID, XB, 0:2], wca1[:], pool[:]).then_inc(sem("mlp1_ps"), 1)
                yield wavelet_at(10)
                wait(pe, sem("hid_ready"), bt)
                mm(ps[:, XB, 0:1], wca2[:], hsum[:]).then_inc(sem("mlp2_ps"), 1)
                yield wavelet_at(13)
                wait(pe, sem("chout_ready"), bt)
                for k in range(4):
                    last = mm(ps[:, XB + k // 2, Q * (k % 2):Q * (k % 2 + 1)], part(wpr, k), chout[:])
                    if k % 2:
                        last.then_inc(sem("proj_ps"), 1)

            def queries(bt):
                yield from group_averages(L2, bt, grp8, "2", mv, ps[:, XB, 0:1], ps[:, XB + 1, 0:1])
                yield from split_products(L2 + GN, bt, "q2", "k2", wq_s[:], wk_s[:], wpv[:], "2")
                for u in range(NC * NH):
                    yield maxima2_at(u)
                    if u == 0:
                        wait(pe, sem("v2_ready"), bt)
                    if u >= 2:
                        wait(pe, sem("mx2_ready"), bt, NC * NH, u - 1)
                    mm(ps[:, XB + u % 2, :], part(qh, u // NH), half(kh, u % NH)).then_inc(sem("s2max_ps"), 1)
                yield maxima2_at(NC * NH)
                wait(pe, sem("nm2_ready"), bt)
                nc.tensor.transpose(ps[0:NC, XB, 0:128], nm2[:], ident[:]).then_inc(sem("nm2T_ps"), 1)

            def attention(bt):
                def scores(h, j):
                    u = NC * h + j
                    if u:
                        wait(pe, sem("p2_ready"), bt, NC * NH, u)
                    o = ps[:, XB, :]
                    mm(o, part(kh, j), half(qh, h), stop=False)
                    mm(o, part(kh, j), half(ql, h), start=False, stop=False)
                    mm(o, part(kl, j), half(qh, h), start=False, stop=False)
                    mm(o, ones_r[0:1, :], half(nmrow, h), start=False).then_inc(sem("s2_ps"), 1)

                def values(h, j):
                    u = NC * h + j
                    wait(pe, sem("p2_ready"), bt, NC * NH, u + 1)
                    mm(ps[:, XB + 1, :], vT[:, j, :], p2[:, u % 4, :], start=j == 0, stop=j == NC - 1).then_inc(sem("pv2_done"), 1)

                yield A2[0]
                wait(pe, sem("nm2_row_in"), bt, 16)
                for h in range(NH):
                    for j in range(NC):
                        yield key_at(h, j)
                        scores(h, j)
                        if j == 1 and h:
                            wait(pe, sem("x3_ready"), bt, NH, h)
                        if j:
                            values(h, j - 1)
                    yield A2[h] + A2_QUARTERS * NC // 4 + A2_END[0]
                    values(h, NC - 1)
                    yield A2[h] + A2_QUARTERS * NC // 4 + A2_END[1]
                    wait(pe, sem("y2_ready"), bt, NH, h + 1)
                    wait(pe, sem("acc_steps"), bt, (NC - 1) * NH, (NC - 1) * (h + 1))
                    for c in range(NC // 2):
                        last = mm(ps[:, XB + 1, c:c + 1], part(acc[:, h, :], c), ones[:, 0:1])
                    last.then_inc(sem("den2_ps"), 1)
                    yield A2[h] + A2_QUARTERS * NC // 4 + A2_END[2]
                    wait(pe, sem("inv2_ready"), bt, NH, h + 1)
                    for c in range(NC // 2):
                        last = mm(ps[:, XB + 1, 128 * c:128 * (c + 1)], inv2[:, c:c + 1].to_broadcast([128, 128]), ident[:])
                    last.then_inc(sem("inv2_ps"), 1)
                yield from group_averages(A3, bt, grp4, "3", mv, ps[:, XB, 0:1], ps[:, XB + 1, 0:1])
                yield from split_products(A3 + GN, bt, "q3", "k3", wqkv[:, 0:128], wqkv[:, 128:256], wqkv[:, 256:384], "3")

            def head_norm(bt, g, at):
                yield at
                inv3w, banks = heads_inverse[g], HEAD_BANKS[g]
                wait(pe, sem("og_ready"), bt, NG * NH, NH * (g + 1))
                if g == 0:
                    wait(pe, sem("v3_ready"), bt + 1)
                elif (bt + 3).exists():
                    wait(pe, sem("x1_ready"), bt + 3, NH)
                else:
                    wait(pe, sem("xo_ready"), bt + -1, NH)
                    wait(pe, sem("x1_ready"), bt + 3, NH)
                for c in range(NC):
                    last = mm(ps[:, banks[0], GH * c:GH * (c + 1)], part(og[:, g, :], c), den_row[:])
                last.then_inc(sem("den3_ps"), 1)
                for h in range(NH):
                    yield at + 2 + 2 * h
                    if h:
                        wait(pe, sem("yn_ready"), bt, NG * NH, NH * g + h)
                    else:
                        wait(pe, sem("inv3w_ready"), bt, NG, g + 1)
                    for c in range(NC // 2):
                        last = mm(part(ps[:, banks[h], :], c), inv3w[:, NC // 2 * h + c, :, :].rearrange("p i r -> p (i r)"), ident[:])
                    last.then_inc(sem("inv3_ps"), 1)

            def tail(bt):
                for h in range(NH):
                    yield tail_at(6 + 2 * h)
                    if h:
                        wait(pe, sem("x4_ready"), bt, NH, h)
                    else:
                        wait(pe, sem("yn_ready"), bt, NG * NH)
                    for g in range(NG):
                        last = mm(ps[:, YB, :], wo[:, g, :], half(og[:, g, :], h), start=g == 0, stop=g == NG - 1)
                    last.then_inc(sem("o3_ps"), 1)
                yield from group_averages(tail_at(10), bt, grp4, "4", mv4, ps[:, YB, 0:1], ps[:, YB, 1:2])
                yield tail_at(17)
                wait(pe, sem("h4_ready"), bt)
                for h in range(NH):
                    last = mm(ps[MLP * h:MLP * (h + 1), YB, :], wm1[:], half(hn4, h))
                last.then_inc(sem("h4_ps"), 1)
                for h in range(NH):
                    yield tail_at(20 + 2 * h)
                    if h:
                        wait(pe, sem("xo_ready"), bt, NH, h)
                    else:
                        wait(pe, sem("gelu_ready"), bt)
                    rows = slice(MLP * h, MLP * (h + 1))
                    mm(ps[:, YB, :], wm2[rows, :], gl[rows, :]).then_inc(sem("m4_ps"), 1)

            def scores_in_rows(n, mb, mg):
                hd, c, hh = GH * mg + n // (NC * NH), n // NH % NC, n % NH
                if n % (2 * NC * NH) == 0:
                    wait(pe, sem(f"packed{hd % GH // 2}"), mb, 16 * 12 * NG, 16 * 12 * (mg + 1))
                if n == 0:
                    wait(pe, sem("nm3T_ready"), mb, NG, mg)
                wait(pe, sem("mx3_ready"), mb, NG * TILES, mg * TILES + n - 1)
                mm(ps[:, MB + n % 2, :], part(qp[0:ROWS, hd // 2, :], c), half(kp[0:ROWS, hd, :], hh)).then_inc(sem("s3max_ps"), 1)

            def passes(bt, sides):
                if (bt + 1).exists() and not bt.exists():
                    pe.wait_ge(sem("v_ones"), 2)
                    pe.wait_ge(sem("wo_in"), 16 * HEADS)
                    pe.wait_ge(sem("k_ones_in"), 16 * HEADS)
                    pe.wait_ge(sem("packs_zeroed"), 2)
                heads = bt.exists()
                for g, (mb, mg) in enumerate(((bt, 1), (bt + 1, 0))):
                    maxima = mb.exists()
                    if heads:
                        wait(pe, sem("nm3_row_in"), bt, 16 * HEADS, 16 * GH * (g + 1))
                    for p in range(LAPS):
                        s, i = divmod(p, GH)
                        h, j = divmod(s, NC)
                        if heads and s < STEPS:
                            hd, u = GH * g + i, g * TILES + p
                            wait(pe, sem("p3_ready"), bt, NG * TILES, u - 1)
                            mm(ps[:, SB + p % 2, :], part(kp[:, hd, :], j), half(qp[:, hd // 2, :], h)).then_inc(sem("s3_ps"), 1)
                        early, late = maxima_at(mg, p) if maxima else ((), ())
                        for n in early:
                            scores_in_rows(n, mb, mg)
                        if heads and i == GH - 1 and s:
                            h, j = divmod(s - 1, NC)
                            if j == 0:
                                wait(pe, sem("og_ready"), bt, NG * NH, NH * g + h)
                                wait(pe, sem("vt3_ready"), bt, NG, g + 1)
                            wait(pe, sem("p3_ready"), bt, NG * TILES, g * TILES + GH * s)
                            for q in range(GH):
                                last = mm(ps[32 * q:32 * (q + 1), VB, :], vt3[g][:, j, q, :], p3[:, (s - 1) % 2, q, :],
                                          start=j == 0, stop=j == NC - 1)
                            last.then_inc(sem("pv3_done"), 1)
                        if maxima and p == M_END + 1:
                            wait(pe, sem("nm3_ready"), mb, NG, mg + 1)
                            nc.tensor.transpose(ps[0:GH * NC, MB, 0:128], nm3[:], ident[:]).then_inc(sem("nm3T_ps"), 1)
                        for side in sides:
                            side.upto(LAPS * g + p)
                        for n in late:
                            scores_in_rows(n, mb, mg)
                for side in sides:
                    side.finish()

            walk(pe, start, late_start, non_local, wavelet, queries, attention, head_norm, tail, passes)


def kernel(**inputs):
    import concourse.bacc as bacc
    from concourse.bass_utils import run_bass_kernel_spmd

    i = {k.replace("_conv_", "_"): np.asarray(v) for k, v in inputs.items()}

    def t(a):
        return np.ascontiguousarray(a.T)

    cols = {k: i["L0_" + k] for k in ("b_W", "bn_gamma", "bn_beta", "bn_mean", "bn_var")}
    cols |= {k: i["L1_" + k] for k in ("fusion_b", "bn1_g", "bn1_b", "bn1_m", "bn1_v")}
    for k in ("proj_b", "bn2_g", "bn2_b", "bn2_m", "bn2_v"):
        for n in range(4):
            cols[f"{k}{n}"] = i["L1_" + k][C * n:C * (n + 1)]
    cols |= {k: i["L2_" + k] for k in ("gamma", "beta", "bq", "bk", "bv", "bp")}
    cols |= {k: i["L3_" + k] for k in ("b_out", "g1", "beta1", "g2", "beta2", "b_mlp2")}
    cols["temp"] = np.repeat(i["L3_temperature"].reshape(HEADS), HD)
    cols["b_phig"] = np.concatenate([i["L0_b_phi"], i["L0_b_g"]])
    arrays = {
        "x": np.ascontiguousarray(i["x"]),
        "vecs": np.ascontiguousarray(np.stack([cols[k] for k in VECS], axis=1)),
        "w_theta": t(i["L0_w_theta"]),
        "b_theta": np.ascontiguousarray(i["L0_b_theta"].reshape(CI, 1)),
        "w_phig": t(np.concatenate([i["L0_w_phi"], i["L0_w_g"]])),
        "w_W": t(i["L0_w_W"]),
        "w_fuse": np.ascontiguousarray(i["L1_fusion_w"].reshape(C, 4, C).transpose(2, 1, 0).reshape(C, 4 * C)),
        "sa_w": np.ascontiguousarray(i["L1_sa_w"].reshape(2, TAPS, TAPS)),
        "ca_w1": t(i["L1_ca_w1"]),
        "ca_w2": t(i["L1_ca_w2"]),
        "w_proj": t(i["L1_proj_w"]),
        "wq": t(i["L2_wq"]),
        "wk": t(i["L2_wk"]),
        "wv": np.ascontiguousarray(i["L2_wv"]),
        "wp": t(i["L2_wp"]),
        "w_qkv": t(i["L3_w_qkv"]),
        "w_out": t(i["L3_w_out"]),
        "w_mlp1": t(i["L3_w_mlp1"]),
        "b_mlp1": np.ascontiguousarray(i["L3_b_mlp1"].reshape(MLP, 1)),
        "w_mlp2": t(i["L3_w_mlp2"]),
    }
    nc = bacc.Bacc("TRN2", target_bir_lowering=False, num_devices=1)
    aps = [nc.dram_tensor(f"in_{k}", a.shape, mybir.dt.from_np(a.dtype), kind="ExternalInput").ap() for k, a in arrays.items()]
    out = nc.dram_tensor("out", (B, C, H, W), F32, kind="ExternalOutput").ap()
    nc.disable_value_cache = True
    build(nc, *aps, out)
    r = run_bass_kernel_spmd(nc, [{f"in_{k}": a for k, a in arrays.items()}], core_ids=[0])
    return r.results[0]["out"]
```
